# Optimizing a Trainium2 kernel written in Bass

```python
import numpy as np
import jax
import jax.numpy as jnp

def _softmax(x, axis=-1):
    return jax.nn.softmax(x, axis=axis)

def _gelu(x):
    return jax.nn.gelu(x, approximate=True)

def _silu(x):
    return jax.nn.silu(x)

def _sigmoid(x):
    return jax.nn.sigmoid(x)

def _layernorm(x, axis=-1, eps=1e-05):
    m = jnp.mean(x, axis=axis, keepdims=True)
    v = jnp.var(x, axis=axis, keepdims=True)
    return (x - m) / jnp.sqrt(v + eps)

def _scatter_add(tgt, idx, src, axis=0):
    return tgt.at[idx].add(src)

def _segment_sum(src, seg, n):
    return jax.ops.segment_sum(src, seg, n)
kernel_name = 'mk_seq_postln_d4_jaxref_r8_5e3ff8'

def setup_inputs(seed: int=0):
    np.random.seed(seed)
    _w = jnp.asarray

    def _L0_attn_setup():
        import jax, jax.numpy as jnp
        import numpy as np
        B, T, H, S, F, G = (2, 256, 512, 128, 1248, 6)
        GRAD_ORDER_MIN = 4
        THD = 2.5
        key = jax.random.key(seed)
        ks = jax.random.split(key, 9)
        sc = 0.02
        hidden_states = jax.random.normal(ks[0], (B, T, H), jnp.float32)
        up_w = jax.random.normal(ks[1], (S, H), jnp.float32) * sc
        gate_w = jax.random.normal(ks[2], (S, H), jnp.float32) / np.sqrt(H)
        local_point = jax.random.normal(ks[3], (S,), jnp.float32)
        local_approx_output = jax.random.normal(ks[4], (H, S), jnp.float32) * sc
        fuse_weight = jax.random.normal(ks[5], (H, S, G), jnp.float32) * sc
        discount_factor = jnp.asarray(np.cumsum(np.log(np.arange(1, G + 1, dtype=np.float64))), jnp.float32)
        ffn_gate_w = jax.random.normal(ks[6], (F, H), jnp.float32) * sc
        ffn_up_w = jax.random.normal(ks[7], (F, H), jnp.float32) * sc
        ffn_down_w = jax.random.normal(ks[8], (H, F), jnp.float32) * sc
        return {'hidden_states': hidden_states, 'up_w': up_w, 'gate_w': gate_w, 'local_point': local_point, 'local_approx_output': local_approx_output, 'fuse_weight': fuse_weight, 'discount_factor': discount_factor, 'ffn_gate_w': ffn_gate_w, 'ffn_up_w': ffn_up_w, 'ffn_down_w': ffn_down_w}
    _L0_attn_in = _L0_attn_setup()

    def _L0_ffn_setup():
        import jax, jax.numpy as jnp
        import numpy as np
        import math
        B, S, IN, OUT = (4, 256, 512, 512)
        E, R, K = (8, 64, 128)
        SCALE = 64.0 / 64.0
        MULTIPLIER = 1.0
        key = jax.random.key(seed)
        ks = jax.random.split(key, 6)
        return {'x': jax.random.normal(ks[0], (B, S, IN), jnp.float32), 'W_org': jax.random.normal(ks[1], (OUT, IN), jnp.float32) * 0.02, 'lora_down': jax.random.normal(ks[2], (E, IN, R), jnp.float32) * 0.02, 'lora_up': jax.random.normal(ks[3], (E, R, OUT), jnp.float32) * 0.02, 'lora_keys': jax.random.normal(ks[4], (E, K), jnp.float32), 'Wq': jax.random.normal(ks[5], (K, IN), jnp.float32) * 0.02}
    _L0_ffn_in = _L0_ffn_setup()

    def _L1_attn_setup():
        import jax, jax.numpy as jnp
        import numpy as np
        SEQ, BATCH, HIDDEN = (256, 1, 512)
        NUM_HEADS, NUM_KV_HEADS, HEAD_DIM = (32, 8, 128)
        Q_PER_GROUP = NUM_HEADS // NUM_KV_HEADS
        TOTAL_PROJ = NUM_KV_HEADS * (Q_PER_GROUP + 2) * HEAD_DIM
        key = jax.random.key(seed)
        k1, k2, k3 = jax.random.split(key, 3)
        tokens = jax.random.normal(k1, (SEQ, BATCH, HIDDEN), dtype=jnp.float32)
        weight_qkv = jax.random.normal(k2, (TOTAL_PROJ, HIDDEN), dtype=jnp.float32) * (2.0 / (TOTAL_PROJ + HIDDEN)) ** 0.5
        weight_proj = jax.random.normal(k3, (HIDDEN, NUM_HEADS * HEAD_DIM), dtype=jnp.float32) * (2.0 / (HIDDEN + NUM_HEADS * HEAD_DIM)) ** 0.5
        return {'tokens': tokens, 'weight_qkv': weight_qkv, 'weight_proj': weight_proj}
    _L1_attn_in = _L1_attn_setup()

    def _L1_ffn_setup():
        import jax, jax.numpy as jnp
        import numpy as np
        GROUP_SIZE = 128

        def dequantize(imatrix, scales, zeros, group_size, out_dtype):
            rs = jnp.repeat(scales, group_size, axis=0)
            rz = jnp.repeat(zeros, group_size, axis=0)
            return ((imatrix.astype(rs.dtype) - rz.astype(rs.dtype)) * rs).astype(out_dtype)
        key = jax.random.key(seed)
        ks = jax.random.split(key, 10)
        H, I, G = (512, 1792, GROUP_SIZE)
        B, S = (4, 256)
        x = jax.random.normal(ks[0], (B, S, H), dtype=jnp.float32)
        gate_w = jax.random.randint(ks[1], (H, I), 0, 16, dtype=jnp.int32)
        gate_z = jax.random.randint(ks[2], (H // G, I), 0, 16, dtype=jnp.int32)
        gate_s = jax.random.uniform(ks[3], (H // G, I), dtype=jnp.float32) * 0.01
        up_w = jax.random.randint(ks[4], (H, I), 0, 16, dtype=jnp.int32)
        up_z = jax.random.randint(ks[5], (H // G, I), 0, 16, dtype=jnp.int32)
        up_s = jax.random.uniform(ks[6], (H // G, I), dtype=jnp.float32) * 0.01
        down_w = jax.random.randint(ks[7], (I, H), 0, 16, dtype=jnp.int32)
        down_z = jax.random.randint(ks[8], (I // G, H), 0, 16, dtype=jnp.int32)
        down_s = jax.random.uniform(ks[9], (I // G, H), dtype=jnp.float32) * 0.01
        return {'x': x, 'gate_w': gate_w, 'gate_z': gate_z, 'gate_s': gate_s, 'up_w': up_w, 'up_z': up_z, 'up_s': up_s, 'down_w': down_w, 'down_z': down_z, 'down_s': down_s}
    _L1_ffn_in = _L1_ffn_setup()

    def _L2_attn_setup():
        import jax, jax.numpy as jnp
        import numpy as np
        DEPTH, DIM, DFF, VOCAB = (4, 64, 256, 512)
        EPS = 1e-05

        def layernorm(x, w, b):
            mu = jnp.mean(x, axis=-1, keepdims=True)
            var = jnp.mean((x - mu) ** 2, axis=-1, keepdims=True)
            return (x - mu) * jax.lax.rsqrt(var + EPS) * w + b

        def sconv(x, phazor_c, last_conv_c):
            B, L, D = x.shape
            r = jnp.abs(phazor_c)
            p = jnp.tanh(r) * jnp.exp(1j * jnp.angle(phazor_c))
            prog = p[None, :] ** jnp.arange(L, dtype=jnp.float32)[:, None]
            filt_fft = jnp.fft.fft(prog, n=2 * L, axis=0)
            x_fft = jnp.fft.fft(x.astype(jnp.complex64), n=2 * L, axis=1)
            conv = jnp.fft.ifft(filt_fft[None] * x_fft, axis=1)[:, :L]
            conv = conv + last_conv_c[None, None, :] * prog[None] * p[None, None, :]
            return conv.real.astype(x.dtype)

        def _forward(x, Win, bin, ln1_w, ln1_b, phz_re, phz_im, lc_re, lc_im, sc_lin, ln2_w, ln2_b, W1, b1, W2, b2, lnl_w, lnl_b, Wout, bout):
            h = jnp.einsum('blv,dv->bld', x, Win) + bin

            def body(h, p):
                l1w, l1b, pr, pi, lr, li, scl, l2w, l2b, w1, b1_, w2, b2_ = p
                y = jax.nn.silu(layernorm(h, l1w, l1b))
                y = sconv(y, pr + 1j * pi, lr + 1j * li)
                h = h + y * scl
                y = layernorm(h, l2w, l2b)
                y = jax.nn.silu(jnp.einsum('bld,fd->blf', y, w1) + b1_)
                y = jnp.einsum('blf,df->bld', y, w2) + b2_
                return (h + y, None)
            xs = (ln1_w, ln1_b, phz_re, phz_im, lc_re, lc_im, sc_lin, ln2_w, ln2_b, W1, b1, W2, b2)
            h, _ = jax.lax.scan(body, h, xs)
            h = layernorm(h, lnl_w, lnl_b)
            return jnp.einsum('bld,vd->blv', h, Wout) + bout
        key = jax.random.key(seed)
        ks = jax.random.split(key, 20)
        f32 = jnp.float32
        inp = {}
        inp['x'] = jax.random.normal(ks[0], (2, 512, VOCAB), dtype=f32)
        inp['Win'] = jax.random.normal(ks[1], (DIM, VOCAB), dtype=f32) * VOCAB ** (-0.5)
        inp['bin'] = jnp.zeros((DIM,), f32)
        inp['ln1_w'] = jnp.ones((DEPTH, DIM), f32)
        inp['ln1_b'] = jnp.zeros((DEPTH, DIM), f32)
        ang = 2 * np.pi * jnp.arange(DIM, dtype=f32) / DIM
        mag = jnp.abs(jax.random.normal(ks[2], (DEPTH, DIM), dtype=f32))
        inp['phz_re'] = mag * jnp.cos(ang)[None]
        inp['phz_im'] = mag * jnp.sin(ang)[None]
        inp['lc_re'] = jax.random.normal(ks[3], (DEPTH, DIM), dtype=f32)
        inp['lc_im'] = jax.random.normal(ks[4], (DEPTH, DIM), dtype=f32)
        inp['sc_lin'] = jnp.ones((DEPTH, DIM), f32)
        inp['ln2_w'] = jnp.ones((DEPTH, DIM), f32)
        inp['ln2_b'] = jnp.zeros((DEPTH, DIM), f32)
        inp['W1'] = jax.random.normal(ks[5], (DEPTH, DFF, DIM), dtype=f32) * DIM ** (-0.5)
        inp['b1'] = jnp.zeros((DEPTH, DFF), f32)
        inp['W2'] = jax.random.normal(ks[6], (DEPTH, DIM, DFF), dtype=f32) * DFF ** (-0.5)
        inp['b2'] = jnp.zeros((DEPTH, DIM), f32)
        inp['lnl_w'] = jnp.ones((DIM,), f32)
        inp['lnl_b'] = jnp.zeros((DIM,), f32)
        inp['Wout'] = jax.random.normal(ks[7], (VOCAB, DIM), dtype=f32) * DIM ** (-0.5)
        inp['bout'] = jnp.zeros((VOCAB,), f32)
        return inp
    _L2_attn_in = _L2_attn_setup()

    def _L2_ffn_setup():
        import jax, jax.numpy as jnp
        import numpy as np
        B_, S, D_IN, D_OUT, R = (4, 256, 512, 512, 64)
        SCALING = 16 / 64
        key = jax.random.key(seed)
        ks = jax.random.split(key, 7)
        return {'x': jax.random.normal(ks[0], (B_, S, D_IN), dtype=jnp.float32), 'W_base': jax.random.normal(ks[1], (D_OUT, D_IN), dtype=jnp.float32) * 0.02, 'b_base': jax.random.normal(ks[2], (D_OUT,), dtype=jnp.float32) * 0.02, 'A': jax.random.normal(ks[3], (R, D_IN), dtype=jnp.float32) * 0.02, 'B': jax.random.normal(ks[4], (D_OUT, R), dtype=jnp.float32) * 0.02, 'WL': jax.random.normal(ks[5], (R, D_IN), dtype=jnp.float32) * 0.02, 'WR': jax.random.normal(ks[6], (D_OUT, R), dtype=jnp.float32) * 0.02}
    _L2_ffn_in = _L2_ffn_setup()

    def _L3_attn_setup():
        import jax, jax.numpy as jnp
        import numpy as np
        B, T, D = (2, 256, 512)
        H = 32
        HKV = 1
        HD = D // H
        key = jax.random.key(seed)
        ks = jax.random.split(key, 9)
        s = lambda fan_in: 1.0 / np.sqrt(fan_in)
        return {'x': jax.random.normal(ks[0], (B, T, D), dtype=jnp.float32), 'wq_w': jax.random.normal(ks[1], (H * HD, D), dtype=jnp.float32) * s(D), 'wq_b': jax.random.normal(ks[2], (H * HD,), dtype=jnp.float32) * 0.02, 'wk_w': jax.random.normal(ks[3], (HKV * HD, D), dtype=jnp.float32) * s(D), 'wk_b': jax.random.normal(ks[4], (HKV * HD,), dtype=jnp.float32) * 0.02, 'wv_w': jax.random.normal(ks[5], (HKV * HD, D), dtype=jnp.float32) * s(D), 'wv_b': jax.random.normal(ks[6], (HKV * HD,), dtype=jnp.float32) * 0.02, 'wo_w': jax.random.normal(ks[7], (D, H * HD), dtype=jnp.float32) * s(H * HD), 'wo_b': jax.random.normal(ks[8], (D,), dtype=jnp.float32) * 0.02}
    _L3_attn_in = _L3_attn_setup()

    def _L3_ffn_setup():
        import jax, jax.numpy as jnp
        import numpy as np
        DIM = 512
        HIDDEN = 1376
        B, S = (4, 256)

        def _qlinear(x, w_int, scale):
            w = w_int.astype(x.dtype) * scale
            return jnp.einsum('bsd,hd->bsh', x, w)
        key = jax.random.key(seed)
        k_x, k_g, k_u, k_d = jax.random.split(key, 4)
        x = jax.random.normal(k_x, (B, S, DIM), dtype=jnp.float32)
        w_gate = jax.random.randint(k_g, (HIDDEN, DIM), -127, 128, dtype=jnp.int32)
        w_up = jax.random.randint(k_u, (HIDDEN, DIM), -127, 128, dtype=jnp.int32)
        w_down = jax.random.randint(k_d, (DIM, HIDDEN), -127, 128, dtype=jnp.int32)
        scale_gate = jnp.float32(0.01)
        scale_up = jnp.float32(0.01)
        scale_down = jnp.float32(0.01)
        return {'x': x, 'w_gate': w_gate, 'w_up': w_up, 'w_down': w_down, 'scale_gate': scale_gate, 'scale_up': scale_up, 'scale_down': scale_down}
    _L3_ffn_in = _L3_ffn_setup()
    _d = {'L0_attn_hidden_states': _L0_attn_in['hidden_states'], 'L0_attn_up_w': _L0_attn_in['up_w'], 'L0_attn_gate_w': _L0_attn_in['gate_w'], 'L0_attn_local_point': _L0_attn_in['local_point'], 'L0_attn_local_approx_output': _L0_attn_in['local_approx_output'], 'L0_attn_fuse_weight': _L0_attn_in['fuse_weight'], 'L0_attn_discount_factor': _L0_attn_in['discount_factor'], 'L0_attn_ffn_gate_w': _L0_attn_in['ffn_gate_w'], 'L0_attn_ffn_up_w': _L0_attn_in['ffn_up_w'], 'L0_attn_ffn_down_w': _L0_attn_in['ffn_down_w'], 'L0_ffn_W_org': _L0_ffn_in['W_org'], 'L0_ffn_lora_down': _L0_ffn_in['lora_down'], 'L0_ffn_lora_up': _L0_ffn_in['lora_up'], 'L0_ffn_lora_keys': _L0_ffn_in['lora_keys'], 'L0_ffn_Wq': _L0_ffn_in['Wq'], 'L1_attn_weight_qkv': _L1_attn_in['weight_qkv'], 'L1_attn_weight_proj': _L1_attn_in['weight_proj'], 'L1_ffn_gate_w': _L1_ffn_in['gate_w'], 'L1_ffn_gate_z': _L1_ffn_in['gate_z'], 'L1_ffn_gate_s': _L1_ffn_in['gate_s'], 'L1_ffn_up_w': _L1_ffn_in['up_w'], 'L1_ffn_up_z': _L1_ffn_in['up_z'], 'L1_ffn_up_s': _L1_ffn_in['up_s'], 'L1_ffn_down_w': _L1_ffn_in['down_w'], 'L1_ffn_down_z': _L1_ffn_in['down_z'], 'L1_ffn_down_s': _L1_ffn_in['down_s'], 'L2_attn_Win': _L2_attn_in['Win'], 'L2_attn_bin': _L2_attn_in['bin'], 'L2_attn_ln1_w': _L2_attn_in['ln1_w'], 'L2_attn_ln1_b': _L2_attn_in['ln1_b'], 'L2_attn_phz_re': _L2_attn_in['phz_re'], 'L2_attn_phz_im': _L2_attn_in['phz_im'], 'L2_attn_lc_re': _L2_attn_in['lc_re'], 'L2_attn_lc_im': _L2_attn_in['lc_im'], 'L2_attn_sc_lin': _L2_attn_in['sc_lin'], 'L2_attn_ln2_w': _L2_attn_in['ln2_w'], 'L2_attn_ln2_b': _L2_attn_in['ln2_b'], 'L2_attn_W1': _L2_attn_in['W1'], 'L2_attn_b1': _L2_attn_in['b1'], 'L2_attn_W2': _L2_attn_in['W2'], 'L2_attn_b2': _L2_attn_in['b2'], 'L2_attn_lnl_w': _L2_attn_in['lnl_w'], 'L2_attn_lnl_b': _L2_attn_in['lnl_b'], 'L2_attn_Wout': _L2_attn_in['Wout'], 'L2_attn_bout': _L2_attn_in['bout'], 'L2_ffn_W_base': _L2_ffn_in['W_base'], 'L2_ffn_b_base': _L2_ffn_in['b_base'], 'L2_ffn_A': _L2_ffn_in['A'], 'L2_ffn_B': _L2_ffn_in['B'], 'L2_ffn_WL': _L2_ffn_in['WL'], 'L2_ffn_WR': _L2_ffn_in['WR'], 'L3_attn_wq_w': _L3_attn_in['wq_w'], 'L3_attn_wq_b': _L3_attn_in['wq_b'], 'L3_attn_wk_w': _L3_attn_in['wk_w'], 'L3_attn_wk_b': _L3_attn_in['wk_b'], 'L3_attn_wv_w': _L3_attn_in['wv_w'], 'L3_attn_wv_b': _L3_attn_in['wv_b'], 'L3_attn_wo_w': _L3_attn_in['wo_w'], 'L3_attn_wo_b': _L3_attn_in['wo_b'], 'L3_ffn_w_gate': _L3_ffn_in['w_gate'], 'L3_ffn_w_up': _L3_ffn_in['w_up'], 'L3_ffn_w_down': _L3_ffn_in['w_down'], 'L3_ffn_scale_gate': _L3_ffn_in['scale_gate'], 'L3_ffn_scale_up': _L3_ffn_in['scale_up'], 'L3_ffn_scale_down': _L3_ffn_in['scale_down']}
    _x0 = _d['L0_attn_hidden_states']
    _d['L0_attn_hidden_states'] = jax.random.normal(jax.random.fold_in(jax.random.key(seed), 1), (1, 1024, 512), dtype=_x0.dtype)
    del _x0
    return _d

def reference(L0_attn_hidden_states, L0_attn_up_w, L0_attn_gate_w, L0_attn_local_point, L0_attn_local_approx_output, L0_attn_fuse_weight, L0_attn_discount_factor, L0_attn_ffn_gate_w, L0_attn_ffn_up_w, L0_attn_ffn_down_w, L0_ffn_W_org, L0_ffn_lora_down, L0_ffn_lora_up, L0_ffn_lora_keys, L0_ffn_Wq, L1_attn_weight_qkv, L1_attn_weight_proj, L1_ffn_gate_w, L1_ffn_gate_z, L1_ffn_gate_s, L1_ffn_up_w, L1_ffn_up_z, L1_ffn_up_s, L1_ffn_down_w, L1_ffn_down_z, L1_ffn_down_s, L2_attn_Win, L2_attn_bin, L2_attn_ln1_w, L2_attn_ln1_b, L2_attn_phz_re, L2_attn_phz_im, L2_attn_lc_re, L2_attn_lc_im, L2_attn_sc_lin, L2_attn_ln2_w, L2_attn_ln2_b, L2_attn_W1, L2_attn_b1, L2_attn_W2, L2_attn_b2, L2_attn_lnl_w, L2_attn_lnl_b, L2_attn_Wout, L2_attn_bout, L2_ffn_W_base, L2_ffn_b_base, L2_ffn_A, L2_ffn_B, L2_ffn_WL, L2_ffn_WR, L3_attn_wq_w, L3_attn_wq_b, L3_attn_wk_w, L3_attn_wk_b, L3_attn_wv_w, L3_attn_wv_b, L3_attn_wo_w, L3_attn_wo_b, L3_ffn_w_gate, L3_ffn_w_up, L3_ffn_w_down, L3_ffn_scale_gate, L3_ffn_scale_up, L3_ffn_scale_down):

    def _L0_attn_ref(hidden_states, up_w, gate_w, local_point, local_approx_output, fuse_weight, discount_factor, ffn_gate_w, ffn_up_w, ffn_down_w):
        import jax, jax.numpy as jnp
        import numpy as np
        B, T, H, S, F, G = (2, 256, 512, 128, 1248, 6)
        GRAD_ORDER_MIN = 4
        THD = 2.5
        approx_up = hidden_states @ up_w.T
        gate_pre = hidden_states @ gate_w.T
        delta = gate_pre - local_point
        neg_factor = jnp.where(delta > 0, 1.0, -1.0).astype(hidden_states.dtype)
        delta_abs = jnp.abs(delta)
        log_delta = jnp.log(delta_abs)
        keep = (delta_abs <= THD).astype(hidden_states.dtype)
        approx_out = approx_up @ local_approx_output.T
        for idx in range(G):
            m = idx + 1
            dterm = jnp.exp(log_delta * m - discount_factor[idx])
            if m % 2 == 1:
                dterm = dterm * neg_factor
            tmp = dterm * approx_up
            if m > GRAD_ORDER_MIN:
                tmp = tmp * keep
            approx_out = approx_out + tmp @ fuse_weight[:, :, idx].T
        ffn_out = jax.nn.silu(hidden_states @ ffn_gate_w.T) * (hidden_states @ ffn_up_w.T) @ ffn_down_w.T
        return approx_out + ffn_out

    def _L0_ffn_ref(x, W_org, lora_down, lora_up, lora_keys, Wq):
        import jax, jax.numpy as jnp
        import numpy as np
        import math
        B, S, IN, OUT = (4, 256, 512, 512)
        E, R, K = (8, 64, 128)
        SCALE = 64.0 / 64.0
        MULTIPLIER = 1.0
        base = jnp.einsum('bsi,oi->bso', x, W_org)
        q = jnp.einsum('bi,ki->bk', x.mean(axis=1), Wq)
        scores = jnp.einsum('bk,ek->be', q, lora_keys) / math.sqrt(K)
        coeffs = jax.nn.softmax(scores, axis=-1)
        h = jnp.einsum('bsi,eir->bser', x, lora_down)
        delta = jnp.einsum('be,bser,ero->bso', coeffs, h, lora_up)
        return base + delta * (SCALE * MULTIPLIER)

    def _L1_attn_ref(tokens, weight_qkv, weight_proj):
        import jax, jax.numpy as jnp
        import numpy as np
        SEQ, BATCH, HIDDEN = (256, 1, 512)
        NUM_HEADS, NUM_KV_HEADS, HEAD_DIM = (32, 8, 128)
        Q_PER_GROUP = NUM_HEADS // NUM_KV_HEADS
        TOTAL_PROJ = NUM_KV_HEADS * (Q_PER_GROUP + 2) * HEAD_DIM
        S, B, H = tokens.shape
        scale = 1.0 / HEAD_DIM ** 0.5
        qkv = jnp.einsum('sbh,ph->sbp', tokens, weight_qkv)
        qkv = qkv.reshape(S, B, NUM_KV_HEADS, Q_PER_GROUP + 2, HEAD_DIM)
        q = qkv[:, :, :, :Q_PER_GROUP, :].reshape(S, B, NUM_HEADS, HEAD_DIM)
        k = qkv[:, :, :, Q_PER_GROUP, :]
        v = qkv[:, :, :, Q_PER_GROUP + 1, :]
        k = jnp.repeat(k, Q_PER_GROUP, axis=2)
        v = jnp.repeat(v, Q_PER_GROUP, axis=2)
        q = q.transpose(1, 2, 0, 3)
        k = k.transpose(1, 2, 0, 3)
        v = v.transpose(1, 2, 0, 3)
        scores = jnp.einsum('bhsd,bhtd->bhst', q, k) * scale
        causal = jnp.tril(jnp.ones((S, S), dtype=bool))
        scores = jnp.where(causal, scores, jnp.finfo(scores.dtype).min)
        attn = jax.nn.softmax(scores, axis=-1)
        out = jnp.einsum('bhst,bhtd->bhsd', attn, v)
        out = out.transpose(2, 0, 1, 3).reshape(S, B, NUM_HEADS * HEAD_DIM)
        return jnp.einsum('sbe,he->sbh', out, weight_proj)

    def _L1_ffn_ref(x, gate_w, gate_z, gate_s, up_w, up_z, up_s, down_w, down_z, down_s):
        import jax, jax.numpy as jnp
        import numpy as np
        GROUP_SIZE = 128

        def dequantize(imatrix, scales, zeros, group_size, out_dtype):
            rs = jnp.repeat(scales, group_size, axis=0)
            rz = jnp.repeat(zeros, group_size, axis=0)
            return ((imatrix.astype(rs.dtype) - rz.astype(rs.dtype)) * rs).astype(out_dtype)
        dt = x.dtype
        gate_proj = dequantize(gate_w, gate_s, gate_z, GROUP_SIZE, dt)
        up_proj = dequantize(up_w, up_s, up_z, GROUP_SIZE, dt)
        down_proj = dequantize(down_w, down_s, down_z, GROUP_SIZE, dt)
        gate = jax.nn.silu(jnp.dot(x, gate_proj))
        up = jnp.dot(x, up_proj)
        return jnp.dot(gate * up, down_proj)

    def _L2_attn_ref(x, Win, bin, ln1_w, ln1_b, phz_re, phz_im, lc_re, lc_im, sc_lin, ln2_w, ln2_b, W1, b1, W2, b2, lnl_w, lnl_b, Wout, bout):
        import jax, jax.numpy as jnp
        import numpy as np
        DEPTH, DIM, DFF, VOCAB = (4, 64, 256, 512)
        EPS = 1e-05

        def layernorm(x, w, b):
            mu = jnp.mean(x, axis=-1, keepdims=True)
            var = jnp.mean((x - mu) ** 2, axis=-1, keepdims=True)
            return (x - mu) * jax.lax.rsqrt(var + EPS) * w + b

        def sconv(x, phazor_c, last_conv_c):
            B, L, D = x.shape
            r = jnp.abs(phazor_c)
            p = jnp.tanh(r) * jnp.exp(1j * jnp.angle(phazor_c))
            prog = p[None, :] ** jnp.arange(L, dtype=jnp.float32)[:, None]
            filt_fft = jnp.fft.fft(prog, n=2 * L, axis=0)
            x_fft = jnp.fft.fft(x.astype(jnp.complex64), n=2 * L, axis=1)
            conv = jnp.fft.ifft(filt_fft[None] * x_fft, axis=1)[:, :L]
            conv = conv + last_conv_c[None, None, :] * prog[None] * p[None, None, :]
            return conv.real.astype(x.dtype)

        def _forward(x, Win, bin, ln1_w, ln1_b, phz_re, phz_im, lc_re, lc_im, sc_lin, ln2_w, ln2_b, W1, b1, W2, b2, lnl_w, lnl_b, Wout, bout):
            h = jnp.einsum('blv,dv->bld', x, Win) + bin

            def body(h, p):
                l1w, l1b, pr, pi, lr, li, scl, l2w, l2b, w1, b1_, w2, b2_ = p
                y = jax.nn.silu(layernorm(h, l1w, l1b))
                y = sconv(y, pr + 1j * pi, lr + 1j * li)
                h = h + y * scl
                y = layernorm(h, l2w, l2b)
                y = jax.nn.silu(jnp.einsum('bld,fd->blf', y, w1) + b1_)
                y = jnp.einsum('blf,df->bld', y, w2) + b2_
                return (h + y, None)
            xs = (ln1_w, ln1_b, phz_re, phz_im, lc_re, lc_im, sc_lin, ln2_w, ln2_b, W1, b1, W2, b2)
            h, _ = jax.lax.scan(body, h, xs)
            h = layernorm(h, lnl_w, lnl_b)
            return jnp.einsum('bld,vd->blv', h, Wout) + bout
        return _forward(x, Win, bin, ln1_w, ln1_b, phz_re, phz_im, lc_re, lc_im, sc_lin, ln2_w, ln2_b, W1, b1, W2, b2, lnl_w, lnl_b, Wout, bout)

    def _L2_ffn_ref(x, W_base, b_base, A, B, WL, WR):
        import jax, jax.numpy as jnp
        import numpy as np
        B_, S, D_IN, D_OUT, R = (4, 256, 512, 512, 64)
        SCALING = 16 / 64
        result = jnp.einsum('bsi,oi->bso', x, W_base) + b_base
        a = jnp.einsum('bsi,ri->bsr', x, A) + jnp.einsum('bsi,ri->bsr', x, WL)
        b = jnp.einsum('bsr,or->bso', a, B) + jnp.einsum('bsr,or->bso', a, WR)
        return result + b * SCALING

    def _L3_attn_ref(x, wq_w, wq_b, wk_w, wk_b, wv_w, wv_b, wo_w, wo_b):
        import jax, jax.numpy as jnp
        import numpy as np
        B, T, D = (2, 256, 512)
        H = 32
        HKV = 1
        HD = D // H
        b, t, d = x.shape
        q = (x @ wq_w.T + wq_b).reshape(b, t, H, HD)
        k = (x @ wk_w.T + wk_b).reshape(b, t, HKV, HD)
        v = (x @ wv_w.T + wv_b).reshape(b, t, HKV, HD)
        k1 = k[:, :, 0, :]
        v1 = v[:, :, 0, :]
        scores = jnp.einsum('bqhd,bkd->bhqk', q, k1) / jnp.sqrt(jnp.float32(HD))
        causal = jnp.tril(jnp.ones((t, t), dtype=bool))
        scores = jnp.where(causal, scores, -jnp.inf)
        weights = jax.nn.softmax(scores, axis=-1)
        attn = jnp.einsum('bhqk,bkd->bqhd', weights, v1)
        attn = attn.reshape(b, t, H * HD)
        return attn @ wo_w.T + wo_b

    def _L3_ffn_ref(x, w_gate, w_up, w_down, scale_gate, scale_up, scale_down):
        import jax, jax.numpy as jnp
        import numpy as np
        DIM = 512
        HIDDEN = 1376
        B, S = (4, 256)

        def _qlinear(x, w_int, scale):
            w = w_int.astype(x.dtype) * scale
            return jnp.einsum('bsd,hd->bsh', x, w)
        x_gate = _qlinear(x, w_gate, scale_gate)
        x_up = _qlinear(x, w_up, scale_up)
        x_mid = jax.nn.silu(x_gate) * x_up
        x_out = _qlinear(x_mid, w_down, scale_down)
        return x_out
    x = L0_attn_hidden_states
    x = _layernorm(x + _L0_attn_ref(x, L0_attn_up_w, L0_attn_gate_w, L0_attn_local_point, L0_attn_local_approx_output, L0_attn_fuse_weight, L0_attn_discount_factor, L0_attn_ffn_gate_w, L0_attn_ffn_up_w, L0_attn_ffn_down_w), axis=-1)
    x = _layernorm(x + _L0_ffn_ref(x, L0_ffn_W_org, L0_ffn_lora_down, L0_ffn_lora_up, L0_ffn_lora_keys, L0_ffn_Wq), axis=-1)
    x = _layernorm(x + _L1_attn_ref(x, L1_attn_weight_qkv, L1_attn_weight_proj), axis=-1)
    x = _layernorm(x + _L1_ffn_ref(x, L1_ffn_gate_w, L1_ffn_gate_z, L1_ffn_gate_s, L1_ffn_up_w, L1_ffn_up_z, L1_ffn_up_s, L1_ffn_down_w, L1_ffn_down_z, L1_ffn_down_s), axis=-1)
    x = _layernorm(x + _L2_attn_ref(x, L2_attn_Win, L2_attn_bin, L2_attn_ln1_w, L2_attn_ln1_b, L2_attn_phz_re, L2_attn_phz_im, L2_attn_lc_re, L2_attn_lc_im, L2_attn_sc_lin, L2_attn_ln2_w, L2_attn_ln2_b, L2_attn_W1, L2_attn_b1, L2_attn_W2, L2_attn_b2, L2_attn_lnl_w, L2_attn_lnl_b, L2_attn_Wout, L2_attn_bout), axis=-1)
    x = _layernorm(x + _L2_ffn_ref(x, L2_ffn_W_base, L2_ffn_b_base, L2_ffn_A, L2_ffn_B, L2_ffn_WL, L2_ffn_WR), axis=-1)
    x = _layernorm(x + _L3_attn_ref(x, L3_attn_wq_w, L3_attn_wq_b, L3_attn_wk_w, L3_attn_wk_b, L3_attn_wv_w, L3_attn_wv_b, L3_attn_wo_w, L3_attn_wo_b), axis=-1)
    x = _layernorm(x + _L3_ffn_ref(x, L3_ffn_w_gate, L3_ffn_w_up, L3_ffn_w_down, L3_ffn_scale_gate, L3_ffn_scale_up, L3_ffn_scale_down), axis=-1)
    return x

_drawn_inputs = setup_inputs


def setup_inputs(seed=0):
    import zlib

    import numpy as np

    out = dict(_drawn_inputs(seed))
    spreads = {'L2_attn_bin': (0.0, 0.1),
     'L2_attn_ln1_w': (1.0, 0.2),
     'L2_attn_ln1_b': (0.0, 0.1),
     'L2_attn_sc_lin': (1.0, 0.2),
     'L2_attn_ln2_w': (1.0, 0.2),
     'L2_attn_ln2_b': (0.0, 0.1),
     'L2_attn_b1': (0.0, 0.1),
     'L2_attn_b2': (0.0, 0.1),
     'L2_attn_lnl_w': (1.0, 0.2),
     'L2_attn_lnl_b': (0.0, 0.1),
     'L2_attn_bout': (0.0, 0.1)}
    factors = {'L0_ffn_lora_keys': 8.0,
     'L0_ffn_Wq': 22.072,
     'L2_attn_lc_re': 3.102,
     'L3_attn_wq_b': 8.0,
     'L3_attn_wk_b': 64.0}
    for name, (base, spread) in spreads.items():
        noise = np.random.default_rng([zlib.crc32(name.encode()), seed]).standard_normal(out[name].shape)
        drawn = base * np.exp(spread * noise) if base else spread * noise
        out[name] = jnp.asarray(drawn.astype(out[name].dtype))
    for name, factor in factors.items():
        out[name] = (out[name] * factor).astype(out[name].dtype)
    return out
```

```python
from contextlib import ExitStack

import numpy as np

import concourse.bass as bass
from concourse import mybir

F32 = mybir.dt.float32
F32R = mybir.dt.float32r
BF16 = mybir.dt.bfloat16
I32 = mybir.dt.int32
ALU = mybir.AluOpType
ACT = mybir.ActivationFunctionType
AX = mybir.AxisListType

P = 128
TOK = 1024
DIM = 512
NT = TOK // P
KC = DIM // P
HALF = 512
EPS = 1e-5


class Chip:

    def __init__(self, nc, ctx):
        self.nc, self.ctx = nc, ctx
        self.x_tok = self.sb("x_tok", [P, NT, DIM], F32)
        self.x_feat = self.sb("x_feat", [P, KC, TOK], F32)
        self.ident = self.sb("ident", [P, P], F32)
        self.stats = self.sb("ln_stats", [P, NT, 6], F32)
        self.mean_var = self.sb("ln_mean_var", [P, NT, 2], F32)
        self.std = self.sb("ln_std", [P, NT], F32)
        self.rstd = self.sb("ln_rstd", [P, NT], F32)
        self.tail_sems = [self.sem(n) for n in Tail.NAMES]
        self.tails = self.ln_count = 0
        psum = ctx.enter_context(nc.psum_tensor("psum", [P, 8, 512], F32))
        self.bank = [psum[:, i, :] for i in range(8)]

    def sb(self, name, shape, dt, ctx=None):
        return (ctx or self.ctx).enter_context(self.nc.sbuf_tensor(name, shape, dt))

    def sem(self, name):
        return self.ctx.enter_context(self.nc.semaphore(name))


class Tail:

    NAMES = ("out_ready", "out_taken", "ln_step", "var_ready", "std_ready", "normed", "transposed", "feat_ready")

    def __init__(self, chip, out_bank, tr_bank, last=False):
        self.c, self.out_bank, self.tr_bank, self.last = chip, out_bank, tr_bank, last
        (self.out_ready, self.out_taken, self.ln_step, self.var_ready, self.std_ready, self.normed,
         self.transposed, self.feat_ready) = chip.tail_sems
        self.base = NT * chip.tails
        chip.tails += 1

    def dve(self, dve, t, bias=None):
        c, nc = self.c, self.c.nc
        row = c.x_tok[:, t, :]

        def step(ins):
            c.ln_count += 1
            ins.then_inc(self.ln_step, 1)
            dve.wait_ge(self.ln_step, c.ln_count)

        dve.wait_ge(self.out_ready, self.base + t + 1)
        if bias is None:
            nc.vector.tensor_tensor(row, row, self.out_bank[t % 2][:, :], ALU.add).then_inc(self.out_taken, 1)
            dve.wait_ge(self.out_taken, self.base + t + 1)
        else:
            nc.vector.tensor_tensor(row, row, self.out_bank[t % 2][:, :], ALU.add).then_inc(self.out_taken, 1)
            dve.wait_ge(self.out_taken, self.base + t + 1)
            step(nc.vector.tensor_tensor(row, row, bias[:, :], ALU.add))
        step(nc.vector.bn_stats(c.stats[:, t, :], row))
        nc.vector.bn_aggr(c.mean_var[:, t, :], c.stats[:, t, :]).then_inc(self.var_ready, 1)
        dve.wait_ge(self.std_ready, self.base + t + 1)
        step(nc.vector.reciprocal(c.rstd[:, t:t + 1], c.std[:, t:t + 1]))
        nc.vector.tensor_scalar(row, row, c.mean_var[:, t, 0:1], c.rstd[:, t:t + 1],
                                ALU.subtract, ALU.mult).then_inc(self.normed, 1)

    def act_std(self, act, t):
        c, nc = self.c, self.c.nc
        act.wait_ge(self.var_ready, self.base + t + 1)
        nc.scalar.activation(c.std[:, t:t + 1], c.mean_var[:, t, 1:2], ACT.Sqrt,
                             bias=c.eps[:, 0:1]).then_inc(self.std_ready, 1)

    def act_copy(self, act, t):
        c, nc = self.c, self.c.nc
        act.wait_ge(self.transposed, self.base + t + 1)
        src = self.tr_bank[t % 2][:, :].rearrange("p (k n) -> p k n", k=KC)
        nc.scalar.copy(c.x_feat[:, :, t * P:(t + 1) * P], src).then_inc(self.feat_ready, 1)

    def act(self, act):
        for t in range(NT):
            self.act_std(act, t)
            if t and not self.last:
                self.act_copy(act, t - 1)
        if not self.last:
            self.act_copy(act, NT - 1)
            act.wait_ge(self.feat_ready, self.base + NT)

    def pe(self, pe, t):
        c, nc = self.c, self.c.nc
        if self.last:
            return
        pe.wait_ge(self.normed, self.base + t + 1)
        if t >= 2:
            pe.wait_ge(self.feat_ready, self.base + t - 1)
        for k in range(KC):
            ins = nc.tensor.transpose(self.tr_bank[t % 2][:, k * P:(k + 1) * P],
                                      c.x_tok[:, t, k * P:(k + 1) * P], c.ident[:, :])
        ins.then_inc(self.transposed, 1)


def each_tile(eng, tiles, body):
    body(0, 0, True)
    body(1, 1, True)
    if tiles >= 4:
        with eng.Fori(1, tiles // 2) as i:
            body(2 * i, 0, False)
            body(2 * i + 1, 1, False)
    if tiles % 2:
        body(tiles - 1, 0, False)


def setup(c, x_tok_dram, x_feat_dram):
    nc = c.nc
    c.eps = c.sb("eps", [P, 1], F32)
    loaded, ready, zeroed = c.sem("x_loaded"), c.sem("const_ready"), c.sem("ident_zeroed")
    with nc.Block() as block:

        @block.sync
        def _(sp):
            sp.dma_start(c.x_feat[:, :, :], x_feat_dram.rearrange("(k p) n -> p k n", p=P)).then_inc(loaded, 16)
            sp.dma_start(c.x_tok[:, :, :], x_tok_dram.rearrange("(t p) n -> p t n", p=P)).then_inc(loaded, 16)
            sp.wait_ge(loaded, 32)

        @block.gpsimd
        def _(pool):
            nc.gpsimd.memset(c.eps[:, :], EPS)
            nc.gpsimd.memset(c.ident[:, :], 0.0).then_inc(zeroed, 1)
            pool.wait_ge(zeroed, 1)
            nc.gpsimd.affine_select(out=c.ident[:, :], in_=c.ident[:, :], compare_op=ALU.not_equal, fill=1.0,
                                    base=0, pattern=[[-1, P]], channel_multiplier=1).then_inc(ready, 1)
            pool.wait_ge(ready, 1)


def swiglu(c, name, tiles, weights, zeros=None, scales=None, scale=None, down=None, last=None,
           extra_loads=None, extra_dve=None, extra_pe=None, extra_act=None, extra_pool=None):
    nc = c.nc
    quantised = down is None
    width = 2 * KC * P + (DIM if quantised else 0)
    with ExitStack() as own:
        def sb(n, shape, dt):
            return c.sb(f"{name}_{n}", shape, dt, own)

        def sem(n):
            return c.sem(f"{name}_{n}")

        w_up = sb("w_up", [P, 2, width], F32)
        w_down = sb("w_down", [P, tiles, DIM], F32)
        if quantised:
            w_int = sb("w_int", [P, 2, width], I32)
        if zeros is not None:
            z_int = sb("z_int", [P, 2, width], I32)
            s_all = sb("s_all", [P, 2, width], F32)
        if scale is not None:
            sc = sb("sc", [P, 3], F32)
        gate = sb("gate", [P, 2, HALF], F32)
        hidden = sb("hidden", [P, tiles, TOK], F32)
        g_bank, u_bank = c.bank[0:2], c.bank[2:4]
        tail = Tail(c, c.bank[4:6], c.bank[6:8], last is not None)
        loaded = [sem(f"loaded{i}") for i in range(2)]
        scale_loaded, down_loaded = sem("scale_loaded"), sem("down_loaded")
        centred, dequantised = sem("centred"), sem("dequantised")
        gate_done, up_done = sem("gate_done"), sem("up_done")
        gated, product, stored = sem("gated"), sem("product"), sem("stored")

        with nc.Block() as block:

            @block.sync
            def _(sp):
                if scale is not None:
                    for i, s in enumerate(scale):
                        sp.dma_start(sc[:, i:i + 1], s.partition_broadcast(P)).then_inc(scale_loaded, 16)

                def load(f, slot, first):
                    if not first and quantised:
                        sp.wait_ge(dequantised, f - 1)
                    elif not first:
                        sp.wait_ge(up_done, 2 * f - 2)
                    dst = w_int if quantised else w_up
                    sp.dma_start(dst[:, slot, :], weights[f]).then_inc(loaded[slot], 16)
                    if zeros is not None:
                        sp.dma_start(z_int[:, slot, :], zeros[f].partition_broadcast(P)).then_inc(loaded[slot], 16)
                        sp.dma_start(s_all[:, slot, :], scales[f].partition_broadcast(P)).then_inc(loaded[slot], 16)

                def load_all(f, slot, first):
                    load(f, slot, first)
                    if first and slot == 1 and extra_loads is not None:
                        extra_loads(sp)
                    if first and slot == 1 and not quantised:
                        sp.dma_start(w_down[:, :, :], down).then_inc(down_loaded, 16)

                each_tile(sp, tiles, load_all)
                if last is not None:
                    for t in range(NT):
                        sp.wait_ge(tail.normed, tail.base + t + 1)
                        sp.dma_start(last[t], c.x_tok[:, t, :]).then_inc(stored, 16)
                    sp.wait_ge(stored, 16 * NT)

            if extra_pool is not None:
                block.gpsimd(extra_pool)

            @block.tensor
            def _(pe):
                if extra_pe is not None:
                    extra_pe[0](pe)

                def gate_and_up(f, slot, first):
                    if quantised:
                        pe.wait_ge(dequantised, f + 1)
                    else:
                        pe.wait_ge(loaded[slot], 8 * (f - slot) + 16)
                    for half in range(2):
                        if not (first and slot == 0):
                            pe.wait_ge(product, 2 * f + half - 1)
                        for which, bank, done in ((0, g_bank, gate_done), (1, u_bank, up_done)):
                            for k in range(KC):
                                at = (which * KC + k) * P
                                ins = nc.tensor.matmul(bank[half][:, :], w_up[:, slot, at:at + P],
                                                       c.x_feat[:, k, half * HALF:(half + 1) * HALF],
                                                       start=k == 0, stop=k == KC - 1)
                            ins.then_inc(done, 1)

                each_tile(pe, tiles, gate_and_up)
                if not quantised:
                    pe.wait_ge(down_loaded, 16)
                pe.wait_ge(product, 2 * tiles)
                for t in range(NT):
                    if t >= 2:
                        pe.wait_ge(tail.out_taken, tail.base + t - 1)
                    rows = slice(t * P, (t + 1) * P)
                    if extra_pe is not None:
                        extra_pe[1](pe, t, tail.out_bank[t % 2])
                    for f in range(tiles):
                        ins = nc.tensor.matmul(tail.out_bank[t % 2][:, :], hidden[:, f, rows], w_down[:, f, :],
                                               start=f == 0 and extra_pe is None, stop=f == tiles - 1)
                    ins.then_inc(tail.out_ready, 1)
                    if t:
                        tail.pe(pe, t - 1)
                tail.pe(pe, NT - 1)

            @block.scalar
            def _(act):
                if extra_act is not None:
                    extra_act(act)
                if scale is not None:
                    act.wait_ge(scale_loaded, 16 * len(scale))

                def silu(f, slot, first):
                    for half in range(2):
                        act.wait_ge(gate_done, 2 * f + half + 1)
                        if not (first and slot == 0):
                            act.wait_ge(product, 2 * f + half - 1)
                        nc.scalar.activation(gate[:, half, :], g_bank[half][:, :], ACT.Silu).then_inc(gated, 1)

                each_tile(act, tiles, silu)
                tail.act(act)

            @block.vector
            def _(dve):
                if scale is not None:
                    dve.wait_ge(scale_loaded, 16 * len(scale))

                def dequantise(f, slot, first):
                    n = 2 * KC * P
                    dve.wait_ge(loaded[slot], (8 if zeros is None else 24) * (f - slot + 2))
                    if not first:
                        dve.wait_ge(up_done, 2 * f - 2)
                    if zeros is None:
                        nc.vector.tensor_scalar(w_up[:, slot, 0:n // 2], w_int[:, slot, 0:n // 2],
                                                sc[:, 0:1], None, ALU.mult)
                        nc.vector.tensor_scalar(w_up[:, slot, n // 2:n], w_int[:, slot, n // 2:n],
                                                sc[:, 1:2], None, ALU.mult)
                        nc.vector.tensor_scalar(w_down[:, f, :], w_int[:, slot, n:width], sc[:, 2:3], None,
                                                ALU.mult).then_inc(dequantised, 1)
                        return
                    nc.vector.tensor_tensor(w_up[:, slot, :], w_int[:, slot, :], z_int[:, slot, :],
                                            ALU.subtract).then_inc(centred, 1)
                    dve.wait_ge(centred, f + 1)
                    nc.vector.tensor_tensor(w_down[:, f, :], w_up[:, slot, n:width], s_all[:, slot, n:width],
                                            ALU.mult)
                    nc.vector.tensor_tensor(w_up[:, slot, 0:n], w_up[:, slot, 0:n], s_all[:, slot, 0:n],
                                            ALU.mult).then_inc(dequantised, 1)

                def multiply(f):
                    for half in range(2):
                        dve.wait_ge(gated, 2 * f + half + 1)
                        dve.wait_ge(up_done, 2 * f + half + 1)
                        nc.vector.tensor_tensor(hidden[:, f, half * HALF:(half + 1) * HALF], gate[:, half, :],
                                                u_bank[half][:, :], ALU.mult).then_inc(product, 1)

                def tile(f, slot, first):
                    multiply(f)
                    if quantised:
                        dequantise(f + 2, slot, False)

                if quantised:
                    dequantise(0, 0, True)
                    dequantise(1, 1, True)
                if extra_dve is not None:
                    extra_dve(dve)
                each_tile(dve, tiles - 2, tile)
                multiply(tiles - 2)
                multiply(tiles - 1)
                for t in range(NT):
                    tail.dve(dve, t)


def gradient_ffn(c, a):
    nc = c.nc
    G, GRAD_ORDER_MIN, THD = 6, 4, 2.5
    tiles = a["L0_w"].shape[0]
    with ExitStack() as own:
        def sb(n, shape):
            return c.sb(f"series_{n}", shape, F32, own)

        w_proj = sb("w_proj", [P, 2, KC, P])
        w_fuse = sb("w_fuse", [P, G + 1, DIM])
        terms = sb("terms", [P, G + 1, TOK])
        delta, keep = sb("delta", [P, TOK]), sb("keep", [P, TOK])
        point, disc = sb("point", [P, 1]), sb("disc", [P, G])
        diff, ratio = sb("diff", [P, G]), sb("ratio", [P, G])
        proj_loaded, small_loaded = c.sem("series_proj_loaded"), c.sem("series_small_loaded")
        fuse_loaded, projected = c.sem("series_fuse_loaded"), c.sem("series_projected")
        diff_ready, ratio_ready = c.sem("series_diff_ready"), c.sem("series_ratio_ready")
        step = c.sem("series_step")

        def loads(sp):
            c.rot.load(sp, a)
            sp.dma_start(w_proj[:, :, :, :], a["L0_proj"]).then_inc(proj_loaded, 16)
            sp.dma_start(point[:, :], a["L0_point"]).then_inc(small_loaded, 16)
            sp.dma_start(disc[:, :], a["L0_disc"].partition_broadcast(P)).then_inc(small_loaded, 16)
            sp.dma_start(w_fuse[:, :, :], a["L0_fuse"]).then_inc(fuse_loaded, 16)

        def project(pe):
            pe.wait_ge(proj_loaded, 16)
            for which in range(2):
                for half in range(2):
                    for k in range(KC):
                        ins = nc.tensor.matmul(c.bank[4 + 2 * which + half][:, :], w_proj[:, which, k, :],
                                               c.x_feat[:, k, half * HALF:(half + 1) * HALF],
                                               start=k == 0, stop=k == KC - 1)
            ins.then_inc(projected, 1)

        def series(pe, t, bank):
            if t == 0:
                pe.wait_ge(fuse_loaded, 16)
                pe.wait_ge(step, G + 5)
            for m in range(G + 1):
                nc.tensor.matmul(bank[:, :], terms[:, m, t * P:(t + 1) * P], w_fuse[:, m, :],
                                 start=m == 0, stop=False)

        def ratios(act):
            c.rot.act(act)
            act.wait_ge(diff_ready, 2)
            nc.scalar.activation(ratio[:, :], diff[:, :], ACT.Exp).then_inc(ratio_ready, 1)

        def make_terms(dve):
            count = 0

            def then(ins):
                nonlocal count
                count += 1
                ins.then_inc(step, 1)
                dve.wait_ge(step, count)

            dve.wait_ge(small_loaded, 32)
            nc.vector.tensor_scalar(diff[:, 0:1], disc[:, 0:1], -1.0, None, ALU.mult).then_inc(diff_ready, 1)
            nc.vector.tensor_tensor(diff[:, 1:G], disc[:, 0:G - 1], disc[:, 1:G], ALU.subtract).then_inc(diff_ready, 1)
            c.rot.dve(dve)
            dve.wait_ge(projected, 1)
            for half in range(2):
                cols = slice(half * HALF, (half + 1) * HALF)
                nc.vector.tensor_copy(terms[:, 0, cols], c.bank[4 + half][:, :])
                then(nc.vector.tensor_scalar(delta[:, cols], c.bank[6 + half][:, :], point[:, 0:1], None,
                                             ALU.subtract))
            then(nc.vector.tensor_scalar(keep[:, :], delta[:, :], THD, None, ALU.is_le))
            then(nc.vector.scalar_tensor_tensor(keep[:, :], delta[:, :], -THD, keep[:, :], ALU.is_ge, ALU.mult))
            dve.wait_ge(ratio_ready, 1)
            for m in range(1, G + 1):
                then(nc.vector.scalar_tensor_tensor(terms[:, m, :], terms[:, m - 1, :], ratio[:, m - 1:m],
                                                    delta[:, :], ALU.mult, ALU.mult))
                if m == GRAD_ORDER_MIN + 1:
                    then(nc.vector.tensor_tensor(terms[:, m, :], terms[:, m, :], keep[:, :], ALU.mult))

        swiglu(c, "L0_attn", tiles, a["L0_w"], down=a["L0_down"], extra_loads=loads, extra_dve=make_terms,
               extra_pe=(project, series), extra_act=ratios, extra_pool=c.rot.pool)


def product_tiles(c, pe, tail, w, t, chunks=KC):
    nc = c.nc
    if t >= 2:
        pe.wait_ge(tail.out_taken, tail.base + t - 1)
    for k in range(chunks):
        ins = nc.tensor.matmul(tail.out_bank[t % 2][:, :], c.x_feat[:, k, t * P:(t + 1) * P], w[:, k, :],
                               start=k == 0, stop=k == chunks - 1)
    ins.then_inc(tail.out_ready, 1)


def merged_lora(c, a):
    nc = c.nc
    E, R, K = 8, 64, P
    RC = E * R // P
    with ExitStack() as own:
        def sb(n, shape):
            return c.sb(f"lora_{n}", shape, F32, own)

        def sem(n):
            return c.sem(f"lora_{n}")

        w_org, w_eff = sb("w_org", [P, KC, DIM]), sb("w_eff", [P, KC, DIM])
        down, up, up_c = sb("down", [P, RC, DIM]), sb("up", [P, RC, DIM]), sb("up_c", [P, RC, DIM])
        wq, keys = sb("wq", [P, KC, K]), sb("keys", [P, E])
        mean, q, q_wide = sb("mean", [P, KC]), sb("q", [P, 1]), sb("q_wide", [P, P])
        top, neg, e, total, inv, coeff = (sb("top", [P, 1]), sb("neg", [P, 1]), sb("e", [P, E]),
                                          sb("total", [P, 1]), sb("inv", [P, 1]), sb("coeff", [P, E]))
        ones = sb("ones", [P, P])
        tail = Tail(c, c.bank[4:6], c.bank[6:8])
        w_loaded, q_loaded = sem("w_loaded"), sem("q_loaded")
        ones_ready, mean_ready, q_ready, wide_ready = sem("ones"), sem("mean"), sem("q"), sem("wide")
        scores_ready, top_ready, e_ready, coeff_ready = sem("scores"), sem("top"), sem("e"), sem("coeff")
        delta_ready, eff_ready, step = sem("delta"), sem("eff"), sem("step")

        with nc.Block() as block:

            @block.sync
            def _(sp):
                sp.dma_start(wq[:, :, :], a["L0_wq"]).then_inc(q_loaded, 16)
                sp.dma_start(keys[:, :], a["L0_keys"]).then_inc(q_loaded, 16)
                sp.dma_start(up[:, :, :], a["L0_up"]).then_inc(w_loaded, 16)
                sp.dma_start(down[:, :, :], a["L0_lora_down"]).then_inc(w_loaded, 16)
                sp.dma_start(w_org[:, :, :], a["L0_org"]).then_inc(w_loaded, 16)

            @block.gpsimd
            def _(pool):
                nc.gpsimd.memset(ones[:, :], 1.0).then_inc(ones_ready, 1)

            @block.tensor
            def _(pe):
                pe.wait_ge(q_loaded, 32)
                pe.wait_ge(mean_ready, 1)
                for k in range(KC):
                    ins = nc.tensor.matmul(c.bank[0][:, 0:1], wq[:, k, :], mean[:, k:k + 1],
                                           start=k == 0, stop=k == KC - 1)
                ins.then_inc(q_ready, 1)
                pe.wait_ge(wide_ready, 1)
                nc.tensor.matmul(c.bank[1][:, 0:E], q_wide[:, :], keys[:, :], start=True, stop=True)\
                    .then_inc(scores_ready, 1)
                pe.wait_ge(w_loaded, 48)
                pe.wait_ge(coeff_ready, 1)
                for i in range(KC):
                    for r in range(RC):
                        ins = nc.tensor.matmul(c.bank[i][:, :], down[:, r, i * P:(i + 1) * P], up_c[:, r, :],
                                               start=r == 0, stop=r == RC - 1)
                    ins.then_inc(delta_ready, 1)
                pe.wait_ge(eff_ready, KC)
                for t in range(NT):
                    product_tiles(c, pe, tail, w_eff, t)
                    if t:
                        tail.pe(pe, t - 1)
                tail.pe(pe, NT - 1)

            @block.scalar
            def _(act):
                act.wait_ge(top_ready, 1)
                nc.scalar.activation(e[:, :], c.bank[1][:, 0:E], ACT.Exp, bias=neg[:, 0:1], scale=K ** -0.5)\
                    .then_inc(e_ready, 1)
                tail.act(act)

            @block.vector
            def _(dve):
                count = 0

                def then(ins):
                    nonlocal count
                    count += 1
                    ins.then_inc(step, 1)
                    dve.wait_ge(step, count)

                then(nc.vector.tensor_reduce(mean[:, :], c.x_feat[:, :, :], AX.X, ALU.add))
                nc.vector.tensor_scalar(mean[:, :], mean[:, :], 1.0 / TOK, None, ALU.mult).then_inc(mean_ready, 1)
                dve.wait_ge(q_ready, 1)
                then(nc.vector.tensor_copy(q[:, :], c.bank[0][:, 0:1]))
                dve.wait_ge(ones_ready, 1)
                nc.vector.tensor_scalar(q_wide[:, :], ones[:, :], q[:, 0:1], None, ALU.mult).then_inc(wide_ready, 1)
                dve.wait_ge(scores_ready, 1)
                then(nc.vector.tensor_reduce(top[:, :], c.bank[1][:, 0:E], AX.X, ALU.max))
                nc.vector.tensor_scalar(neg[:, :], top[:, :], -(K ** -0.5), None, ALU.mult).then_inc(top_ready, 1)
                dve.wait_ge(e_ready, 1)
                then(nc.vector.tensor_reduce(total[:, :], e[:, :], AX.X, ALU.add))
                then(nc.vector.reciprocal(inv[:, :], total[:, :]))
                then(nc.vector.tensor_scalar(coeff[:, :], e[:, :], inv[:, 0:1], None, ALU.mult))
                dve.wait_ge(w_loaded, 48)
                for r in range(RC):
                    for h in range(P // R):
                        rows, expert = slice(h * R, (h + 1) * R), r * (P // R) + h
                        ins = nc.vector.tensor_scalar(up_c[rows, r, :], up[rows, r, :],
                                                      coeff[rows, expert:expert + 1], None, ALU.mult)
                ins.then_inc(coeff_ready, 1)
                for i in range(KC):
                    dve.wait_ge(delta_ready, i + 1)
                    nc.vector.tensor_tensor(w_eff[:, i, :], w_org[:, i, :], c.bank[i][:, :], ALU.add)\
                        .then_inc(eff_ready, 1)
                for t in range(NT):
                    tail.dve(dve, t)


def single_key_attention(c, a):
    nc = c.nc
    KV, PER = 8, 4
    with ExitStack() as own:
        def sb(n, shape):
            return c.sb(f"single_{n}", shape, F32, own)

        def sem(n):
            return c.sem(f"single_{n}")

        wv, wo = sb("wv", [P, KV, DIM]), sb("wo", [P, KV, PER, DIM])
        pair, wo_sum, w_eff = sb("pair", [P, 2, DIM]), sb("wo_sum", [P, KV, DIM]), sb("w_eff", [P, KC, DIM])
        tail = Tail(c, c.bank[4:6], c.bank[6:8])
        wv_loaded, wo_loaded = sem("wv_loaded"), [sem(f"wo_loaded{g}") for g in range(KV)]
        paired, summed, merged, eff_ready = sem("paired"), sem("summed"), sem("merged"), sem("eff_ready")

        with nc.Block() as block:

            @block.sync
            def _(sp):
                sp.dma_start(wv[:, :, :], a["L1_wv"]).then_inc(wv_loaded, 16)
                for g in range(KV):
                    sp.dma_start(wo[:, g, :, :], a["L1_wo"][g]).then_inc(wo_loaded[g], 16)

            @block.tensor
            def _(pe):
                pe.wait_ge(wv_loaded, 16)
                for g in range(KV):
                    pe.wait_ge(summed, g + 1)
                    for i in range(KC):
                        ins = nc.tensor.matmul(c.bank[i][:, :], wv[:, g, i * P:(i + 1) * P], wo_sum[:, g, :],
                                               start=g == 0, stop=g == KV - 1)
                ins.then_inc(merged, 1)
                pe.wait_ge(eff_ready, 1)
                for t in range(NT):
                    product_tiles(c, pe, tail, w_eff, t)
                    if t:
                        tail.pe(pe, t - 1)
                tail.pe(pe, NT - 1)

            @block.scalar
            def _(act):
                tail.act(act)

            @block.vector
            def _(dve):
                for g in range(KV):
                    dve.wait_ge(wo_loaded[g], 16)
                    if g:
                        dve.wait_ge(summed, g)
                    nc.vector.tensor_tensor(pair[:, :, :], wo[:, g, 0:2, :], wo[:, g, 2:4, :], ALU.add)\
                        .then_inc(paired, 1)
                    dve.wait_ge(paired, g + 1)
                    nc.vector.tensor_tensor(wo_sum[:, g, :], pair[:, 0, :], pair[:, 1, :], ALU.add)\
                        .then_inc(summed, 1)
                dve.wait_ge(merged, 1)
                for i in range(KC):
                    ins = nc.vector.tensor_copy(w_eff[:, i, :], c.bank[i][:, :])
                ins.then_inc(eff_ready, 1)
                for t in range(NT):
                    tail.dve(dve, t)


def two_loras(c, a):
    nc = c.nc
    R, SCALING = 64, 16 / 64
    with ExitStack() as own:
        def sb(n, shape):
            return c.sb(f"two_{n}", shape, F32, own)

        def sem(n):
            return c.sem(f"two_{n}")

        base, w_eff, bias = sb("base", [P, KC, DIM]), sb("w_eff", [P, KC, DIM]), sb("bias", [P, DIM])
        low, high = sb("low", [R, 2, DIM]), sb("high", [R, 2, DIM])
        low_sum, high_sum = sb("low_sum", [R, DIM]), sb("high_sum", [R, DIM])
        tail = Tail(c, c.bank[4:6], c.bank[6:8])
        loaded, summed, delta_ready, eff_ready = sem("loaded"), sem("summed"), sem("delta"), sem("eff")
        base_loaded = sem("base_loaded")

        with nc.Block() as block:

            @block.sync
            def _(sp):
                sp.dma_start(low[:, :, :], a["L2_low"]).then_inc(loaded, 16)
                sp.dma_start(high[:, :, :], a["L2_high"]).then_inc(loaded, 16)
                sp.dma_start(base[:, :, :], a["L2_base"]).then_inc(base_loaded, 16)
                sp.dma_start(bias[:, :], a["L2_bias"].partition_broadcast(P)).then_inc(base_loaded, 16)

            @block.tensor
            def _(pe):
                pe.wait_ge(summed, 2)
                for i in range(KC):
                    nc.tensor.matmul(c.bank[i][:, :], low_sum[:, i * P:(i + 1) * P], high_sum[:, :],
                                     start=True, stop=True).then_inc(delta_ready, 1)
                pe.wait_ge(eff_ready, KC)
                for t in range(NT):
                    product_tiles(c, pe, tail, w_eff, t)
                    if t:
                        tail.pe(pe, t - 1)
                tail.pe(pe, NT - 1)

            @block.scalar
            def _(act):
                tail.act(act)

            @block.vector
            def _(dve):
                dve.wait_ge(loaded, 32)
                for pair, total in ((low, low_sum), (high, high_sum)):
                    nc.vector.tensor_tensor(total[:, :], pair[:, 0, :], pair[:, 1, :], ALU.add).then_inc(summed, 1)
                dve.wait_ge(base_loaded, 32)
                for i in range(KC):
                    dve.wait_ge(delta_ready, i + 1)
                    nc.vector.scalar_tensor_tensor(w_eff[:, i, :], c.bank[i][:, :], SCALING, base[:, i, :],
                                                   ALU.mult, ALU.add).then_inc(eff_ready, 1)
                for t in range(NT):
                    tail.dve(dve, t, bias)


C_DIM, C_DEPTH, C_FF = 64, 4, 256


class Rotation:

    LEVELS = 10

    def __init__(self, c, own):
        self.c = c
        self.wave = c.sb("wave", [P, C_DEPTH, TOK], F32)
        self.decay = c.sb("decay", [P, C_DEPTH], F32)
        self.start = c.sb("scan_start", [P, C_DEPTH], F32)
        self.half_ready = c.sem("rot_done")
        self.other = c.sb("rot_other", [P, C_DEPTH, TOK // 2], F32, own)
        self.tmp = c.sb("rot_tmp", [P, C_DEPTH, TOK // 2], F32, own)
        self.par = c.sb("rot_par", [P, 4, C_DEPTH], F32, own)
        self.turn = c.sb("rot_turn", [P, self.LEVELS, 2, C_DEPTH], F32, own)
        self.small = c.sb("rot_small", [P, 8, C_DEPTH], F32, own)
        self.sign = c.sb("rot_sign", [P, 1], F32, own)
        self.loaded, self.step = c.sem("rot_loaded"), c.sem("rot_step")
        self.size_ready, self.root_ready = c.sem("rot_size"), c.sem("rot_root")
        self.decay_ready = c.sem("rot_decay")
        self.turns_ready, self.turn_step = c.sem("rot_turns"), c.sem("rot_turn_step")

    def load(self, sp, a):
        sp.dma_start(self.par[:, :, :], a["L2_par"]).then_inc(self.loaded, 16)

    def act(self, act):
        nc, small = self.c.nc, self.small
        act.wait_ge(self.size_ready, 1)
        nc.scalar.activation(small[:, 5, :], small[:, 4, :], ACT.Sqrt).then_inc(self.root_ready, 1)
        act.wait_ge(self.size_ready, 2)
        nc.scalar.activation(self.decay[:, :], small[:, 6, :], ACT.Tanh).then_inc(self.decay_ready, 1)

    def dve(self, dve):
        nc, small, par = self.c.nc, self.small, self.par
        count = 0

        def then(ins):
            nonlocal count
            count += 1
            ins.then_inc(self.turn_step, 1)
            dve.wait_ge(self.turn_step, count)

        tt, ts, stt = nc.vector.tensor_tensor, nc.vector.tensor_scalar, nc.vector.scalar_tensor_tensor
        big, zero, re, im, size, root, length = (small[:, i, :] for i in range(7))
        dve.wait_ge(self.loaded, 16)
        then(stt(re, par[:, 0, :], -1.0, par[:, 0, :], ALU.mult, ALU.max))
        then(stt(im, par[:, 1, :], -1.0, par[:, 1, :], ALU.mult, ALU.max))
        then(tt(big, re, im, ALU.max))
        then(ts(zero, big, 0.0, None, ALU.is_equal))
        then(tt(length, big, zero, ALU.add))
        then(nc.vector.reciprocal(size, length))
        then(tt(re, par[:, 0, :], size, ALU.mult))
        then(tt(im, par[:, 1, :], size, ALU.mult))
        then(tt(re, re, zero, ALU.add))
        then(tt(size, re, re, ALU.mult))
        then(tt(root, im, im, ALU.mult))
        tt(size, size, root, ALU.add).then_inc(self.size_ready, 1)
        dve.wait_ge(self.root_ready, 1)
        then(tt(length, big, root, ALU.mult))
        nc.vector.tensor_copy(length, length).then_inc(self.size_ready, 1)
        then(nc.vector.reciprocal(size, root))
        then(tt(re, re, size, ALU.mult))
        then(tt(im, im, size, ALU.mult))
        then(tt(size, re, re, ALU.mult))
        then(tt(root, im, im, ALU.mult))
        then(tt(size, size, root, ALU.add))
        then(ts(size, size, -0.5, 1.5, ALU.mult, ALU.add))
        turn = self.turn
        then(tt(turn[:, 0, 0, :], re, size, ALU.mult))
        then(tt(turn[:, 0, 1, :], im, size, ALU.mult))
        for n in range(1, self.LEVELS):
            cos, sin = turn[:, n - 1, 0, :], turn[:, n - 1, 1, :]
            then(tt(re, cos, cos, ALU.mult))
            then(tt(im, sin, sin, ALU.mult))
            then(tt(turn[:, n, 0, :], re, im, ALU.subtract))
            then(stt(turn[:, n, 1, :], cos, 2.0, sin, ALU.mult, ALU.mult))
        nc.vector.tensor_copy(re, re).then_inc(self.turns_ready, 1)

    def pool(self, pool):
        nc, wave, other, tmp = self.c.nc, self.wave, self.other, self.tmp
        count = 0

        def then(ins):
            nonlocal count
            count += 1
            ins.then_inc(self.step, 1)
            pool.wait_ge(self.step, count)

        mul = nc.gpsimd.tensor_tensor
        for half, (re, im, sign) in enumerate(((1.0, 0.0, 1.0), (0.0, 1.0, -1.0))):
            rows = slice(half * C_DIM, (half + 1) * C_DIM)
            nc.gpsimd.memset(wave[rows, :, 0:1], re)
            nc.gpsimd.memset(other[rows, :, 0:1], im)
            then(nc.gpsimd.memset(self.sign[rows, :], sign))
        pool.wait_ge(self.turns_ready, 1)
        for level in range(self.LEVELS):
            n = 1 << level
            cos, sin = (self.turn[:, level, i, :].unsqueeze(2).to_broadcast([P, C_DEPTH, n]) for i in range(2))
            src, dst = slice(0, n), slice(n, 2 * n)
            then(mul(tmp[:, :, src], other[:, :, src], sin, ALU.mult))
            then(mul(wave[:, :, dst], wave[:, :, src], cos, ALU.mult))
            then(mul(wave[:, :, dst], wave[:, :, dst], tmp[:, :, src], ALU.subtract))
            if level < self.LEVELS - 1:
                then(mul(tmp[:, :, src], wave[:, :, src], sin, ALU.mult))
                then(mul(other[:, :, dst], other[:, :, src], cos, ALU.mult))
                then(mul(other[:, :, dst], other[:, :, dst], tmp[:, :, src], ALU.add))
        pool.wait_ge(self.loaded, 16)
        then(mul(tmp[:, :, 0], self.par[:, 2, :], wave[:, :, 1], ALU.mult))
        then(mul(tmp[:, :, 1], self.par[:, 3, :], other[:, :, 1], ALU.mult))
        then(mul(tmp[:, :, 0], tmp[:, :, 0], tmp[:, :, 1], ALU.subtract))
        nc.gpsimd.tensor_scalar(self.start[:, :], tmp[:, :, 0], self.sign[:, 0:1], None, ALU.mult)\
            .then_inc(self.half_ready, 1)


def conv_stack(c, a):
    nc, rot = c.nc, c.rot
    FT = C_FF // P
    LOW = C_DIM
    with ExitStack() as own:
        def sb(n, shape):
            return c.sb(f"conv_{n}", shape, F32, own)

        def sem(n):
            return c.sem(f"conv_{n}")

        w_in, w_out = sb("w_in", [P, KC, LOW]), sb("w_out", [LOW, DIM])
        w1_all, w2 = sb("w1_all", [LOW, C_DEPTH, C_FF]), sb("w2", [P, C_DEPTH, FT, LOW])
        w1 = sb("w1", [LOW, C_FF])
        cols, col, last_cols = sb("cols", [P, C_DEPTH, 4 + FT]), sb("col", [P, 4 + FT]), sb("last_cols", [LOW, 2])
        rows = sb("rows", [P, 2 * C_DEPTH + 1, LOW])
        out_bias = sb("out_bias", [P, DIM])
        fold = sb("fold", [P, LOW])
        fold_sc = sb("fold_sc", [P, C_DEPTH, LOW])
        h, centred, square = sb("h", [P, NT, LOW]), sb("centred", [P, NT, LOW]), sb("square", [P, NT, LOW])
        twice = sb("twice", [P, NT, 2, LOW])
        total, mean, var, rstd = sb("total", [P, NT]), sb("mean", [P, NT]), sb("var", [P, NT]), sb("rstd", [P, NT])
        power = sb("power", [P, NT])
        y, turned, state, back = sb("y", [P, TOK]), sb("turned", [P, TOK]), sb("state", [P, TOK]), sb("back", [P, TOK])
        normed2, hidden = sb("normed2", [LOW, TOK]), sb("hidden", [P, FT, TOK])
        tail = Tail(c, c.bank[4:6], c.bank[6:8])
        tr_bank, conv_bank, ff_bank, mlp_bank = c.bank[0:2], c.bank[2], c.bank[3:7], c.bank[7]

        loaded, const = sem("loaded"), sem("const")
        step, h_in = sem("step"), sem("h_in")
        var_ready, rstd_ready = sem("var_ready"), sem("rstd_ready")
        normed, turned_up, y_ready = sem("normed"), sem("transposed"), sem("y_ready")
        back_ready, conv_ready = sem("back_ready"), sem("conv_ready")
        w1_ready, ff_ready, hidden_ready, mlp_ready = sem("w1_ready"), sem("ff_ready"), sem("hidden"), sem("mlp")
        n2_ready, col_ready = sem("n2_ready"), sem("col_ready")
        LOADS = 16 * 10

        with nc.Block() as block:

            @block.sync
            def _(sp):
                for dst, src in ((w_in, "C_in"), (w_out, "C_out"), (w1_all, "C_w1"), (w2, "C_w2"), (cols, "C_cols"),
                                 (last_cols, "C_last")):
                    sp.dma_start(dst[:], a[src]).then_inc(loaded, 16)
                for i, src in enumerate(("C_b2", "C_sc")):
                    part = rows[:, i * C_DEPTH:(i + 1) * C_DEPTH, :]
                    sp.dma_start(part, a[src].partition_broadcast(P)).then_inc(loaded, 16)
                sp.dma_start(rows[:, 2 * C_DEPTH, :], a["C_bin"].partition_broadcast(P)).then_inc(loaded, 16)
                sp.dma_start(out_bias[:, :], a["C_bout"].partition_broadcast(P)).then_inc(loaded, 16)

            @block.gpsimd
            def _(pool):
                nc.gpsimd.memset(power[:, :], -0.5).then_inc(const, 1)
                nc.gpsimd.memset(fold[:, :], 0.0).then_inc(const, 1)
                pool.wait_ge(const, 2)
                nc.gpsimd.affine_select(out=fold[:, :], in_=fold[:, :], compare_op=ALU.not_equal, fill=1.0,
                                        base=0, pattern=[[-1, LOW]], channel_multiplier=1).then_inc(const, 1)
                pool.wait_ge(const, 3)
                nc.gpsimd.affine_select(out=fold[:, :], in_=fold[:, :], compare_op=ALU.not_equal, fill=1.0,
                                        base=-LOW, pattern=[[-1, LOW]], channel_multiplier=1).then_inc(const, 1)
                pool.wait_ge(const, 4)
                pool.wait_ge(loaded, LOADS)
                for i in range(C_DEPTH):
                    ins = nc.gpsimd.tensor_tensor(fold_sc[:, i, :], fold[:, :], rows[:, C_DEPTH + i, :], ALU.mult)
                ins.then_inc(const, 1)

                def root(n):
                    pool.wait_ge(var_ready, n + 1)
                    nc.gpsimd.tensor_tensor(rstd[:, :], var[:, :], power[:, :], ALU.pow).then_inc(rstd_ready, 1)

                def prepare(i, first):
                    if not first:
                        pool.wait_ge(ff_ready, 4 * i)
                    nc.gpsimd.tensor_copy(w1[:, :], w1_all[:, i, :]).then_inc(w1_ready, 1)
                    if not first:
                        pool.wait_ge(hidden_ready, 4 * i)
                    nc.gpsimd.tensor_copy(col[:, :], cols[:, i, :]).then_inc(col_ready, 1)
                    root(2 * i)
                    root(2 * i + 1)

                prepare(0, True)
                with pool.Fori(1, C_DEPTH) as i:
                    prepare(i, False)
                root(2 * C_DEPTH)

            @block.tensor
            def _(pe):
                pe.wait_ge(loaded, LOADS)
                for t in range(NT):
                    for k in range(KC):
                        ins = nc.tensor.matmul(conv_bank[:, t * LOW:(t + 1) * LOW],
                                               c.x_feat[:, k, t * P:(t + 1) * P], w_in[:, k, :],
                                               start=k == 0, stop=k == KC - 1)
                ins.then_inc(h_in, 1)

                def transposes(n):
                    pe.wait_ge(normed, n + 1)
                    for half in range(2):
                        for t in range(NT // 2):
                            ins = nc.tensor.transpose(tr_bank[half][:, t * P:(t + 1) * P],
                                                      twice[:, half * NT // 2 + t, :, :]
                                                      .rearrange("p a d -> p (a d)"), c.ident[:, :])
                        ins.then_inc(turned_up, 1)

                def layer(i):
                    transposes(2 * i)
                    for half in range(2):
                        pe.wait_ge(back_ready, 2 * i + half + 1)
                        for t in range(half * NT // 2, (half + 1) * NT // 2):
                            ins = nc.tensor.matmul(conv_bank[:, t * LOW:(t + 1) * LOW],
                                                   back[:, t * P:(t + 1) * P], fold_sc[:, i, :],
                                                   start=True, stop=True)
                    ins.then_inc(conv_ready, 1)
                    transposes(2 * i + 1)
                    pe.wait_ge(w1_ready, i + 1)
                    for half in range(2):
                        pe.wait_ge(n2_ready, 2 * i + half + 1)
                        for f in range(FT):
                            nc.tensor.matmul(ff_bank[2 * half + f][:, :], w1[:, f * P:(f + 1) * P],
                                             normed2[:, half * HALF:(half + 1) * HALF],
                                             start=True, stop=True).then_inc(ff_ready, 1)
                    for half in range(2):
                        pe.wait_ge(hidden_ready, 4 * i + 2 * half + 2)
                        for t in range(half * NT // 2, (half + 1) * NT // 2):
                            for f in range(FT):
                                ins = nc.tensor.matmul(mlp_bank[:, t * LOW:(t + 1) * LOW],
                                                       hidden[:, f, t * P:(t + 1) * P], w2[:, i, f, :],
                                                       start=f == 0, stop=f == FT - 1)
                    ins.then_inc(mlp_ready, 1)

                pe.wait_ge(const, 5)
                with pe.Fori(0, C_DEPTH) as i:
                    layer(i)
                transposes(2 * C_DEPTH)
                pe.wait_ge(n2_ready, 2 * C_DEPTH + 2)
                for t in range(NT):
                    if t >= 2:
                        pe.wait_ge(tail.out_taken, tail.base + t - 1)
                    nc.tensor.matmul(tail.out_bank[t % 2][:, :], normed2[:, t * P:(t + 1) * P], w_out[:, :],
                                     start=True, stop=True).then_inc(tail.out_ready, 1)
                    if t:
                        tail.pe(pe, t - 1)
                tail.pe(pe, NT - 1)

            @block.scalar
            def _(act):
                act.wait_ge(loaded, LOADS)

                def affine(n, weight, bias):
                    for half in range(2):
                        act.wait_ge(turned_up, 2 * n + half + 1)
                        nc.scalar.activation(normed2[:, half * HALF:(half + 1) * HALF], tr_bank[half][0:LOW, :],
                                             ACT.Identity, scale=weight, bias=bias).then_inc(n2_ready, 1)

                with act.Fori(0, C_DEPTH) as i:
                    act.wait_ge(col_ready, i + 1)
                    for half in range(2):
                        act.wait_ge(turned_up, 4 * i + half + 1)
                        nc.scalar.activation(y[:, half * HALF:(half + 1) * HALF], tr_bank[half][:, :], ACT.Silu,
                                             scale=col[:, 0:1], bias=col[:, 1:2])\
                            .then_inc(y_ready, 1)
                    affine(2 * i + 1, col[0:LOW, 2:3], col[0:LOW, 3:4])
                    for half in range(2):
                        for f in range(FT):
                            act.wait_ge(ff_ready, 4 * i + 2 * half + f + 1)
                            nc.scalar.activation(hidden[:, f, half * HALF:(half + 1) * HALF],
                                                 ff_bank[2 * half + f][:, :], ACT.Silu,
                                                 bias=col[:, 4 + f:5 + f]).then_inc(hidden_ready, 1)
                affine(2 * C_DEPTH, last_cols[:, 0:1], last_cols[:, 1:2])
                tail.act(act)

            @block.vector
            def _(dve):
                state_of = {"count": 0, "base": 0}

                def then(ins):
                    state_of["count"] += 1
                    ins.then_inc(step, 1)
                    dve.wait_ge(step, state_of["base"] + state_of["count"])

                tt, ts = nc.vector.tensor_tensor, nc.vector.tensor_scalar

                def by_tile(x):
                    return x[:, :].unsqueeze(2).to_broadcast([P, NT, LOW])

                def norm(n, copies):
                    then(nc.vector.tensor_reduce(total[:, :], h[:, :, :], AX.X, ALU.add))
                    then(ts(mean[:, :], total[:, :], 1.0 / LOW, None, ALU.mult))
                    then(tt(centred[:, :, :], h[:, :, :], by_tile(mean), ALU.subtract))
                    then(tt(square[:, :, :], centred[:, :, :], centred[:, :, :], ALU.mult))
                    then(nc.vector.tensor_reduce(total[:, :], square[:, :, :], AX.X, ALU.add))
                    ts(var[:, :], total[:, :], 1.0 / LOW, EPS, ALU.mult, ALU.add).then_inc(var_ready, 1)
                    dve.wait_ge(rstd_ready, n + 1)
                    for j in range(copies):
                        ins = tt(twice[:, :, j, :], centred[:, :, :], by_tile(rstd), ALU.mult)
                    ins.then_inc(normed, 1)

                h_flat = h[:, :, :].rearrange("p t d -> p (t d)")
                dve.wait_ge(loaded, LOADS)
                dve.wait_ge(rot.half_ready, 1)
                dve.wait_ge(rot.decay_ready, 1)
                dve.wait_ge(h_in, 1)
                then(nc.vector.tensor_copy(h_flat, conv_bank[:, :]))
                then(tt(h[:, :, :], h[:, :, :],
                        rows[:, 2 * C_DEPTH, :].unsqueeze(1).to_broadcast([P, NT, LOW]), ALU.add))
                PRE, STEPS = state_of["count"], 17

                with dve.Fori(0, C_DEPTH) as i:
                    state_of["count"], state_of["base"] = PRE, STEPS * i
                    norm(2 * i, 2)
                    for half in range(2):
                        part = slice(half * HALF, (half + 1) * HALF)
                        dve.wait_ge(y_ready, 2 * i + half + 1)
                        then(tt(turned[:, part], y[:, part], rot.wave[:, i, part], ALU.mult))
                        before = rot.start[:, bass.ds(i, 1)] if half == 0 else state[:, HALF - 1:HALF]
                        then(nc.vector.tensor_tensor_scan(state[:, part],
                                                          rot.decay[:, bass.ds(i, 1)].to_broadcast([P, HALF]),
                                                          turned[:, part], before, ALU.mult, ALU.add))
                        tt(back[:, part], state[:, part], rot.wave[:, i, part], ALU.mult).then_inc(back_ready, 1)
                    dve.wait_ge(conv_ready, i + 1)
                    then(tt(h_flat, h_flat, conv_bank[:, :], ALU.add))
                    norm(2 * i + 1, 1)
                    dve.wait_ge(mlp_ready, i + 1)
                    then(tt(h_flat, h_flat, mlp_bank[:, :], ALU.add))
                    then(tt(h[:, :, :], h[:, :, :], rows[:, bass.ds(i, 1), :].to_broadcast([P, NT, LOW]), ALU.add))
                    assert state_of["count"] == PRE + STEPS, state_of
                state_of["count"], state_of["base"] = PRE + STEPS * C_DEPTH, 0
                norm(2 * C_DEPTH, 1)
                for t in range(NT):
                    tail.dve(dve, t, out_bias)


HEADS, HD = 32, 16
PAIRS = HEADS // 2
SPLIT = 3 * 2 * HD
SHIFTED = SPLIT + 4


def attention_plan():
    order = list(range(NT - 1, -1, -1))

    def max_units(i):
        keys = (order[i] + 1) * P
        found = []
        for lo in range(0, keys, HALF):
            n = min(HALF, keys - lo)
            per = HALF // n
            found += [(range(h, min(h + per, HEADS)), lo, n) for h in range(0, HEADS, per)]
        return found

    plan, pending, step, value_lag = [], [], 0, 2
    n_max = n_score = n_value = 0

    def later(steps, *event):
        pending.append((step + steps, event))

    def flush(everything=False):
        while pending and (everything or min(pending)[0] <= step):
            at = pending.index(min(pending, key=lambda x: x[0]))
            _, event = pending.pop(at)
            plan.append(event)
            if event[0] == "value" and event[4] and event[3] % 2:
                later(3, "heads", event[1], event[3] // 2)
            elif event[0] == "heads" and event[2] == 3:
                later(2, "turn", event[1])
            elif event[0] == "turn":
                later(2, "project", event[1])
            elif event[0] == "project":
                later(3, "std", event[1])
            elif event[0] == "std":
                later(1, "norm", event[1])
            elif event[0] == "norm":
                later(3, "feat", event[1])

    for unit in max_units(0):
        plan.append(("max", 0, n_max, *unit))
        n_max += 1
    plan += [("shift", 0), ("shift_rows", 0)]
    for i, qt in enumerate(order):
        todo = max_units(i + 1) if i + 1 < NT else []
        total, steps = len(todo), 8 * (qt + 1)
        for n in range(steps):
            u, kt = divmod(n, qt + 1)
            plan.append(("score", i, n_score, u, kt))
            later(value_lag, "value", i, n_score, u, kt == qt, kt)
            n_score += 1
            step += 1
            flush()
            done = total - len(todo)
            want = min(total, -(-total * (n + 1) * 5 // (4 * steps)))
            for _ in range(want - done):
                plan.append(("max", i + 1, n_max, *todo.pop(0)))
                n_max += 1
                if not todo:
                    plan.append(("shift", i + 1))
                    later(2, "shift_rows", i + 1)
        rest = [p for p in pending if p[1][0] == "shift_rows"]
        for p in rest:
            pending.remove(p)
            plan.append(p[1])
    step += 1000
    flush(everything=True)
    while pending:
        flush(everything=True)
    return order, plan


def causal_attention(c, a):
    nc = c.nc
    order, plan = attention_plan()
    turn_use = {e: n for n, e in enumerate(e for e in plan if e[0] in ("shift_rows", "heads", "turn", "feat"))}
    SCALE = HD ** -0.5
    HIDE = -3.0e38
    with ExitStack() as own:
        def sb(n, shape, dt=F32, scope=own):
            return c.sb(f"mqa_{n}", shape, dt, scope)

        def sem(n):
            return c.sem(f"mqa_{n}")

        wq, wo = sb("wq", [P, KC, DIM]), sb("wo", [P, KC, DIM])
        wk = sb("wk", [P, KC, 2, P])
        bq, bk, bo = sb("bq", [P, KC]), sb("bk", [P, 2]), sb("bo", [P, DIM])
        stack = sb("stack", [P, PAIRS, TOK], F32R)
        q_hi, q_lo = sb("q_hi", [P, 2, TOK], F32R), sb("q_lo", [P, 2, TOK], F32R)
        keys = sb("keys", [P, 2, TOK], F32R)
        v_feat, v = sb("v_feat", [P, TOK]), sb("v", [P, NT, 2 * HD])
        ident_b, hide_k, hide_q = sb("ident_b", [P, P], BF16), sb("hide_k", [P, P], BF16), sb("hide_q", [P, 4, P], BF16)
        top, shift = sb("top", [P, 2, 2, HEADS]), sb("shift", [P, 2, 2, 2, PAIRS], F32R)
        both = sb("both", [P, HEADS])
        rows = sb("rows", [4 * PAIRS, 2, P], F32R)
        prob = sb("prob", [P, 4, HALF])
        o_sb = sb("o_sb", [P, 4, P])
        inv = sb("inv", [P, 2, 4])
        attn, a_feat = sb("attn", [P, 2, DIM]), sb("a_feat", [P, 2, KC, P])
        max_bank, score_bank, value_bank = c.bank[0:2], c.bank[2:4], c.bank[4:6]
        turn_bank, out_bank = c.bank[6], c.bank[7]

        w_loaded, wo_loaded, const = sem("w_loaded"), sem("wo_loaded"), sem("const")
        q_ready, q_rounded, q_split = sem("q_ready"), sem("q_rounded"), sem("q_split")
        k_ready, k_rounded, k_split, v_turned, v_ready = (sem("k_ready"), sem("k_rounded"), sem("k_split"),
                                                          sem("v_turned"), sem("v_ready"))
        stacked = [sem(f"stacked{i}") for i in range(KC)]
        max_ready, max_taken, step = sem("max_ready"), sem("max_taken"), sem("step")
        shift_ready, shift_turned = sem("shift_ready"), sem("shift_turned")
        rows_sent = [sem(f"rows_sent{i}") for i in range(2)]
        score_ready, exp_ready, value_done = sem("score_ready"), sem("exp_ready"), sem("value_done")
        o_copied, heads_turned = sem("o_copied"), sem("heads_turned")
        turned, out_ready, added = sem("turned"), sem("out_ready"), sem("added")
        var_ready, std_ready, normed = sem("var_ready"), sem("std_ready"), sem("normed")
        feat_turned, turn_taken = sem("feat_turned"), sem("turn_taken")

        def cols(t):
            return slice(t * P, (t + 1) * P)

        with nc.Block() as block:

            @block.sync
            def _(sp):
                for dst, src in ((wq, "A_wq"), (wk, "A_wk"), (bq, "A_bq"), (bk, "A_bk")):
                    sp.dma_start(dst[:], a[src]).then_inc(w_loaded, 16)
                sp.dma_start(wo[:, :, :], a["A_wo"]).then_inc(wo_loaded, 16)
                sp.dma_start(bo[:, :], a["A_bo"].partition_broadcast(P)).then_inc(wo_loaded, 16)
                for m in range(KC):
                    sp.wait_ge(q_split, 2 * m + 2)
                    for j in range(4):
                        src = slice(32 * j, 32 * j + 32)
                        for slot, part in enumerate((q_hi, q_hi, q_lo)):
                            sp.dma_start(stack[32 * slot:32 * slot + 32, 4 * m + j, :].bitcast(F32),
                                         part[src, m % 2, :].bitcast(F32))\
                                .then_inc(stacked[m], 16)
                for event in plan:
                    if event[0] == "shift_rows":
                        i = event[1]
                        sp.wait_ge(turn_taken, turn_use[event] + 1)
                        sp.dma_start(stack[SPLIT:SHIFTED, :, cols(order[i])].bitcast(F32), rows[:, i % 2, :].bitcast(F32))\
                            .then_inc(rows_sent[i % 2], 16)

            @block.gpsimd
            def _(pool):
                nc.gpsimd.memset(ident_b[:, :], 0.0)
                nc.gpsimd.memset(hide_k[:, :], 0.0)
                nc.gpsimd.memset(hide_q[:, :, :], 0.0).then_inc(const, 1)
                pool.wait_ge(const, 1)
                nc.gpsimd.affine_select(out=ident_b[:, :], in_=ident_b[:, :], compare_op=ALU.not_equal, fill=1.0,
                                        base=0, pattern=[[-1, P]], channel_multiplier=1)
                nc.gpsimd.affine_select(out=hide_k[:, :], in_=hide_k[:, :], compare_op=ALU.is_ge, fill=HIDE,
                                        base=0, pattern=[[-1, P]], channel_multiplier=1)
                nc.gpsimd.affine_select(out=hide_q[:, :, :], in_=hide_q[:, :, :], compare_op=ALU.is_ge, fill=HIDE,
                                        base=0, pattern=[[0, 4], [1, P]], channel_multiplier=-1).then_inc(const, 1)

            @block.tensor
            def _(pe):
                pe.wait_ge(w_loaded, 64)
                for head in range(2):
                    for half in range(2):
                        for k in range(KC):
                            ins = nc.tensor.matmul(c.bank[4 + 2 * head + half], wk[:, k, head, :],
                                                   c.x_feat[:, k, half * HALF:(half + 1) * HALF],
                                                   start=k == 0, stop=k == KC - 1)
                        ins.then_inc(k_ready, 1)
                for m in range(KC):
                    for half in range(2):
                        n = 2 * m + half
                        if n >= 4:
                            pe.wait_ge(q_split, n - 3)
                        for k in range(KC):
                            ins = nc.tensor.matmul(c.bank[n % 4], wq[:, k, cols(m)],
                                                   c.x_feat[:, k, half * HALF:(half + 1) * HALF],
                                                   start=k == 0, stop=k == KC - 1)
                        ins.then_inc(q_ready, 1)
                pe.wait_ge(k_split, 4)
                for t in range(NT):
                    ins = nc.tensor.transpose(c.bank[4][:, t * 2 * HD:(t + 1) * 2 * HD], v_feat[SPLIT:P, cols(t)],
                                              c.ident[SPLIT:P, SPLIT:P])
                ins.then_inc(v_turned, 1)
                pe.wait_ge(q_split, 8)
                pe.wait_ge(v_ready, 2)
                pe.wait_ge(const, 2)

                for event in plan:
                    kind, i = event[0], event[1]
                    qt = order[i]
                    if turn_use.get(event, 0):
                        pe.wait_ge(turn_taken, turn_use[event])
                    if kind == "max":
                        _, _, n, heads, lo, width = event
                        if n >= 2:
                            pe.wait_ge(max_taken, n - 1)
                        for at, head in enumerate(heads):
                            if i == 0 and lo == 0 and head % 8 == 0:
                                pe.wait_ge(stacked[head // 8], 16 * 12)
                            masked = lo + width == (qt + 1) * P
                            out = max_bank[n % 2]
                            ins = nc.tensor.matmul(out[:, at * width:(at + 1) * width],
                                                   stack[0:SPLIT, head // 2, cols(qt)],
                                                   keys[0:SPLIT, head % 2, lo:lo + width],
                                                   start=True, stop=not masked)
                            if masked:
                                ins = nc.tensor.matmul(out[:, (at + 1) * width - P:(at + 1) * width],
                                                       ident_b[:, :], hide_k[:, :], start=False, stop=True)
                        ins.then_inc(max_ready, 1)
                    elif kind == "shift_rows":
                        pe.wait_ge(shift_ready, i + 1)
                        nc.tensor.transpose(turn_bank[0:4 * PAIRS, 0:P],
                                            shift[:, i % 2, :, :, :].rearrange("p h s j -> p (h s j)").bitcast(F32),
                                            c.ident[:, :]).then_inc(shift_turned, 1)
                    elif kind == "score":
                        _, _, n, u, kt = event
                        if u == 0 and kt == 0:
                            pe.wait_ge(rows_sent[i % 2], 16 * (i // 2 + 1))
                        if n >= 2:
                            pe.wait_ge(exp_ready, n - 1)
                        g, head = divmod(u, 2)
                        ins = nc.tensor.matmul(score_bank[n % 2], keys[0:SHIFTED, head, cols(kt)],
                                               stack[0:SHIFTED, 4 * g:4 * g + 4, cols(qt)],
                                               start=True, stop=kt != qt)
                        if kt == qt:
                            ins = nc.tensor.matmul(score_bank[n % 2], ident_b[:, :],
                                                   hide_q[:, :, :].rearrange("p a b -> p (a b)"),
                                                   start=False, stop=True)
                        ins.then_inc(score_ready, 1)
                    elif kind == "value":
                        _, _, n, u, final, kt = event
                        unit = 8 * i + u
                        if kt == 0 and unit >= 2:
                            pe.wait_ge(o_copied, unit - 1)
                        pe.wait_ge(exp_ready, n + 1)
                        for j in range(4):
                            ins = nc.tensor.matmul(value_bank[unit % 2][32 * j:32 * j + 32, 0:P], v[:, kt, :],
                                                   prob[:, n % 4, cols(j)], start=kt == 0, stop=final)
                        ins.then_inc(value_done, 1)
                    elif kind == "heads":
                        g = event[2]
                        unit = 8 * i + 2 * g
                        pe.wait_ge(o_copied, unit + 2)
                        for j in range(2):
                            ins = nc.tensor.transpose(turn_bank[:, cols(j)], o_sb[:, (unit + j) % 4, :], c.ident[:, :])
                        ins.then_inc(heads_turned, 1)
                    elif kind == "turn":
                        pe.wait_ge(turn_taken, turn_use[("heads", i, 3)] + 1)
                        for k in range(KC):
                            ins = nc.tensor.transpose(turn_bank[:, cols(k)], attn[:, i % 2, cols(k)], c.ident[:, :])
                        ins.then_inc(turned, 1)
                    elif kind == "project":
                        if i == 0:
                            pe.wait_ge(wo_loaded, 32)
                        else:
                            pe.wait_ge(added, i)
                        pe.wait_ge(turn_taken, turn_use[("turn", i)] + 1)
                        for k in range(KC):
                            ins = nc.tensor.matmul(out_bank, a_feat[:, i % 2, k, :], wo[:, k, :],
                                                   start=k == 0, stop=k == KC - 1)
                        ins.then_inc(out_ready, 1)
                    elif kind == "feat":
                        pe.wait_ge(normed, i + 1)
                        for k in range(KC):
                            ins = nc.tensor.transpose(turn_bank[:, cols(k)], c.x_tok[:, qt, cols(k)], c.ident[:, :])
                        ins.then_inc(feat_turned, 1)

            @block.scalar
            def _(act):
                act.wait_ge(w_loaded, 64)
                for head in range(2):
                    for half in range(2):
                        part, bank = slice(half * HALF, (half + 1) * HALF), c.bank[4 + 2 * head + half]
                        act.wait_ge(k_ready, 2 * head + half + 1)
                        if head == 0:
                            nc.scalar.activation(v_feat[SPLIT:P, part], bank[SPLIT:P, :], ACT.Identity,
                                                 bias=bk[SPLIT:P, 0:1])
                        nc.scalar.activation(keys[0:SPLIT, head, part], bank[0:SPLIT, :], ACT.Identity,
                                             bias=bk[0:SPLIT, head:head + 1]).then_inc(k_rounded, 1)
                for n in range(2 * KC):
                    m, half = divmod(n, 2)
                    act.wait_ge(q_ready, n + 1)
                    if m >= 2 and half == 0:
                        act.wait_ge(stacked[m - 2], 16 * 12)
                    nc.scalar.activation(q_hi[:, m % 2, half * HALF:(half + 1) * HALF], c.bank[n % 4], ACT.Identity,
                                         bias=bq[:, m:m + 1]).then_inc(q_rounded, 1)

                for event in plan:
                    kind, i = event[0], event[1]
                    qt = order[i]
                    if kind == "score":
                        n = event[2]
                        act.wait_ge(score_ready, n + 1)
                        if n >= 4:
                            act.wait_ge(value_done, n - 3)
                        nc.scalar.activation(prob[:, n % 4, :], score_bank[n % 2], ACT.Exp, scale=SCALE)\
                            .then_inc(exp_ready, 1)
                    elif kind == "value" and event[4]:
                        _, _, n, u, _, _ = event
                        unit = 8 * i + u
                        act.wait_ge(value_done, n + 1)
                        if unit >= 4:
                            act.wait_ge(heads_turned, (unit - 4) // 2 + 1)
                        nc.scalar.copy(o_sb[:, unit % 4, :], value_bank[unit % 2][:, 0:P]).then_inc(o_copied, 1)
                    elif kind == "shift_rows":
                        act.wait_ge(shift_turned, i + 1)
                        if i >= 2:
                            act.wait_ge(rows_sent[i % 2], 16 * (i // 2))
                        nc.scalar.copy(rows[:, i % 2, :], turn_bank[0:4 * PAIRS, 0:P]).then_inc(turn_taken, 1)
                    elif kind == "turn":
                        act.wait_ge(turned, i + 1)
                        if i >= 2:
                            act.wait_ge(out_ready, i - 1)
                        nc.scalar.copy(a_feat[:, i % 2, :, :].rearrange("p k n -> p (k n)"), turn_bank)\
                            .then_inc(turn_taken, 1)
                    elif kind == "std":
                        act.wait_ge(var_ready, i + 1)
                        nc.scalar.activation(c.std[:, qt:qt + 1], c.mean_var[:, qt, 1:2], ACT.Sqrt,
                                             bias=c.eps[:, 0:1]).then_inc(std_ready, 1)
                    elif kind == "feat":
                        act.wait_ge(feat_turned, i + 1)
                        nc.scalar.copy(c.x_feat[:, :, cols(qt)], turn_bank.rearrange("p (k n) -> p k n", k=KC))\
                            .then_inc(turn_taken, 1)

            @block.vector
            def _(dve):
                count = 0

                def then(ins):
                    nonlocal count
                    count += 1
                    ins.then_inc(step, 1)
                    dve.wait_ge(step, count)

                tt, ts, stt = nc.vector.tensor_tensor, nc.vector.tensor_scalar, nc.vector.scalar_tensor_tensor
                last = slice(SPLIT, SHIFTED)
                for head, (both_rows, first_rows) in enumerate(((0.0, 1.0), (1.0, 0.0))):
                    then(nc.vector.memset(keys[last, head, :].bitcast(F32), both_rows))
                    then(nc.vector.memset(keys[SPLIT:SPLIT + 2, head, :].bitcast(F32), first_rows))
                dve.wait_ge(w_loaded, 64)
                mid = slice(32, 64)
                for head in range(2):
                    for half in range(2):
                        part, bank = slice(half * HALF, (half + 1) * HALF), c.bank[4 + 2 * head + half]
                        dve.wait_ge(k_rounded, 2 * head + half + 1)
                        stt(keys[mid, head, part], bank[mid, :], bk[mid, head:head + 1],
                            keys[mid, head, part].bitcast(F32), ALU.add, ALU.subtract).then_inc(k_split, 1)
                for n in range(2 * KC):
                    m, half = divmod(n, 2)
                    part = slice(half * HALF, (half + 1) * HALF)
                    dve.wait_ge(q_rounded, n + 1)
                    stt(q_lo[:, m % 2, part], c.bank[n % 4], bq[:, m:m + 1],
                        q_hi[:, m % 2, part].bitcast(F32), ALU.add, ALU.subtract).then_inc(q_split, 1)
                dve.wait_ge(v_turned, 1)
                nc.vector.tensor_copy(v[:, :, :], c.bank[4][:, 0:NT * 2 * HD].rearrange("p (t d) -> p t d", t=NT))\
                    .then_inc(v_ready, 1)
                dve.wait_ge(v_ready, 1)
                nc.vector.memset(v[:, :, HD:HD + 1], 1.0).then_inc(v_ready, 1)

                for event in plan:
                    kind, i = event[0], event[1]
                    qt = order[i]
                    row = c.x_tok[:, qt, :]
                    segments = -(-(qt + 1) * P // HALF)
                    if kind == "max":
                        _, _, n, heads, lo, width = event
                        dve.wait_ge(max_ready, n + 1)
                        nc.vector.tensor_reduce(top[:, i % 2, lo // HALF, heads[0]:heads[-1] + 1],
                                                max_bank[n % 2][:, 0:len(heads) * width]
                                                .rearrange("p (h k) -> p h k", h=len(heads)), AX.X, ALU.max)\
                            .then_inc(max_taken, 1)
                    elif kind == "shift":
                        last_max = max(e[2] for e in plan if e[0] == "max" and e[1] == i)
                        dve.wait_ge(max_taken, last_max + 1)
                        if i >= 2:
                            dve.wait_ge(shift_turned, i - 1)
                        if segments == 2:
                            then(tt(both[:, :], top[:, i % 2, 0, :], top[:, i % 2, 1, :], ALU.max))
                            found = both[:, :]
                        else:
                            found = top[:, i % 2, 0, :]
                        found = found.rearrange("p (j h) -> p h j", h=2)
                        high, low = shift[:, i % 2, :, 0, :], shift[:, i % 2, :, 1, :]
                        then(ts(high, found, -1.0, None, ALU.mult))
                        stt(low, found, -1.0, high.bitcast(F32), ALU.mult, ALU.subtract).then_inc(shift_ready, 1)
                    elif kind == "heads":
                        g = event[2]
                        dve.wait_ge(heads_turned, 4 * i + g + 1)
                        if i >= 2 and g == 0:
                            dve.wait_ge(turned, i - 1)
                        parts = turn_bank[:, 0:2 * P].rearrange("p (h j d) -> p h j d", h=2, j=4)
                        then(nc.vector.reciprocal(inv[:, :, :], parts[:, :, :, HD]))
                        dst = attn[:, i % 2, g * P:(g + 1) * P].rearrange("p (j h d) -> p h j d", j=4, h=2)
                        tt(dst, parts[:, :, :, 0:HD], inv[:, :, :].unsqueeze(3).to_broadcast([P, 2, 4, HD]),
                           ALU.mult).then_inc(turn_taken, 1)
                    elif kind == "project":
                        dve.wait_ge(out_ready, i + 1)
                        if i == 0:
                            dve.wait_ge(wo_loaded, 32)
                        tt(row, row, out_bank, ALU.add).then_inc(added, 1)
                        dve.wait_ge(added, i + 1)
                        then(tt(row, row, bo[:, :], ALU.add))
                        then(nc.vector.bn_stats(c.stats[:, qt, :], row))
                        nc.vector.bn_aggr(c.mean_var[:, qt, :], c.stats[:, qt, :]).then_inc(var_ready, 1)
                    elif kind == "norm":
                        dve.wait_ge(std_ready, i + 1)
                        then(nc.vector.reciprocal(c.rstd[:, qt:qt + 1], c.std[:, qt:qt + 1]))
                        ts(row, row, c.mean_var[:, qt, 0:1], c.rstd[:, qt:qt + 1], ALU.subtract, ALU.mult)\
                            .then_inc(normed, 1)


def only_rotation(c, a):
    with c.nc.Block() as block:
        @block.sync
        def _(sp):
            c.rot.load(sp, a)

        @block.vector
        def _(dve):
            c.rot.dve(dve)

        @block.scalar
        def _(act):
            c.rot.act(act)

        @block.gpsimd
        def _(pool):
            c.rot.pool(pool)


LAYERS = ["L0_attn", "L0_ffn", "L1_attn", "L1_ffn", "L2_attn", "L2_ffn", "L3_attn", "L3_ffn"]


def build(nc, a, out):
    with ExitStack() as ctx:
        c = Chip(nc, ctx)
        setup(c, a["x_tok"], a["x_feat"])
        c.rot_scope = ExitStack()
        c.rot = Rotation(c, c.rot_scope)
        with c.rot_scope:
            if "L0_attn" in LAYERS:
                gradient_ffn(c, a)
            else:
                only_rotation(c, a)
        out_rows = out.rearrange("(t p) n -> t p n", p=P)
        if "L0_ffn" in LAYERS:
            merged_lora(c, a)
        if "L1_attn" in LAYERS:
            single_key_attention(c, a)
        if "L1_ffn" in LAYERS:
            swiglu(c, "L1_ffn", a["L1_w"].shape[0], a["L1_w"], zeros=a["L1_z"], scales=a["L1_s"])
        if "L2_attn" in LAYERS:
            conv_stack(c, a)
        if "L2_ffn" in LAYERS:
            two_loras(c, a)
        if "L3_attn" in LAYERS:
            causal_attention(c, a)
        swiglu(c, "L3_ffn", a["L3_w"].shape[0], a["L3_w"],
               scale=[a["L3_scale_gate"], a["L3_scale_up"], a["L3_scale_down"]], last=out_rows)


def up_tiles(w, tiles):
    w = np.asarray(w)
    w = np.pad(w, ((0, 0), (0, tiles * P - w.shape[1])))
    return w.reshape(KC, P, tiles, P).transpose(2, 1, 0, 3).reshape(tiles, P, KC * P)


def down_tiles(w, tiles):
    w = np.asarray(w)
    return np.pad(w, ((0, tiles * P - w.shape[0]), (0, 0))).reshape(tiles, P, w.shape[1])


def chunks(w):
    return w.reshape(-1, P, w.shape[1]).transpose(1, 0, 2)


def layout(v):
    v = {k: np.asarray(x) for k, x in v.items()}
    x = np.asarray(v["L0_attn_hidden_states"])[0]
    a = {"x_tok": x, "x_feat": x.T}
    a["L1_w"] = np.concatenate([up_tiles(v["L1_ffn_gate_w"], 14), up_tiles(v["L1_ffn_up_w"], 14),
                                down_tiles(v["L1_ffn_down_w"], 14)], 2)
    for n, k in (("z", "z"), ("s", "s")):
        g, u, d = (np.asarray(v[f"L1_ffn_{w}_{k}"]) for w in ("gate", "up", "down"))
        cols = lambda m: m.reshape(KC, 14, P).transpose(1, 0, 2).reshape(14, KC * P)
        a["L1_" + n] = np.concatenate([cols(g), cols(u), d], 1)
    a["L3_w"] = np.concatenate([up_tiles(v["L3_ffn_w_gate"].T, 11), up_tiles(v["L3_ffn_w_up"].T, 11),
                                down_tiles(v["L3_ffn_w_down"].T, 11)], 2)
    for n in ("scale_gate", "scale_up", "scale_down"):
        a["L3_" + n] = v["L3_ffn_" + n].reshape(1)
    a["L0_w"] = np.concatenate([up_tiles(v["L0_attn_ffn_gate_w"].T, 10), up_tiles(v["L0_attn_ffn_up_w"].T, 10)], 2)
    a["L0_down"] = down_tiles(v["L0_attn_ffn_down_w"].T, 10).transpose(1, 0, 2)
    a["L0_proj"] = np.stack([chunks(v["L0_attn_up_w"].T), chunks(v["L0_attn_gate_w"].T)], 1)
    a["L0_fuse"] = np.concatenate([v["L0_attn_local_approx_output"].T[:, None],
                                   v["L0_attn_fuse_weight"].transpose(1, 2, 0)], 1)
    a["L0_point"] = v["L0_attn_local_point"].reshape(P, 1)
    a["L0_disc"] = v["L0_attn_discount_factor"]
    a["L0_org"] = chunks(v["L0_ffn_W_org"].T)
    a["L0_lora_down"] = chunks(v["L0_ffn_lora_down"].transpose(0, 2, 1).reshape(DIM, DIM))
    a["L0_up"] = chunks(v["L0_ffn_lora_up"].reshape(DIM, DIM))
    a["L0_wq"] = chunks(v["L0_ffn_Wq"].T)
    a["L0_keys"] = v["L0_ffn_lora_keys"].T
    qkv = v["L1_attn_weight_qkv"].reshape(8, 6, P, DIM)
    a["L1_wv"] = qkv[:, 5].transpose(1, 0, 2)
    a["L1_wo"] = v["L1_attn_weight_proj"].reshape(DIM, 8, 4, P).transpose(1, 3, 2, 0)
    k_w, k_b = v["L3_attn_wk_w"].T, v["L3_attn_wk_b"]
    wk, bk = np.zeros((DIM, 2, P), k_w.dtype), np.zeros((P, 2), k_b.dtype)
    for head in range(2):
        for slot in range(3):
            at = 32 * slot + HD * head
            wk[:, head, at:at + HD], bk[at:at + HD, head] = k_w, k_b
    wk[:, 0, SPLIT:SPLIT + HD], bk[SPLIT:SPLIT + HD, 0] = v["L3_attn_wv_w"].T, v["L3_attn_wv_b"]
    a["A_wk"] = wk.reshape(KC, P, 2, P).transpose(1, 0, 2, 3)
    a["A_bk"] = bk
    a["A_wq"], a["A_wo"] = chunks(v["L3_attn_wq_w"].T), chunks(v["L3_attn_wo_w"].T)
    a["A_bq"], a["A_bo"] = v["L3_attn_wq_b"].reshape(KC, P).T, v["L3_attn_wo_b"]
    twice = lambda m: np.concatenate([m.T, m.T], 0)
    g = lambda n: v["L2_attn_" + n]
    a["L2_par"] = np.stack([twice(g(n)) for n in ("phz_re", "phz_im", "lc_re", "lc_im")], 1)
    a["C_in"], a["C_out"] = chunks(g("Win").T), g("Wout").T
    a["C_w1"] = g("W1").transpose(2, 0, 1)
    a["C_w2"] = g("W2").reshape(4, 64, 2, P).transpose(3, 0, 2, 1)
    a["C_cols"] = np.concatenate([np.stack([twice(g(n)) for n in ("ln1_w", "ln1_b", "ln2_w", "ln2_b")], 2),
                                  g("b1").reshape(4, 2, P).transpose(2, 0, 1)], 2)
    a["C_last"] = np.stack([g("lnl_w"), g("lnl_b")], 1)
    a["C_b2"], a["C_sc"], a["C_bin"], a["C_bout"] = g("b2"), g("sc_lin"), g("bin"), g("bout")
    a["L2_low"] = np.stack([v["L2_ffn_A"], v["L2_ffn_WL"]], 1)
    a["L2_high"] = np.stack([v["L2_ffn_B"].T, v["L2_ffn_WR"].T], 1)
    a["L2_base"], a["L2_bias"] = chunks(v["L2_ffn_W_base"].T), v["L2_ffn_b_base"]
    return a


def kernel(**inputs):
    import concourse.bacc as bacc
    from concourse.bass_utils import run_bass_kernel_spmd

    nc = bacc.Bacc("TRN2", target_bir_lowering=False, num_devices=1)
    arrays = {f"in_{k}": np.ascontiguousarray(v) for k, v in layout(inputs).items()}
    args = {k[3:]: nc.dram_tensor(k, v.shape, mybir.dt.from_np(v.dtype), kind="ExternalInput").ap()
            for k, v in arrays.items()}
    out = nc.dram_tensor("out_0_dram", (TOK, DIM), F32, kind="ExternalOutput").ap()
    build(nc, args, out)
    r = run_bass_kernel_spmd(nc, [arrays], core_ids=[0])
    return r.results[0]["out_0_dram"].reshape(1, TOK, DIM)
```

```python
from contextlib import ExitStack

import numpy as np

import concourse.bass as bass
from concourse import mybir

F32 = mybir.dt.float32
F32R = mybir.dt.float32r
BF16 = mybir.dt.bfloat16
I32 = mybir.dt.int32
ALU = mybir.AluOpType
ACT = mybir.ActivationFunctionType
AX = mybir.AxisListType

P = 128
TOK = 1024
DIM = 512
NT = TOK // P
KC = DIM // P
HALF = 512
EPS = 1e-5
FFN_COUNTERS = ("x_hi", "x_lo", "w_hi", "w_lo", "gate_done", "up_done", "gated", "product", "wd_hi", "wd_lo",
                "h_hi", "h_lo", "h_used", "dequantised")


class Chip:

    def __init__(self, nc, ctx):
        self.nc, self.ctx = nc, ctx
        self.x_tok = self.sb("x_tok", [P, NT, DIM], F32)
        self.x_feat = self.sb("x_feat", [P, KC, TOK], F32)
        self.ident = self.sb("ident", [P, P], F32)
        self.stats = self.sb("ln_stats", [P, NT, 6], F32)
        self.mean_var = self.sb("ln_mean_var", [P, NT, 2], F32)
        self.std = self.sb("ln_std", [P, NT], F32)
        self.rstd = self.sb("ln_rstd", [P, NT], F32)
        self.tail_sems = [self.sem(n) for n in Tail.NAMES]
        self.ffn_sems = [self.sem("ffn_" + n) for n in FFN_COUNTERS]
        self.ffn_loaded = [self.sem(f"ffn_loaded{i}") for i in range(2)]
        self.ffn_base = {n: 0 for n in FFN_COUNTERS}
        self.ffn_base["loaded"] = [0, 0]
        self.tails = self.ln_count = 0
        psum = ctx.enter_context(nc.psum_tensor("psum", [P, 8, 512], F32))
        self.bank = [psum[:, i, :] for i in range(8)]

    def sb(self, name, shape, dt, ctx=None):
        return (ctx or self.ctx).enter_context(self.nc.sbuf_tensor(name, shape, dt))

    def sem(self, name):
        return self.ctx.enter_context(self.nc.semaphore(name))


class Tail:

    NAMES = ("out_ready", "out_taken", "ln_step", "var_ready", "std_ready", "normed", "transposed", "feat_ready")

    def __init__(self, chip, out_bank, tr_bank, last=False):
        self.c, self.out_bank, self.tr_bank, self.last = chip, out_bank, tr_bank, last
        (self.out_ready, self.out_taken, self.ln_step, self.var_ready, self.std_ready, self.normed,
         self.transposed, self.feat_ready) = chip.tail_sems
        self.base = NT * chip.tails
        chip.tails += 1

    def dve(self, dve, t, bias=None):
        c, nc = self.c, self.c.nc
        row = c.x_tok[:, t, :]

        def step(ins):
            c.ln_count += 1
            ins.then_inc(self.ln_step, 1)
            dve.wait_ge(self.ln_step, c.ln_count)

        dve.wait_ge(self.out_ready, self.base + t + 1)
        if bias is None:
            nc.vector.tensor_tensor(row, row, self.out_bank[t % 2][:, :], ALU.add).then_inc(self.out_taken, 1)
            dve.wait_ge(self.out_taken, self.base + t + 1)
        else:
            nc.vector.tensor_tensor(row, row, self.out_bank[t % 2][:, :], ALU.add).then_inc(self.out_taken, 1)
            dve.wait_ge(self.out_taken, self.base + t + 1)
            step(nc.vector.tensor_tensor(row, row, bias[:, :], ALU.add))
        step(nc.vector.bn_stats(c.stats[:, t, :], row))
        nc.vector.bn_aggr(c.mean_var[:, t, :], c.stats[:, t, :]).then_inc(self.var_ready, 1)
        dve.wait_ge(self.std_ready, self.base + t + 1)
        step(nc.vector.reciprocal(c.rstd[:, t:t + 1], c.std[:, t:t + 1]))
        nc.vector.tensor_scalar(row, row, c.mean_var[:, t, 0:1], c.rstd[:, t:t + 1],
                                ALU.subtract, ALU.mult).then_inc(self.normed, 1)

    def act_std(self, act, t):
        c, nc = self.c, self.c.nc
        act.wait_ge(self.var_ready, self.base + t + 1)
        nc.scalar.activation(c.std[:, t:t + 1], c.mean_var[:, t, 1:2], ACT.Sqrt,
                             bias=c.eps[:, 0:1]).then_inc(self.std_ready, 1)

    def act_copy(self, act, t):
        c, nc = self.c, self.c.nc
        act.wait_ge(self.transposed, self.base + t + 1)
        src = self.tr_bank[t % 2][:, :].rearrange("p (k n) -> p k n", k=KC)
        nc.scalar.copy(c.x_feat[:, :, t * P:(t + 1) * P], src).then_inc(self.feat_ready, 1)

    def act(self, act):
        for t in range(NT):
            self.act_std(act, t)
            if t and not self.last:
                self.act_copy(act, t - 1)
        if not self.last:
            self.act_copy(act, NT - 1)
            act.wait_ge(self.feat_ready, self.base + NT)

    def pe(self, pe, t):
        c, nc = self.c, self.c.nc
        if self.last:
            return
        pe.wait_ge(self.normed, self.base + t + 1)
        if t >= 2:
            pe.wait_ge(self.feat_ready, self.base + t - 1)
        for k in range(KC):
            ins = nc.tensor.transpose(self.tr_bank[t % 2][:, k * P:(k + 1) * P],
                                      c.x_tok[:, t, k * P:(k + 1) * P], c.ident[:, :])
        ins.then_inc(self.transposed, 1)


def each_tile(eng, tiles, body):
    body(0, 0, True)
    body(1, 1, True)
    if tiles >= 4:
        with eng.Fori(1, tiles // 2) as i:
            body(2 * i, 0, False)
            body(2 * i + 1, 1, False)
    if tiles % 2:
        body(tiles - 1, 0, False)


def setup(c, x_tok_dram, x_feat_dram):
    nc = c.nc
    c.eps = c.sb("eps", [P, 1], F32)
    loaded, ready, zeroed = c.sem("x_loaded"), c.sem("const_ready"), c.sem("ident_zeroed")
    with nc.Block() as block:

        @block.sync
        def _(sp):
            sp.dma_start(c.x_feat[:, :, :], x_feat_dram.rearrange("(k p) n -> p k n", p=P)).then_inc(loaded, 16)
            sp.dma_start(c.x_tok[:, :, :], x_tok_dram.rearrange("(t p) n -> p t n", p=P)).then_inc(loaded, 16)
            sp.wait_ge(loaded, 32)

        @block.gpsimd
        def _(pool):
            nc.gpsimd.memset(c.eps[:, :], EPS)
            nc.gpsimd.memset(c.ident[:, :], 0.0).then_inc(zeroed, 1)
            pool.wait_ge(zeroed, 1)
            nc.gpsimd.affine_select(out=c.ident[:, :], in_=c.ident[:, :], compare_op=ALU.not_equal, fill=1.0,
                                    base=0, pattern=[[-1, P]], channel_multiplier=1).then_inc(ready, 1)
            pool.wait_ge(ready, 1)


PASSES = ((0, 0), (0, 1), (1, 0))


def swiglu(c, name, tiles, weights, zeros=None, scales=None, scale=None, down=None, last=None,
           extra_loads=None, extra_dve=None, extra_pe=None, extra_act=None):
    nc = c.nc
    quantised = down is None
    up_width = 2 * KC * P
    width = up_width + (DIM if quantised else 0)
    per = -(-tiles // 2)
    groups = (range(0, per), range(per, tiles))
    with ExitStack() as own:
        def sb(n, shape, dt, scope=own):
            return c.sb(f"{name}_{n}", shape, dt, scope)

        def sem(n):
            return c.sem(f"{name}_{n}")

        w_down = sb("w_down", [P, tiles, DIM], F32)
        hidden = sb("hidden", [P, tiles, TOK], F32)
        with ExitStack() as up_stage:
            x = sb("x", [P, 2, KC, TOK], F32R, up_stage)
            w_up = sb("w_up", [P, 2, 2, up_width], F32R, up_stage)
            stage = sb("stage", [P, 2, width], F32, up_stage)
            w_int = stage.bitcast(I32) if quantised else stage
            if zeros is not None:
                z_int = sb("z_int", [P, width], I32, up_stage)
                s_all = sb("s_all", [P, width], F32, up_stage)
            if scale is not None:
                sc = sb("sc", [P, 3], F32, up_stage)
            gate = sb("gate", [P, HALF], F32, up_stage)
        wd = sb("wd", [P, 2, tiles, DIM], F32R)
        part_h = sb("part_h", [P, 2, 2, per, P], F32R)
        g_bank, u_bank = c.bank[0:2], c.bank[2:4]
        tail = Tail(c, c.bank[4:6], c.bank[6:8], last is not None)
        base = c.ffn_base
        (x_hi, x_lo, w_hi, w_lo, gate_done, up_done, gated, product, wd_hi, wd_lo, h_hi, h_lo, h_used,
         dequantised) = c.ffn_sems
        loaded = c.ffn_loaded
        if not quantised:
            down_loaded = sem("down_loaded")
        if zeros is not None:
            zs_loaded, centred = sem("zs_loaded"), sem("centred")
        if scale is not None:
            scale_loaded = sem("scale_loaded")
        if last is not None:
            stored = sem("stored")

        def split_h(engine, t, g, part):
            src = hidden[:, groups[g].start:groups[g].stop, t * P:(t + 1) * P]
            n, u = len(groups[g]), 2 * t + g
            if part == 0:
                if t and g == 0:
                    engine.wait_ge(h_used, base["h_used"] + t)
                elif t:
                    engine.wait_ge(tail.out_ready, tail.base + t)
                nc.scalar.copy(part_h[:, g, 0, 0:n, :], src).then_inc(h_hi, 1)
            else:
                engine.wait_ge(h_hi, base["h_hi"] + u + 1)
                nc.vector.tensor_tensor(part_h[:, g, 1, 0:n, :], src, part_h[:, g, 0, 0:n, :].bitcast(F32),
                                        ALU.subtract).then_inc(h_lo, 1)

        def split_w_down(engine, g, part):
            for f in groups[g]:
                if part == 0:
                    nc.scalar.copy(wd[:, 0, f, :], w_down[:, f, :]).then_inc(wd_hi, 1)
                else:
                    engine.wait_ge(wd_hi, base["wd_hi"] + f + 1)
                    nc.vector.tensor_tensor(wd[:, 1, f, :], w_down[:, f, :], wd[:, 0, f, :].bitcast(F32),
                                            ALU.subtract).then_inc(wd_lo, 1)

        with nc.Block() as block:

            @block.sync
            def _(sp):
                if scale is not None:
                    for i, s in enumerate(scale):
                        sp.dma_start(sc[:, i:i + 1], s.partition_broadcast(P)).then_inc(scale_loaded, 16)

                def load(f, slot, first):
                    if not first:
                        sp.wait_ge(w_lo, base["w_lo"] + f - 1)
                    sp.dma_start(w_int[:, slot, :], weights[f]).then_inc(loaded[slot], 16)
                    if zeros is not None:
                        if not (first and slot == 0):
                            sp.wait_ge(dequantised, base["dequantised"] + f)
                        sp.dma_start(z_int[:, :], zeros[f].partition_broadcast(P)).then_inc(zs_loaded, 16)
                        sp.dma_start(s_all[:, :], scales[f].partition_broadcast(P)).then_inc(zs_loaded, 16)
                    if first and slot == 1 and extra_loads is not None:
                        extra_loads(sp)
                    if first and slot == 1 and not quantised:
                        sp.dma_start(w_down[:, :, :], down).then_inc(down_loaded, 16)

                each_tile(sp, tiles, load)
                if last is not None:
                    for t in range(NT):
                        sp.wait_ge(tail.normed, tail.base + t + 1)
                        sp.dma_start(last[t], c.x_tok[:, t, :]).then_inc(stored, 16)
                    sp.wait_ge(stored, 16 * NT)

            @block.tensor
            def _(pe):
                if extra_pe is not None:
                    extra_pe[0](pe)

                def gate_and_up(f, slot, first):
                    pe.wait_ge(w_lo, base["w_lo"] + f + 1)
                    for half in range(2):
                        if first and slot == 0:
                            pe.wait_ge(x_lo, base["x_lo"] + half + 1)
                        else:
                            pe.wait_ge(product, base["product"] + 2 * f + half - 1)
                        for which, bank, done in ((0, g_bank, gate_done), (1, u_bank, up_done)):
                            for k in range(KC):
                                at = (which * KC + k) * P
                                for n, (w_part, x_part) in enumerate(PASSES):
                                    ins = nc.tensor.matmul(bank[half][:, :], w_up[:, slot, w_part, at:at + P],
                                                           x[:, x_part, k, half * HALF:(half + 1) * HALF],
                                                           start=k == 0 and n == 0, stop=k == KC - 1 and n == 2)
                            ins.then_inc(done, 1)

                each_tile(pe, tiles, gate_and_up)
                for t in range(NT):
                    if t >= 2:
                        pe.wait_ge(tail.out_taken, tail.base + t - 1)
                    if extra_pe is not None:
                        extra_pe[1](pe, t, tail.out_bank[t % 2])
                    for g in range(2):
                        pe.wait_ge(h_lo, base["h_lo"] + 2 * t + g + 1)
                        for f in groups[g]:
                            if t == 0:
                                pe.wait_ge(wd_lo, base["wd_lo"] + f + 1)
                            for n, (h_part, w_part) in enumerate(PASSES):
                                ins = nc.tensor.matmul(tail.out_bank[t % 2][:, :],
                                                       part_h[:, g, h_part, f - groups[g].start, :],
                                                       wd[:, w_part, f, :],
                                                       start=f == 0 and n == 0 and extra_pe is None,
                                                       stop=f == tiles - 1 and n == 2)
                        ins.then_inc(h_used if g == 0 else tail.out_ready, 1)
                        if g == 0 and t:
                            tail.pe(pe, t - 1)
                tail.pe(pe, NT - 1)

            @block.scalar
            def _(act):
                for half in range(2):
                    cols = slice(half * HALF, (half + 1) * HALF)
                    nc.scalar.copy(x[:, 0, :, cols], c.x_feat[:, :, cols]).then_inc(x_hi, 1)

                def split_w_up(f, slot, first):
                    if quantised:
                        act.wait_ge(dequantised, base["dequantised"] + f + 1)
                    else:
                        act.wait_ge(loaded[slot], base["loaded"][slot] + 8 * (f - slot) + 16)
                    if not first:
                        act.wait_ge(up_done, base["up_done"] + 2 * f - 2)
                    nc.scalar.copy(w_up[:, slot, 0, :], stage[:, slot, 0:up_width]).then_inc(w_hi, 1)

                def silu(f, fresh=False):
                    for half in range(2):
                        act.wait_ge(gate_done, base["gate_done"] + 2 * f + half + 1)
                        if not (fresh and half == 0):
                            act.wait_ge(product, base["product"] + 2 * f + half)
                        nc.scalar.activation(gate[:, :], g_bank[half][:, :], ACT.Silu).then_inc(gated, 1)

                def tile(f, slot, first):
                    silu(f, first and slot == 0)
                    split_w_up(f + 2, slot, False)

                split_w_up(0, 0, True)
                split_w_up(1, 1, True)
                if extra_act is not None:
                    extra_act(act)
                each_tile(act, tiles - 2, tile)
                silu(tiles - 2)
                silu(tiles - 1)
                act.wait_ge(product, base["product"] + 2 * tiles)
                if not quantised:
                    act.wait_ge(down_loaded, 16)
                for g in range(2):
                    split_h(act, 0, g, 0)
                    split_w_down(act, g, 0)
                split_h(act, 1, 0, 0)
                for t in range(NT):
                    if t + 1 < NT:
                        split_h(act, t + 1, 1, 0)
                    tail.act_std(act, t)
                    if t + 2 < NT:
                        split_h(act, t + 2, 0, 0)
                    if t and not tail.last:
                        tail.act_copy(act, t - 1)
                if not tail.last:
                    tail.act_copy(act, NT - 1)
                    act.wait_ge(tail.feat_ready, tail.base + NT)

            @block.vector
            def _(dve):
                if scale is not None:
                    dve.wait_ge(scale_loaded, 16 * len(scale))

                def split_w_up(f, slot, first):
                    if zeros is not None:
                        dve.wait_ge(loaded[slot], base["loaded"][slot] + 8 * (f - slot) + 16)
                        dve.wait_ge(zs_loaded, 32 * f + 32)
                        nc.vector.tensor_tensor(stage[:, slot, :], w_int[:, slot, :], z_int[:, :],
                                                ALU.subtract).then_inc(centred, 1)
                        dve.wait_ge(centred, f + 1)
                        nc.vector.tensor_tensor(w_down[:, f, :], stage[:, slot, up_width:width],
                                                s_all[:, up_width:width], ALU.mult)
                        nc.vector.tensor_tensor(stage[:, slot, 0:up_width], stage[:, slot, 0:up_width],
                                                s_all[:, 0:up_width], ALU.mult).then_inc(dequantised, 1)
                    elif quantised:
                        dve.wait_ge(loaded[slot], base["loaded"][slot] + 8 * (f - slot) + 16)
                        for i in range(2):
                            at = slice(i * KC * P, (i + 1) * KC * P)
                            nc.vector.tensor_scalar(stage[:, slot, at], w_int[:, slot, at], sc[:, i:i + 1], None,
                                                    ALU.mult)
                        nc.vector.tensor_scalar(w_down[:, f, :], w_int[:, slot, up_width:width], sc[:, 2:3], None,
                                                ALU.mult).then_inc(dequantised, 1)
                    dve.wait_ge(w_hi, base["w_hi"] + f + 1)
                    nc.vector.tensor_tensor(w_up[:, slot, 1, :], stage[:, slot, 0:up_width],
                                            w_up[:, slot, 0, :].bitcast(F32), ALU.subtract).then_inc(w_lo, 1)

                def multiply(f):
                    for half in range(2):
                        dve.wait_ge(gated, base["gated"] + 2 * f + half + 1)
                        dve.wait_ge(up_done, base["up_done"] + 2 * f + half + 1)
                        nc.vector.tensor_tensor(hidden[:, f, half * HALF:(half + 1) * HALF], gate[:, :],
                                                u_bank[half][:, :], ALU.mult).then_inc(product, 1)

                def tile(f, slot, first):
                    multiply(f)
                    split_w_up(f + 2, slot, False)

                split_w_up(0, 0, True)
                for half in range(2):
                    dve.wait_ge(x_hi, base["x_hi"] + half + 1)
                    cols = slice(half * HALF, (half + 1) * HALF)
                    nc.vector.tensor_tensor(x[:, 1, :, cols], c.x_feat[:, :, cols], x[:, 0, :, cols].bitcast(F32),
                                            ALU.subtract).then_inc(x_lo, 1)
                split_w_up(1, 1, True)
                if extra_dve is not None:
                    extra_dve(dve)
                each_tile(dve, tiles - 2, tile)
                multiply(tiles - 2)
                multiply(tiles - 1)
                for g in range(2):
                    split_h(dve, 0, g, 1)
                    split_w_down(dve, g, 1)
                split_h(dve, 1, 0, 1)
                for t in range(NT):
                    if t + 1 < NT:
                        split_h(dve, t + 1, 1, 1)
                    tail.dve(dve, t)
                    if t + 2 < NT:
                        split_h(dve, t + 2, 0, 1)

    for counter, times in (("x_hi", 2), ("x_lo", 2), ("w_hi", tiles), ("w_lo", tiles), ("gate_done", 2 * tiles),
                           ("up_done", 2 * tiles), ("gated", 2 * tiles), ("product", 2 * tiles),
                           ("wd_hi", tiles), ("wd_lo", tiles), ("h_hi", 2 * NT), ("h_lo", 2 * NT),
                           ("h_used", NT), ("dequantised", tiles if quantised else 0)):
        base[counter] += times
    for slot in range(2):
        base["loaded"][slot] += 16 * len(range(slot, tiles, 2))


def gradient_ffn(c, a):
    nc = c.nc
    G, GRAD_ORDER_MIN, THD = 6, 4, 2.5
    tiles = a["L0_w"].shape[0]
    with ExitStack() as own:
        def sb(n, shape):
            return c.sb(f"series_{n}", shape, F32, own)

        with ExitStack() as before_terms:
            w_proj = c.sb("series_w_proj", [P, 2, KC, P], F32, before_terms)
        terms = sb("terms", [P, G + 1, TOK])
        w_fuse = sb("w_fuse", [P, G + 1, DIM])
        delta, keep = sb("delta", [P, TOK]), sb("keep", [P, TOK])
        point, disc = sb("point", [P, 1]), sb("disc", [P, G])
        diff, ratio = sb("diff", [P, G]), sb("ratio", [P, G])
        proj_loaded, small_loaded = c.sem("series_proj_loaded"), c.sem("series_small_loaded")
        fuse_loaded, projected = c.sem("series_fuse_loaded"), c.sem("series_projected")
        diff_ready, ratio_ready = c.sem("series_diff_ready"), c.sem("series_ratio_ready")
        step = c.sem("series_step")

        def loads(sp):
            sp.dma_start(w_proj[:, :, :, :], a["L0_proj"]).then_inc(proj_loaded, 16)
            sp.dma_start(point[:, :], a["L0_point"]).then_inc(small_loaded, 16)
            sp.dma_start(disc[:, :], a["L0_disc"].partition_broadcast(P)).then_inc(small_loaded, 16)
            sp.dma_start(w_fuse[:, :, :], a["L0_fuse"]).then_inc(fuse_loaded, 16)

        def project(pe):
            pe.wait_ge(proj_loaded, 16)
            for which in range(2):
                for half in range(2):
                    for k in range(KC):
                        ins = nc.tensor.matmul(c.bank[4 + 2 * which + half][:, :], w_proj[:, which, k, :],
                                               c.x_feat[:, k, half * HALF:(half + 1) * HALF],
                                               start=k == 0, stop=k == KC - 1)
            ins.then_inc(projected, 1)

        def series(pe, t, bank):
            if t == 0:
                pe.wait_ge(fuse_loaded, 16)
                pe.wait_ge(step, G + 5)
            for m in range(G + 1):
                nc.tensor.matmul(bank[:, :], terms[:, m, t * P:(t + 1) * P], w_fuse[:, m, :],
                                 start=m == 0, stop=False)

        def ratios(act):
            act.wait_ge(diff_ready, 2)
            nc.scalar.activation(ratio[:, :], diff[:, :], ACT.Exp).then_inc(ratio_ready, 1)

        def make_terms(dve):
            count = 0

            def then(ins):
                nonlocal count
                count += 1
                ins.then_inc(step, 1)
                dve.wait_ge(step, count)

            dve.wait_ge(small_loaded, 32)
            nc.vector.tensor_scalar(diff[:, 0:1], disc[:, 0:1], -1.0, None, ALU.mult).then_inc(diff_ready, 1)
            nc.vector.tensor_tensor(diff[:, 1:G], disc[:, 0:G - 1], disc[:, 1:G], ALU.subtract).then_inc(diff_ready, 1)
            dve.wait_ge(projected, 1)
            for half in range(2):
                cols = slice(half * HALF, (half + 1) * HALF)
                nc.vector.tensor_copy(terms[:, 0, cols], c.bank[4 + half][:, :])
                then(nc.vector.tensor_scalar(delta[:, cols], c.bank[6 + half][:, :], point[:, 0:1], None,
                                             ALU.subtract))
            then(nc.vector.tensor_scalar(keep[:, :], delta[:, :], THD, None, ALU.is_le))
            then(nc.vector.scalar_tensor_tensor(keep[:, :], delta[:, :], -THD, keep[:, :], ALU.is_ge, ALU.mult))
            dve.wait_ge(ratio_ready, 1)
            for m in range(1, G + 1):
                then(nc.vector.scalar_tensor_tensor(terms[:, m, :], terms[:, m - 1, :], ratio[:, m - 1:m],
                                                    delta[:, :], ALU.mult, ALU.mult))
                if m == GRAD_ORDER_MIN + 1:
                    then(nc.vector.tensor_tensor(terms[:, m, :], terms[:, m, :], keep[:, :], ALU.mult))

        swiglu(c, "L0_attn", tiles, a["L0_w"], down=a["L0_down"], extra_loads=loads, extra_dve=make_terms,
               extra_pe=(project, series), extra_act=ratios)


def product_tiles(c, pe, tail, w, t, chunks=KC):
    nc = c.nc
    if t >= 2:
        pe.wait_ge(tail.out_taken, tail.base + t - 1)
    for k in range(chunks):
        ins = nc.tensor.matmul(tail.out_bank[t % 2][:, :], c.x_feat[:, k, t * P:(t + 1) * P], w[:, k, :],
                               start=k == 0, stop=k == chunks - 1)
    ins.then_inc(tail.out_ready, 1)


def merged_lora(c, a):
    nc = c.nc
    E, R, K = 8, 64, P
    RC = E * R // P
    with ExitStack() as own:
        def sb(n, shape):
            return c.sb(f"lora_{n}", shape, F32, own)

        def sem(n):
            return c.sem(f"lora_{n}")

        w_org, w_eff = sb("w_org", [P, KC, DIM]), sb("w_eff", [P, KC, DIM])
        down, up, up_c = sb("down", [P, RC, DIM]), sb("up", [P, RC, DIM]), sb("up_c", [P, RC, DIM])
        wq, keys = sb("wq", [P, KC, K]), sb("keys", [P, E])
        mean, q, q_wide = sb("mean", [P, KC]), sb("q", [P, 1]), sb("q_wide", [P, P])
        top, neg, e, total, inv, coeff = (sb("top", [P, 1]), sb("neg", [P, 1]), sb("e", [P, E]),
                                          sb("total", [P, 1]), sb("inv", [P, 1]), sb("coeff", [P, E]))
        ones = sb("ones", [P, P])
        tail = Tail(c, c.bank[4:6], c.bank[6:8])
        w_loaded, q_loaded = sem("w_loaded"), sem("q_loaded")
        ones_ready, mean_ready, q_ready, wide_ready = sem("ones"), sem("mean"), sem("q"), sem("wide")
        scores_ready, top_ready, e_ready, coeff_ready = sem("scores"), sem("top"), sem("e"), sem("coeff")
        delta_ready, eff_ready, step = sem("delta"), sem("eff"), sem("step")

        with nc.Block() as block:

            @block.sync
            def _(sp):
                sp.dma_start(wq[:, :, :], a["L0_wq"]).then_inc(q_loaded, 16)
                sp.dma_start(keys[:, :], a["L0_keys"]).then_inc(q_loaded, 16)
                sp.dma_start(up[:, :, :], a["L0_up"]).then_inc(w_loaded, 16)
                sp.dma_start(down[:, :, :], a["L0_lora_down"]).then_inc(w_loaded, 16)
                sp.dma_start(w_org[:, :, :], a["L0_org"]).then_inc(w_loaded, 16)

            @block.gpsimd
            def _(pool):
                nc.gpsimd.memset(ones[:, :], 1.0).then_inc(ones_ready, 1)

            @block.tensor
            def _(pe):
                pe.wait_ge(q_loaded, 32)
                pe.wait_ge(mean_ready, 1)
                for k in range(KC):
                    ins = nc.tensor.matmul(c.bank[0][:, 0:1], wq[:, k, :], mean[:, k:k + 1],
                                           start=k == 0, stop=k == KC - 1)
                ins.then_inc(q_ready, 1)
                pe.wait_ge(wide_ready, 1)
                nc.tensor.matmul(c.bank[1][:, 0:E], q_wide[:, :], keys[:, :], start=True, stop=True)\
                    .then_inc(scores_ready, 1)
                pe.wait_ge(w_loaded, 48)
                pe.wait_ge(coeff_ready, 1)
                for i in range(KC):
                    for r in range(RC):
                        ins = nc.tensor.matmul(c.bank[i][:, :], down[:, r, i * P:(i + 1) * P], up_c[:, r, :],
                                               start=r == 0, stop=r == RC - 1)
                    ins.then_inc(delta_ready, 1)
                pe.wait_ge(eff_ready, KC)
                for t in range(NT):
                    product_tiles(c, pe, tail, w_eff, t)
                    if t:
                        tail.pe(pe, t - 1)
                tail.pe(pe, NT - 1)

            @block.scalar
            def _(act):
                act.wait_ge(top_ready, 1)
                nc.scalar.activation(e[:, :], c.bank[1][:, 0:E], ACT.Exp, bias=neg[:, 0:1], scale=K ** -0.5)\
                    .then_inc(e_ready, 1)
                tail.act(act)

            @block.vector
            def _(dve):
                count = 0

                def then(ins):
                    nonlocal count
                    count += 1
                    ins.then_inc(step, 1)
                    dve.wait_ge(step, count)

                then(nc.vector.tensor_reduce(mean[:, :], c.x_feat[:, :, :], AX.X, ALU.add))
                nc.vector.tensor_scalar(mean[:, :], mean[:, :], 1.0 / TOK, None, ALU.mult).then_inc(mean_ready, 1)
                dve.wait_ge(q_ready, 1)
                then(nc.vector.tensor_copy(q[:, :], c.bank[0][:, 0:1]))
                dve.wait_ge(ones_ready, 1)
                nc.vector.tensor_scalar(q_wide[:, :], ones[:, :], q[:, 0:1], None, ALU.mult).then_inc(wide_ready, 1)
                dve.wait_ge(scores_ready, 1)
                then(nc.vector.tensor_reduce(top[:, :], c.bank[1][:, 0:E], AX.X, ALU.max))
                nc.vector.tensor_scalar(neg[:, :], top[:, :], -(K ** -0.5), None, ALU.mult).then_inc(top_ready, 1)
                dve.wait_ge(e_ready, 1)
                then(nc.vector.tensor_reduce(total[:, :], e[:, :], AX.X, ALU.add))
                then(nc.vector.reciprocal(inv[:, :], total[:, :]))
                then(nc.vector.tensor_scalar(coeff[:, :], e[:, :], inv[:, 0:1], None, ALU.mult))
                dve.wait_ge(w_loaded, 48)
                for r in range(RC):
                    for h in range(P // R):
                        rows, expert = slice(h * R, (h + 1) * R), r * (P // R) + h
                        ins = nc.vector.tensor_scalar(up_c[rows, r, :], up[rows, r, :],
                                                      coeff[rows, expert:expert + 1], None, ALU.mult)
                ins.then_inc(coeff_ready, 1)
                for i in range(KC):
                    dve.wait_ge(delta_ready, i + 1)
                    nc.vector.tensor_tensor(w_eff[:, i, :], w_org[:, i, :], c.bank[i][:, :], ALU.add)\
                        .then_inc(eff_ready, 1)
                for t in range(NT):
                    tail.dve(dve, t)


def single_key_attention(c, a):
    nc = c.nc
    KV, PER = 8, 4
    with ExitStack() as own:
        def sb(n, shape):
            return c.sb(f"single_{n}", shape, F32, own)

        def sem(n):
            return c.sem(f"single_{n}")

        wv, wo = sb("wv", [P, KV, DIM]), sb("wo", [P, KV, PER, DIM])
        pair, wo_sum, w_eff = sb("pair", [P, 2, DIM]), sb("wo_sum", [P, KV, DIM]), sb("w_eff", [P, KC, DIM])
        tail = Tail(c, c.bank[4:6], c.bank[6:8])
        wv_loaded, wo_loaded = sem("wv_loaded"), [sem(f"wo_loaded{g}") for g in range(KV)]
        paired, summed, merged, eff_ready = sem("paired"), sem("summed"), sem("merged"), sem("eff_ready")

        with nc.Block() as block:

            @block.sync
            def _(sp):
                c.rot.load(sp, a)
                sp.dma_start(wv[:, :, :], a["L1_wv"]).then_inc(wv_loaded, 16)
                for g in range(KV):
                    sp.dma_start(wo[:, g, :, :], a["L1_wo"][g]).then_inc(wo_loaded[g], 16)

            block.gpsimd(c.rot.pool)

            @block.tensor
            def _(pe):
                pe.wait_ge(wv_loaded, 16)
                for g in range(KV):
                    pe.wait_ge(summed, g + 1)
                    for i in range(KC):
                        ins = nc.tensor.matmul(c.bank[i][:, :], wv[:, g, i * P:(i + 1) * P], wo_sum[:, g, :],
                                               start=g == 0, stop=g == KV - 1)
                ins.then_inc(merged, 1)
                pe.wait_ge(eff_ready, 1)
                for t in range(NT):
                    product_tiles(c, pe, tail, w_eff, t)
                    if t:
                        tail.pe(pe, t - 1)
                tail.pe(pe, NT - 1)

            @block.scalar
            def _(act):
                c.rot.act(act)
                tail.act(act)

            @block.vector
            def _(dve):
                c.rot.dve(dve)
                for g in range(KV):
                    dve.wait_ge(wo_loaded[g], 16)
                    if g:
                        dve.wait_ge(summed, g)
                    nc.vector.tensor_tensor(pair[:, :, :], wo[:, g, 0:2, :], wo[:, g, 2:4, :], ALU.add)\
                        .then_inc(paired, 1)
                    dve.wait_ge(paired, g + 1)
                    nc.vector.tensor_tensor(wo_sum[:, g, :], pair[:, 0, :], pair[:, 1, :], ALU.add)\
                        .then_inc(summed, 1)
                dve.wait_ge(merged, 1)
                for i in range(KC):
                    ins = nc.vector.tensor_copy(w_eff[:, i, :], c.bank[i][:, :])
                ins.then_inc(eff_ready, 1)
                for t in range(NT):
                    tail.dve(dve, t)


def two_loras(c, a):
    nc = c.nc
    R, SCALING = 64, 16 / 64
    with ExitStack() as own:
        def sb(n, shape):
            return c.sb(f"two_{n}", shape, F32, own)

        def sem(n):
            return c.sem(f"two_{n}")

        base, w_eff, bias = sb("base", [P, KC, DIM]), sb("w_eff", [P, KC, DIM]), sb("bias", [P, DIM])
        low, high = sb("low", [R, 2, DIM]), sb("high", [R, 2, DIM])
        low_sum, high_sum = sb("low_sum", [R, DIM]), sb("high_sum", [R, DIM])
        tail = Tail(c, c.bank[4:6], c.bank[6:8])
        loaded, summed, delta_ready, eff_ready = sem("loaded"), sem("summed"), sem("delta"), sem("eff")
        base_loaded = sem("base_loaded")

        with nc.Block() as block:

            @block.sync
            def _(sp):
                sp.dma_start(low[:, :, :], a["L2_low"]).then_inc(loaded, 16)
                sp.dma_start(high[:, :, :], a["L2_high"]).then_inc(loaded, 16)
                sp.dma_start(base[:, :, :], a["L2_base"]).then_inc(base_loaded, 16)
                sp.dma_start(bias[:, :], a["L2_bias"].partition_broadcast(P)).then_inc(base_loaded, 16)

            @block.tensor
            def _(pe):
                pe.wait_ge(summed, 2)
                for i in range(KC):
                    nc.tensor.matmul(c.bank[i][:, :], low_sum[:, i * P:(i + 1) * P], high_sum[:, :],
                                     start=True, stop=True).then_inc(delta_ready, 1)
                pe.wait_ge(eff_ready, KC)
                for t in range(NT):
                    product_tiles(c, pe, tail, w_eff, t)
                    if t:
                        tail.pe(pe, t - 1)
                tail.pe(pe, NT - 1)

            @block.scalar
            def _(act):
                tail.act(act)

            @block.vector
            def _(dve):
                dve.wait_ge(loaded, 32)
                for pair, total in ((low, low_sum), (high, high_sum)):
                    nc.vector.tensor_tensor(total[:, :], pair[:, 0, :], pair[:, 1, :], ALU.add).then_inc(summed, 1)
                dve.wait_ge(base_loaded, 32)
                for i in range(KC):
                    dve.wait_ge(delta_ready, i + 1)
                    nc.vector.scalar_tensor_tensor(w_eff[:, i, :], c.bank[i][:, :], SCALING, base[:, i, :],
                                                   ALU.mult, ALU.add).then_inc(eff_ready, 1)
                for t in range(NT):
                    tail.dve(dve, t, bias)


C_DIM, C_DEPTH, C_FF = 64, 4, 256


class Rotation:

    LEVELS = 10

    def __init__(self, c, own):
        self.c = c
        self.wave = c.sb("wave", [P, C_DEPTH, TOK], F32)
        self.decay = c.sb("decay", [P, C_DEPTH], F32)
        self.start = c.sb("scan_start", [P, C_DEPTH], F32)
        self.half_ready = c.sem("rot_done")
        self.other = c.sb("rot_other", [P, C_DEPTH, TOK // 2], F32, own)
        self.tmp = c.sb("rot_tmp", [P, C_DEPTH, TOK // 2], F32, own)
        self.par = c.sb("rot_par", [P, 4, C_DEPTH], F32, own)
        self.turn = c.sb("rot_turn", [P, self.LEVELS, 2, C_DEPTH], F32, own)
        self.small = c.sb("rot_small", [P, 8, C_DEPTH], F32, own)
        self.sign = c.sb("rot_sign", [P, 1], F32, own)
        self.loaded, self.step = c.sem("rot_loaded"), c.sem("rot_step")
        self.size_ready, self.root_ready = c.sem("rot_size"), c.sem("rot_root")
        self.decay_ready = c.sem("rot_decay")
        self.turns_ready, self.turn_step = c.sem("rot_turns"), c.sem("rot_turn_step")

    def load(self, sp, a):
        sp.dma_start(self.par[:, :, :], a["L2_par"]).then_inc(self.loaded, 16)

    def act(self, act):
        nc, small = self.c.nc, self.small
        act.wait_ge(self.size_ready, 1)
        nc.scalar.activation(small[:, 5, :], small[:, 4, :], ACT.Sqrt).then_inc(self.root_ready, 1)
        act.wait_ge(self.size_ready, 2)
        nc.scalar.activation(self.decay[:, :], small[:, 6, :], ACT.Tanh).then_inc(self.decay_ready, 1)

    def dve(self, dve):
        nc, small, par = self.c.nc, self.small, self.par
        count = 0

        def then(ins):
            nonlocal count
            count += 1
            ins.then_inc(self.turn_step, 1)
            dve.wait_ge(self.turn_step, count)

        tt, ts, stt = nc.vector.tensor_tensor, nc.vector.tensor_scalar, nc.vector.scalar_tensor_tensor
        big, zero, re, im, size, root, length = (small[:, i, :] for i in range(7))
        dve.wait_ge(self.loaded, 16)
        then(stt(re, par[:, 0, :], -1.0, par[:, 0, :], ALU.mult, ALU.max))
        then(stt(im, par[:, 1, :], -1.0, par[:, 1, :], ALU.mult, ALU.max))
        then(tt(big, re, im, ALU.max))
        then(ts(zero, big, 0.0, None, ALU.is_equal))
        then(tt(length, big, zero, ALU.add))
        then(nc.vector.reciprocal(size, length))
        then(tt(re, par[:, 0, :], size, ALU.mult))
        then(tt(im, par[:, 1, :], size, ALU.mult))
        then(tt(re, re, zero, ALU.add))
        then(tt(size, re, re, ALU.mult))
        then(tt(root, im, im, ALU.mult))
        tt(size, size, root, ALU.add).then_inc(self.size_ready, 1)
        dve.wait_ge(self.root_ready, 1)
        then(tt(length, big, root, ALU.mult))
        nc.vector.tensor_copy(length, length).then_inc(self.size_ready, 1)
        then(nc.vector.reciprocal(size, root))
        then(tt(re, re, size, ALU.mult))
        then(tt(im, im, size, ALU.mult))
        then(tt(size, re, re, ALU.mult))
        then(tt(root, im, im, ALU.mult))
        then(tt(size, size, root, ALU.add))
        then(ts(size, size, -0.5, 1.5, ALU.mult, ALU.add))
        turn = self.turn
        then(tt(turn[:, 0, 0, :], re, size, ALU.mult))
        then(tt(turn[:, 0, 1, :], im, size, ALU.mult))
        for n in range(1, self.LEVELS):
            cos, sin = turn[:, n - 1, 0, :], turn[:, n - 1, 1, :]
            then(tt(re, cos, cos, ALU.mult))
            then(tt(im, sin, sin, ALU.mult))
            then(tt(turn[:, n, 0, :], re, im, ALU.subtract))
            then(stt(turn[:, n, 1, :], cos, 2.0, sin, ALU.mult, ALU.mult))
        nc.vector.tensor_copy(re, re).then_inc(self.turns_ready, 1)

    def pool(self, pool):
        nc, wave, other, tmp = self.c.nc, self.wave, self.other, self.tmp
        count = 0

        def then(ins):
            nonlocal count
            count += 1
            ins.then_inc(self.step, 1)
            pool.wait_ge(self.step, count)

        mul = nc.gpsimd.tensor_tensor
        for half, (re, im, sign) in enumerate(((1.0, 0.0, 1.0), (0.0, 1.0, -1.0))):
            rows = slice(half * C_DIM, (half + 1) * C_DIM)
            nc.gpsimd.memset(wave[rows, :, 0:1], re)
            nc.gpsimd.memset(other[rows, :, 0:1], im)
            then(nc.gpsimd.memset(self.sign[rows, :], sign))
        pool.wait_ge(self.turns_ready, 1)
        for level in range(self.LEVELS):
            n = 1 << level
            cos, sin = (self.turn[:, level, i, :].unsqueeze(2).to_broadcast([P, C_DEPTH, n]) for i in range(2))
            src, dst = slice(0, n), slice(n, 2 * n)
            then(mul(tmp[:, :, src], other[:, :, src], sin, ALU.mult))
            then(mul(wave[:, :, dst], wave[:, :, src], cos, ALU.mult))
            then(mul(wave[:, :, dst], wave[:, :, dst], tmp[:, :, src], ALU.subtract))
            if level < self.LEVELS - 1:
                then(mul(tmp[:, :, src], wave[:, :, src], sin, ALU.mult))
                then(mul(other[:, :, dst], other[:, :, src], cos, ALU.mult))
                then(mul(other[:, :, dst], other[:, :, dst], tmp[:, :, src], ALU.add))
        pool.wait_ge(self.loaded, 16)
        then(mul(tmp[:, :, 0], self.par[:, 2, :], wave[:, :, 1], ALU.mult))
        then(mul(tmp[:, :, 1], self.par[:, 3, :], other[:, :, 1], ALU.mult))
        then(mul(tmp[:, :, 0], tmp[:, :, 0], tmp[:, :, 1], ALU.subtract))
        nc.gpsimd.tensor_scalar(self.start[:, :], tmp[:, :, 0], self.sign[:, 0:1], None, ALU.mult)\
            .then_inc(self.half_ready, 1)


def conv_stack(c, a):
    nc, rot = c.nc, c.rot
    FT = C_FF // P
    LOW = C_DIM
    with ExitStack() as own:
        def sb(n, shape):
            return c.sb(f"conv_{n}", shape, F32, own)

        def sem(n):
            return c.sem(f"conv_{n}")

        w_in, w_out = sb("w_in", [P, KC, LOW]), sb("w_out", [LOW, DIM])
        w1_all, w2 = sb("w1_all", [LOW, C_DEPTH, C_FF]), sb("w2", [P, C_DEPTH, FT, LOW])
        w1 = sb("w1", [LOW, C_FF])
        cols, col, last_cols = sb("cols", [P, C_DEPTH, 4 + FT]), sb("col", [P, 4 + FT]), sb("last_cols", [LOW, 2])
        rows = sb("rows", [P, 2 * C_DEPTH + 1, LOW])
        out_bias = sb("out_bias", [P, DIM])
        fold = sb("fold", [P, LOW])
        fold_sc = sb("fold_sc", [P, C_DEPTH, LOW])
        h, centred, square = sb("h", [P, NT, LOW]), sb("centred", [P, NT, LOW]), sb("square", [P, NT, LOW])
        twice = sb("twice", [P, NT, 2, LOW])
        total, mean, var, rstd = sb("total", [P, NT]), sb("mean", [P, NT]), sb("var", [P, NT]), sb("rstd", [P, NT])
        power = sb("power", [P, NT])
        y, turned, state, back = sb("y", [P, TOK]), sb("turned", [P, TOK]), sb("state", [P, TOK]), sb("back", [P, TOK])
        normed2, hidden = sb("normed2", [LOW, TOK]), sb("hidden", [P, FT, TOK])
        tail = Tail(c, c.bank[4:6], c.bank[6:8])
        tr_bank, half_bank, ff_bank = c.bank[0:2], (c.bank[2], c.bank[7]), c.bank[3:7]
        HT = NT // 2

        loaded, const = sem("loaded"), sem("const")
        step, h_in = sem("step"), sem("h_in")
        var_ready, rstd_ready = sem("var_ready"), sem("rstd_ready")
        normed, turned_up, y_ready = sem("normed"), sem("transposed"), sem("y_ready")
        back_ready, conv_ready = sem("back_ready"), sem("conv_ready")
        w1_ready, ff_ready, hidden_ready, mlp_ready = sem("w1_ready"), sem("ff_ready"), sem("hidden"), sem("mlp")
        n2_ready, col_ready = sem("n2_ready"), sem("col_ready")
        LOADS = 16 * 10

        with nc.Block() as block:

            @block.sync
            def _(sp):
                for dst, src in ((w_in, "C_in"), (w_out, "C_out"), (w1_all, "C_w1"), (w2, "C_w2"), (cols, "C_cols"),
                                 (last_cols, "C_last")):
                    sp.dma_start(dst[:], a[src]).then_inc(loaded, 16)
                for i, src in enumerate(("C_b2", "C_sc")):
                    part = rows[:, i * C_DEPTH:(i + 1) * C_DEPTH, :]
                    sp.dma_start(part, a[src].partition_broadcast(P)).then_inc(loaded, 16)
                sp.dma_start(rows[:, 2 * C_DEPTH, :], a["C_bin"].partition_broadcast(P)).then_inc(loaded, 16)
                sp.dma_start(out_bias[:, :], a["C_bout"].partition_broadcast(P)).then_inc(loaded, 16)

            @block.gpsimd
            def _(pool):
                nc.gpsimd.memset(power[:, :], -0.5).then_inc(const, 1)
                nc.gpsimd.memset(fold[:, :], 0.0).then_inc(const, 1)
                pool.wait_ge(const, 2)
                nc.gpsimd.affine_select(out=fold[:, :], in_=fold[:, :], compare_op=ALU.not_equal, fill=1.0,
                                        base=0, pattern=[[-1, LOW]], channel_multiplier=1).then_inc(const, 1)
                pool.wait_ge(const, 3)
                nc.gpsimd.affine_select(out=fold[:, :], in_=fold[:, :], compare_op=ALU.not_equal, fill=1.0,
                                        base=-LOW, pattern=[[-1, LOW]], channel_multiplier=1).then_inc(const, 1)
                pool.wait_ge(const, 4)
                pool.wait_ge(loaded, LOADS)
                for i in range(C_DEPTH):
                    ins = nc.gpsimd.tensor_tensor(fold_sc[:, i, :], fold[:, :], rows[:, C_DEPTH + i, :], ALU.mult)
                ins.then_inc(const, 1)

                def root(n):
                    for half in range(2):
                        tiles = slice(half * HT, (half + 1) * HT)
                        pool.wait_ge(var_ready, 2 * n + half + 1)
                        nc.gpsimd.tensor_tensor(rstd[:, tiles], var[:, tiles], power[:, tiles], ALU.pow)\
                            .then_inc(rstd_ready, 1)

                def prepare(i, first):
                    if not first:
                        pool.wait_ge(ff_ready, 4 * i)
                    nc.gpsimd.tensor_copy(w1[:, :], w1_all[:, i, :]).then_inc(w1_ready, 1)
                    if not first:
                        pool.wait_ge(hidden_ready, 4 * i)
                    nc.gpsimd.tensor_copy(col[:, :], cols[:, i, :]).then_inc(col_ready, 1)
                    root(2 * i)
                    root(2 * i + 1)

                prepare(0, True)
                with pool.Fori(1, C_DEPTH) as i:
                    prepare(i, False)
                root(2 * C_DEPTH)

            @block.tensor
            def _(pe):
                pe.wait_ge(loaded, LOADS)
                for t in range(NT):
                    for k in range(KC):
                        ins = nc.tensor.matmul(half_bank[t // HT][:, t % HT * LOW:(t % HT + 1) * LOW],
                                               c.x_feat[:, k, t * P:(t + 1) * P], w_in[:, k, :],
                                               start=k == 0, stop=k == KC - 1)
                ins.then_inc(h_in, 1)

                def transposes(n):
                    for half in range(2):
                        pe.wait_ge(normed, 2 * n + half + 1)
                        for t in range(NT // 2):
                            ins = nc.tensor.transpose(tr_bank[half][:, t * P:(t + 1) * P],
                                                      twice[:, half * NT // 2 + t, :, :]
                                                      .rearrange("p a d -> p (a d)"), c.ident[:, :])
                        ins.then_inc(turned_up, 1)

                def layer(i):
                    transposes(2 * i)
                    for half in range(2):
                        pe.wait_ge(back_ready, 2 * i + half + 1)
                        for t in range(half * NT // 2, (half + 1) * NT // 2):
                            ins = nc.tensor.matmul(half_bank[half][:, t % HT * LOW:(t % HT + 1) * LOW],
                                                   back[:, t * P:(t + 1) * P], fold_sc[:, i, :],
                                                   start=True, stop=True)
                        ins.then_inc(conv_ready, 1)
                    transposes(2 * i + 1)
                    pe.wait_ge(w1_ready, i + 1)
                    for half in range(2):
                        pe.wait_ge(n2_ready, 2 * i + half + 1)
                        for f in range(FT):
                            nc.tensor.matmul(ff_bank[2 * half + f][:, :], w1[:, f * P:(f + 1) * P],
                                             normed2[:, half * HALF:(half + 1) * HALF],
                                             start=True, stop=True).then_inc(ff_ready, 1)
                    for half in range(2):
                        pe.wait_ge(hidden_ready, 4 * i + 2 * half + 2)
                        for t in range(half * NT // 2, (half + 1) * NT // 2):
                            for f in range(FT):
                                ins = nc.tensor.matmul(half_bank[half][:, t % HT * LOW:(t % HT + 1) * LOW],
                                                       hidden[:, f, t * P:(t + 1) * P], w2[:, i, f, :],
                                                       start=f == 0, stop=f == FT - 1)
                        ins.then_inc(mlp_ready, 1)

                pe.wait_ge(const, 5)
                with pe.Fori(0, C_DEPTH) as i:
                    layer(i)
                transposes(2 * C_DEPTH)
                pe.wait_ge(n2_ready, 2 * C_DEPTH + 2)
                for t in range(NT):
                    if t >= 2:
                        pe.wait_ge(tail.out_taken, tail.base + t - 1)
                    nc.tensor.matmul(tail.out_bank[t % 2][:, :], normed2[:, t * P:(t + 1) * P], w_out[:, :],
                                     start=True, stop=True).then_inc(tail.out_ready, 1)
                    if t:
                        tail.pe(pe, t - 1)
                tail.pe(pe, NT - 1)

            @block.scalar
            def _(act):
                act.wait_ge(loaded, LOADS)

                def affine(n, weight, bias):
                    for half in range(2):
                        act.wait_ge(turned_up, 2 * n + half + 1)
                        nc.scalar.activation(normed2[:, half * HALF:(half + 1) * HALF], tr_bank[half][0:LOW, :],
                                             ACT.Identity, scale=weight, bias=bias).then_inc(n2_ready, 1)

                with act.Fori(0, C_DEPTH) as i:
                    act.wait_ge(col_ready, i + 1)
                    for half in range(2):
                        act.wait_ge(turned_up, 4 * i + half + 1)
                        nc.scalar.activation(y[:, half * HALF:(half + 1) * HALF], tr_bank[half][:, :], ACT.Silu,
                                             scale=col[:, 0:1], bias=col[:, 1:2])\
                            .then_inc(y_ready, 1)
                    affine(2 * i + 1, col[0:LOW, 2:3], col[0:LOW, 3:4])
                    for half in range(2):
                        for f in range(FT):
                            act.wait_ge(ff_ready, 4 * i + 2 * half + f + 1)
                            nc.scalar.activation(hidden[:, f, half * HALF:(half + 1) * HALF],
                                                 ff_bank[2 * half + f][:, :], ACT.Silu,
                                                 bias=col[:, 4 + f:5 + f]).then_inc(hidden_ready, 1)
                affine(2 * C_DEPTH, last_cols[:, 0:1], last_cols[:, 1:2])
                tail.act(act)

            @block.vector
            def _(dve):
                state_of = {"count": 0, "base": 0}

                def then(ins):
                    state_of["count"] += 1
                    ins.then_inc(step, 1)
                    dve.wait_ge(step, state_of["base"] + state_of["count"])

                tt, ts = nc.vector.tensor_tensor, nc.vector.tensor_scalar

                def tiles(half):
                    return slice(half * HT, (half + 1) * HT)

                def by_tile(x, half):
                    return x[:, tiles(half)].unsqueeze(2).to_broadcast([P, HT, LOW])

                def flat(half):
                    return h[:, tiles(half), :].rearrange("p t d -> p (t d)")

                def norm(n, copies):
                    for half in range(2):
                        at = tiles(half)
                        then(nc.vector.tensor_reduce(total[:, at], h[:, at, :], AX.X, ALU.add))
                        then(ts(mean[:, at], total[:, at], 1.0 / LOW, None, ALU.mult))
                        then(tt(centred[:, at, :], h[:, at, :], by_tile(mean, half), ALU.subtract))
                        then(tt(square[:, at, :], centred[:, at, :], centred[:, at, :], ALU.mult))
                        then(nc.vector.tensor_reduce(total[:, at], square[:, at, :], AX.X, ALU.add))
                        ts(var[:, at], total[:, at], 1.0 / LOW, EPS, ALU.mult, ALU.add).then_inc(var_ready, 1)
                    for half in range(2):
                        at = tiles(half)
                        dve.wait_ge(rstd_ready, 2 * n + half + 1)
                        for j in range(copies):
                            ins = tt(twice[:, at, j, :], centred[:, at, :], by_tile(rstd, half), ALU.mult)
                        ins.then_inc(normed, 1)

                dve.wait_ge(loaded, LOADS)
                dve.wait_ge(rot.half_ready, 1)
                dve.wait_ge(rot.decay_ready, 1)
                dve.wait_ge(h_in, 1)
                for half in range(2):
                    then(tt(h[:, tiles(half), :], half_bank[half][:, 0:HT * LOW].rearrange("p (t d) -> p t d", t=HT),
                            rows[:, 2 * C_DEPTH, :].unsqueeze(1).to_broadcast([P, HT, LOW]), ALU.add))
                PRE, STEPS = state_of["count"], 30

                with dve.Fori(0, C_DEPTH) as i:
                    state_of["count"], state_of["base"] = PRE, STEPS * i
                    norm(2 * i, 2)
                    for half in range(2):
                        part = slice(half * HALF, (half + 1) * HALF)
                        dve.wait_ge(y_ready, 2 * i + half + 1)
                        then(tt(turned[:, part], y[:, part], rot.wave[:, i, part], ALU.mult))
                        before = rot.start[:, bass.ds(i, 1)] if half == 0 else state[:, HALF - 1:HALF]
                        then(nc.vector.tensor_tensor_scan(state[:, part],
                                                          rot.decay[:, bass.ds(i, 1)].to_broadcast([P, HALF]),
                                                          turned[:, part], before, ALU.mult, ALU.add))
                        tt(back[:, part], state[:, part], rot.wave[:, i, part], ALU.mult).then_inc(back_ready, 1)
                    for half in range(2):
                        dve.wait_ge(conv_ready, 2 * i + half + 1)
                        then(tt(flat(half), flat(half), half_bank[half][:, 0:HT * LOW], ALU.add))
                    norm(2 * i + 1, 1)
                    for half in range(2):
                        dve.wait_ge(mlp_ready, 2 * i + half + 1)
                        then(tt(flat(half), flat(half), half_bank[half][:, 0:HT * LOW], ALU.add))
                        then(tt(h[:, tiles(half), :], h[:, tiles(half), :],
                                rows[:, bass.ds(i, 1), :].to_broadcast([P, HT, LOW]), ALU.add))
                    assert state_of["count"] == PRE + STEPS, state_of
                state_of["count"], state_of["base"] = PRE + STEPS * C_DEPTH, 0
                norm(2 * C_DEPTH, 1)
                for t in range(NT):
                    tail.dve(dve, t, out_bias)


HEADS, HD = 32, 16
PROBS = 8
PAIRS = HEADS // 2
SPLIT = 3 * 2 * HD
SHIFTED = SPLIT + 4


def attention_plan():
    order = list(range(NT))

    def max_units(i):
        keys = (order[i] + 1) * P
        found = []
        for lo in range(0, keys, HALF):
            n = min(HALF, keys - lo)
            per = HALF // n
            found += [(range(h, min(h + per, HEADS)), lo, n) for h in range(0, HEADS, per)]
        return found

    plan, pending, step, value_lag = [], [], 0, 5
    n_max = n_score = n_value = 0

    def later(steps, *event):
        pending.append((step + steps, event))

    def flush(everything=False):
        while pending and (everything or min(pending)[0] <= step):
            at = pending.index(min(pending, key=lambda x: x[0]))
            _, event = pending.pop(at)
            plan.append(event)
            if event[0] == "value" and event[4] and event[3] % 4 == 3:
                later(3, "heads", event[1], event[3] // 4)
            elif event[0] == "heads" and event[2] == 1:
                later(2, "turn", event[1])
            elif event[0] == "turn":
                later(2, "project", event[1])
            elif event[0] == "project":
                later(3, "std", event[1])
            elif event[0] == "std":
                later(1, "norm", event[1])
            elif event[0] == "norm":
                later(3, "feat", event[1])

    for unit in max_units(0):
        plan.append(("max", 0, n_max, *unit))
        n_max += 1
    plan += [("shift", 0), ("shift_rows", 0)]
    for i, qt in enumerate(order):
        todo = max_units(i + 1) if i + 1 < NT else []
        total, steps = len(todo), 8 * (qt + 1)
        for n in range(steps):
            four, kt, u = n // (4 * (qt + 1)), n // 4 % (qt + 1), n % 4
            u += 4 * four
            plan.append(("score", i, n_score, u, kt))
            later(value_lag, "value", i, n_score, u, kt == qt, kt)
            n_score += 1
            step += 1
            done = total - len(todo)
            want = min(total, -(-total * (n + 1) * 1 // (1 * max(1, steps - 6))))
            for _ in range(want - done):
                plan.append(("max", i + 1, n_max, *todo.pop(0)))
                n_max += 1
                if not todo:
                    plan.append(("shift", i + 1))
                    later(2, "shift_rows", i + 1)
            flush()
        rest = [p for p in pending if p[1][0] == "shift_rows"]
        for p in rest:
            pending.remove(p)
            plan.append(p[1])
    step += 1000
    flush(everything=True)
    while pending:
        flush(everything=True)
    return order, plan


def causal_attention(c, a):
    nc = c.nc
    order, plan = attention_plan()
    TURNS = ("shift_rows", "heads", "turn", "project", "feat")
    turn_use = {e: n for n, e in enumerate(e for e in plan if e[0] in TURNS)}
    SCALE = HD ** -0.5
    HIDE = -3.0e38
    with ExitStack() as own:
        def sb(n, shape, dt=F32, scope=own):
            return c.sb(f"mqa_{n}", shape, dt, scope)

        def sem(n):
            return c.sem(f"mqa_{n}")

        wq, wo = sb("wq", [P, KC, DIM]), sb("wo", [P, KC, DIM])
        wk = sb("wk", [P, KC, 2, P])
        bq, bk, bo = sb("bq", [P, KC]), sb("bk", [P, 2]), sb("bo", [P, DIM])
        stack = sb("stack", [P, PAIRS, TOK], F32R)
        q_hi, q_lo = sb("q_hi", [P, 2, TOK], F32R), sb("q_lo", [P, 2, TOK], F32R)
        keys = sb("keys", [P, 2, TOK], F32R)
        v_feat, v = sb("v_feat", [P, TOK]), sb("v", [P, NT, 2 * HD])
        ident_b, hide_k, hide_q = sb("ident_b", [P, P], BF16), sb("hide_k", [P, P], BF16), sb("hide_q", [P, 4, P], BF16)
        top, shift = sb("top", [P, 2, 2, HEADS]), sb("shift", [P, 2, 2, 2, PAIRS], F32R)
        both = sb("both", [P, HEADS])
        rows = sb("rows", [4 * PAIRS, 2, P], F32R)
        prob = sb("prob", [P, PROBS, HALF])
        o_sb = sb("o_sb", [P, 2, HALF])
        inv = sb("inv", [P, 4, 2, 2])
        attn, a_feat = sb("attn", [P, 2, DIM]), sb("a_feat", [P, 2, KC, P])
        max_bank, score_bank, value_bank = [c.bank[0], c.bank[1], c.bank[7]], c.bank[2:4], c.bank[4:6]
        turn_bank = c.bank[6]

        w_loaded, wo_loaded, const = sem("w_loaded"), sem("wo_loaded"), sem("const")
        q_ready, q_rounded, q_split = sem("q_ready"), sem("q_rounded"), sem("q_split")
        k_ready, k_rounded, k_split, v_turned, v_ready = (sem("k_ready"), sem("k_rounded"), sem("k_split"),
                                                          sem("v_turned"), sem("v_ready"))
        stacked = [sem(f"stacked{i}") for i in range(KC)]
        max_ready, max_taken, step = sem("max_ready"), sem("max_taken"), sem("step")
        shift_ready, shift_turned = sem("shift_ready"), sem("shift_turned")
        rows_sent = [sem(f"rows_sent{i}") for i in range(2)]
        score_ready, exp_ready, value_done = sem("score_ready"), sem("exp_ready"), sem("value_done")
        o_copied, heads_turned = sem("o_copied"), sem("heads_turned")
        turned, out_ready = sem("turned"), sem("out_ready")
        var_ready, std_ready, normed = sem("var_ready"), sem("std_ready"), sem("normed")
        feat_turned, turn_taken = sem("feat_turned"), sem("turn_taken")

        def cols(t):
            return slice(t * P, (t + 1) * P)

        with nc.Block() as block:

            @block.sync
            def _(sp):
                for dst, src in ((wq, "A_wq"), (wk, "A_wk"), (bq, "A_bq"), (bk, "A_bk")):
                    sp.dma_start(dst[:], a[src]).then_inc(w_loaded, 16)
                sp.dma_start(wo[:, :, :], a["A_wo"]).then_inc(wo_loaded, 16)
                sp.dma_start(bo[:, :], a["A_bo"].partition_broadcast(P)).then_inc(wo_loaded, 16)
                for m in range(KC):
                    sp.wait_ge(q_split, 2 * m + 2)
                    for j in range(4):
                        src = slice(32 * j, 32 * j + 32)
                        for slot, part in enumerate((q_hi, q_hi, q_lo)):
                            sp.dma_start(stack[32 * slot:32 * slot + 32, 4 * m + j, :].bitcast(F32),
                                         part[src, m % 2, :].bitcast(F32))\
                                .then_inc(stacked[m], 16)
                for event in plan:
                    if event[0] == "shift_rows":
                        i = event[1]
                        sp.wait_ge(turn_taken, turn_use[event] + 1)
                        sp.dma_start(stack[SPLIT:SHIFTED, :, cols(order[i])].bitcast(F32), rows[:, i % 2, :].bitcast(F32))\
                            .then_inc(rows_sent[i % 2], 16)

            @block.gpsimd
            def _(pool):
                nc.gpsimd.memset(ident_b[:, :], 0.0)
                nc.gpsimd.memset(hide_k[:, :], 0.0)
                nc.gpsimd.memset(hide_q[:, :, :], 0.0).then_inc(const, 1)
                pool.wait_ge(const, 1)
                nc.gpsimd.affine_select(out=ident_b[:, :], in_=ident_b[:, :], compare_op=ALU.not_equal, fill=1.0,
                                        base=0, pattern=[[-1, P]], channel_multiplier=1)
                nc.gpsimd.affine_select(out=hide_k[:, :], in_=hide_k[:, :], compare_op=ALU.is_ge, fill=HIDE,
                                        base=0, pattern=[[-1, P]], channel_multiplier=1)
                nc.gpsimd.affine_select(out=hide_q[:, :, :], in_=hide_q[:, :, :], compare_op=ALU.is_ge, fill=HIDE,
                                        base=0, pattern=[[0, 4], [1, P]], channel_multiplier=-1).then_inc(const, 1)

            @block.tensor
            def _(pe):
                pe.wait_ge(w_loaded, 64)
                for head in range(2):
                    for half in range(2):
                        for k in range(KC):
                            ins = nc.tensor.matmul(c.bank[4 + 2 * head + half], wk[:, k, head, :],
                                                   c.x_feat[:, k, half * HALF:(half + 1) * HALF],
                                                   start=k == 0, stop=k == KC - 1)
                        ins.then_inc(k_ready, 1)
                for m in range(KC):
                    for half in range(2):
                        n = 2 * m + half
                        if n >= 4:
                            pe.wait_ge(q_split, n - 3)
                        for k in range(KC):
                            ins = nc.tensor.matmul(c.bank[n % 4], wq[:, k, cols(m)],
                                                   c.x_feat[:, k, half * HALF:(half + 1) * HALF],
                                                   start=k == 0, stop=k == KC - 1)
                        ins.then_inc(q_ready, 1)
                pe.wait_ge(k_split, 4)
                for t in range(NT):
                    ins = nc.tensor.transpose(c.bank[4][:, t * 2 * HD:(t + 1) * 2 * HD], v_feat[SPLIT:P, cols(t)],
                                              c.ident[SPLIT:P, SPLIT:P])
                ins.then_inc(v_turned, 1)
                pe.wait_ge(q_split, 8)
                pe.wait_ge(v_ready, 2)
                pe.wait_ge(const, 2)

                for event in plan:
                    kind, i = event[0], event[1]
                    qt = order[i]
                    if turn_use.get(event, 0):
                        pe.wait_ge(turn_taken, turn_use[event])
                    if kind == "max":
                        _, _, n, heads, lo, width = event
                        if n >= 3:
                            pe.wait_ge(max_taken, n - 2)
                        for at, head in enumerate(heads):
                            if i == 0 and lo == 0 and head % 8 == 0:
                                pe.wait_ge(stacked[head // 8], 16 * 12)
                            masked = lo + width == (qt + 1) * P
                            out = max_bank[n % 3]
                            ins = nc.tensor.matmul(out[:, at * width:(at + 1) * width],
                                                   stack[0:SPLIT, head // 2, cols(qt)],
                                                   keys[0:SPLIT, head % 2, lo:lo + width],
                                                   start=True, stop=not masked)
                            if masked:
                                ins = nc.tensor.matmul(out[:, (at + 1) * width - P:(at + 1) * width],
                                                       ident_b[:, :], hide_k[:, :], start=False, stop=True)
                        ins.then_inc(max_ready, 1)
                    elif kind == "shift_rows":
                        pe.wait_ge(shift_ready, i + 1)
                        nc.tensor.transpose(turn_bank[0:4 * PAIRS, 0:P],
                                            shift[:, i % 2, :, :, :].rearrange("p h s j -> p (h s j)").bitcast(F32),
                                            c.ident[:, :]).then_inc(shift_turned, 1)
                    elif kind == "score":
                        _, _, n, u, kt = event
                        if u == 0 and kt == 0:
                            pe.wait_ge(rows_sent[i % 2], 16 * (i // 2 + 1))
                        if n >= 2:
                            pe.wait_ge(exp_ready, n - 1)
                        g, head = divmod(u, 2)
                        ins = nc.tensor.matmul(score_bank[n % 2], keys[0:SHIFTED, head, cols(kt)],
                                               stack[0:SHIFTED, 4 * g:4 * g + 4, cols(qt)],
                                               start=True, stop=kt != qt)
                        if kt == qt:
                            ins = nc.tensor.matmul(score_bank[n % 2], ident_b[:, :],
                                                   hide_q[:, :, :].rearrange("p a b -> p (a b)"),
                                                   start=False, stop=True)
                        ins.then_inc(score_ready, 1)
                    elif kind == "value":
                        _, _, n, u, final, kt = event
                        four, row = 2 * i + u // 4, 32 * (u % 4)
                        if kt == 0 and u % 4 == 0 and four >= 2:
                            pe.wait_ge(o_copied, four - 1)
                        pe.wait_ge(exp_ready, n + 1)
                        nc.tensor.matmul(value_bank[four % 2][row:row + 32, :], v[:, kt, :], prob[:, n % PROBS, :],
                                         start=kt == 0, stop=final).then_inc(value_done, 1)
                    elif kind == "heads":
                        four = 2 * i + event[2]
                        pe.wait_ge(o_copied, four + 1)
                        for j in range(4):
                            ins = nc.tensor.transpose(turn_bank[:, cols(j)], o_sb[:, four % 2, cols(j)], c.ident[:, :])
                        ins.then_inc(heads_turned, 1)
                    elif kind == "turn":
                        pe.wait_ge(turn_taken, turn_use[("heads", i, 1)] + 1)
                        for k in range(KC):
                            ins = nc.tensor.transpose(turn_bank[:, cols(k)], attn[:, i % 2, cols(k)], c.ident[:, :])
                        ins.then_inc(turned, 1)
                    elif kind == "project":
                        if i == 0:
                            pe.wait_ge(wo_loaded, 32)
                        pe.wait_ge(turn_taken, turn_use[("turn", i)] + 1)
                        for k in range(KC):
                            ins = nc.tensor.matmul(turn_bank, a_feat[:, i % 2, k, :], wo[:, k, :],
                                                   start=k == 0, stop=k == KC - 1)
                        ins.then_inc(out_ready, 1)
                    elif kind == "feat":
                        pe.wait_ge(normed, i + 1)
                        for k in range(KC):
                            ins = nc.tensor.transpose(turn_bank[:, cols(k)], c.x_tok[:, qt, cols(k)], c.ident[:, :])
                        ins.then_inc(feat_turned, 1)

            @block.scalar
            def _(act):
                act.wait_ge(w_loaded, 64)
                for head in range(2):
                    for half in range(2):
                        part, bank = slice(half * HALF, (half + 1) * HALF), c.bank[4 + 2 * head + half]
                        act.wait_ge(k_ready, 2 * head + half + 1)
                        if head == 0:
                            nc.scalar.activation(v_feat[SPLIT:P, part], bank[SPLIT:P, :], ACT.Identity,
                                                 bias=bk[SPLIT:P, 0:1])
                        nc.scalar.activation(keys[0:SPLIT, head, part], bank[0:SPLIT, :], ACT.Identity,
                                             bias=bk[0:SPLIT, head:head + 1]).then_inc(k_rounded, 1)
                for n in range(2 * KC):
                    m, half = divmod(n, 2)
                    act.wait_ge(q_ready, n + 1)
                    if m >= 2 and half == 0:
                        act.wait_ge(stacked[m - 2], 16 * 12)
                    nc.scalar.activation(q_hi[:, m % 2, half * HALF:(half + 1) * HALF], c.bank[n % 4], ACT.Identity,
                                         bias=bq[:, m:m + 1]).then_inc(q_rounded, 1)

                for event in plan:
                    kind, i = event[0], event[1]
                    qt = order[i]
                    if kind == "score":
                        n = event[2]
                        act.wait_ge(score_ready, n + 1)
                        if n >= PROBS:
                            act.wait_ge(value_done, n - PROBS + 1)
                        nc.scalar.activation(prob[:, n % PROBS, :], score_bank[n % 2], ACT.Exp, scale=SCALE)\
                            .then_inc(exp_ready, 1)
                    elif kind == "value" and event[4] and event[3] % 4 == 3:
                        _, _, n, u, _, _ = event
                        four = 2 * i + u // 4
                        act.wait_ge(value_done, n + 1)
                        if four >= 2:
                            act.wait_ge(heads_turned, four - 1)
                        nc.scalar.copy(o_sb[:, four % 2, :], value_bank[four % 2]).then_inc(o_copied, 1)
                    elif kind == "shift_rows":
                        act.wait_ge(shift_turned, i + 1)
                        if i >= 2:
                            act.wait_ge(rows_sent[i % 2], 16 * (i // 2))
                        nc.scalar.copy(rows[:, i % 2, :], turn_bank[0:4 * PAIRS, 0:P]).then_inc(turn_taken, 1)
                    elif kind == "turn":
                        act.wait_ge(turned, i + 1)
                        if i >= 2:
                            act.wait_ge(out_ready, i - 1)
                        nc.scalar.copy(a_feat[:, i % 2, :, :].rearrange("p k n -> p (k n)"), turn_bank)\
                            .then_inc(turn_taken, 1)
                    elif kind == "std":
                        act.wait_ge(var_ready, i + 1)
                        nc.scalar.activation(c.std[:, qt:qt + 1], c.mean_var[:, qt, 1:2], ACT.Sqrt,
                                             bias=c.eps[:, 0:1]).then_inc(std_ready, 1)
                    elif kind == "feat":
                        act.wait_ge(feat_turned, i + 1)
                        nc.scalar.copy(c.x_feat[:, :, cols(qt)], turn_bank.rearrange("p (k n) -> p k n", k=KC))\
                            .then_inc(turn_taken, 1)

            @block.vector
            def _(dve):
                count = 0

                def then(ins):
                    nonlocal count
                    count += 1
                    ins.then_inc(step, 1)
                    dve.wait_ge(step, count)

                tt, ts, stt = nc.vector.tensor_tensor, nc.vector.tensor_scalar, nc.vector.scalar_tensor_tensor
                last = slice(SPLIT, SHIFTED)
                for head, (both_rows, first_rows) in enumerate(((0.0, 1.0), (1.0, 0.0))):
                    then(nc.vector.memset(keys[last, head, :].bitcast(F32), both_rows))
                    then(nc.vector.memset(keys[SPLIT:SPLIT + 2, head, :].bitcast(F32), first_rows))
                dve.wait_ge(w_loaded, 64)
                mid = slice(32, 64)
                for head in range(2):
                    for half in range(2):
                        part, bank = slice(half * HALF, (half + 1) * HALF), c.bank[4 + 2 * head + half]
                        dve.wait_ge(k_rounded, 2 * head + half + 1)
                        stt(keys[mid, head, part], bank[mid, :], bk[mid, head:head + 1],
                            keys[mid, head, part].bitcast(F32), ALU.add, ALU.subtract).then_inc(k_split, 1)
                for n in range(2 * KC):
                    m, half = divmod(n, 2)
                    part = slice(half * HALF, (half + 1) * HALF)
                    dve.wait_ge(q_rounded, n + 1)
                    stt(q_lo[:, m % 2, part], c.bank[n % 4], bq[:, m:m + 1],
                        q_hi[:, m % 2, part].bitcast(F32), ALU.add, ALU.subtract).then_inc(q_split, 1)
                dve.wait_ge(v_turned, 1)
                nc.vector.tensor_copy(v[:, :, :], c.bank[4][:, 0:NT * 2 * HD].rearrange("p (t d) -> p t d", t=NT))\
                    .then_inc(v_ready, 1)
                dve.wait_ge(v_ready, 1)
                nc.vector.memset(v[:, :, HD:HD + 1], 1.0).then_inc(v_ready, 1)

                for event in plan:
                    kind, i = event[0], event[1]
                    qt = order[i]
                    row = c.x_tok[:, qt, :]
                    segments = -(-(qt + 1) * P // HALF)
                    if kind == "max":
                        _, _, n, heads, lo, width = event
                        dve.wait_ge(max_ready, n + 1)
                        nc.vector.tensor_reduce(top[:, i % 2, lo // HALF, heads[0]:heads[-1] + 1],
                                                max_bank[n % 3][:, 0:len(heads) * width]
                                                .rearrange("p (h k) -> p h k", h=len(heads)), AX.X, ALU.max)\
                            .then_inc(max_taken, 1)
                    elif kind == "shift":
                        last_max = max(e[2] for e in plan if e[0] == "max" and e[1] == i)
                        dve.wait_ge(max_taken, last_max + 1)
                        if i >= 2:
                            dve.wait_ge(shift_turned, i - 1)
                        if segments == 2:
                            then(tt(both[:, :], top[:, i % 2, 0, :], top[:, i % 2, 1, :], ALU.max))
                            found = both[:, :]
                        else:
                            found = top[:, i % 2, 0, :]
                        found = found.rearrange("p (j h) -> p h j", h=2)
                        high, low = shift[:, i % 2, :, 0, :], shift[:, i % 2, :, 1, :]
                        then(ts(high, found, -1.0, None, ALU.mult))
                        stt(low, found, -1.0, high.bitcast(F32), ALU.mult, ALU.subtract).then_inc(shift_ready, 1)
                    elif kind == "heads":
                        four = event[2]
                        dve.wait_ge(heads_turned, 2 * i + four + 1)
                        if i >= 2 and four == 0:
                            dve.wait_ge(turned, i - 1)
                        parts = turn_bank.rearrange("p (j g h d) -> p g j h d", j=4, g=2, h=2)
                        then(nc.vector.reciprocal(inv[:, :, :, :], turn_bank.rearrange(
                            "p (j g h d) -> p j g h d", j=4, g=2, h=2)[:, :, :, :, HD]))
                        for g in range(2):
                            at = (2 * four + g) * P
                            dst = attn[:, i % 2, at:at + P].rearrange("p (j h d) -> p j h d", j=4, h=2)
                            ins = tt(dst, parts[:, g, :, :, 0:HD],
                                     inv[:, :, g, :].unsqueeze(3).to_broadcast([P, 4, 2, HD]), ALU.mult)
                        ins.then_inc(turn_taken, 1)
                    elif kind == "project":
                        dve.wait_ge(out_ready, i + 1)
                        if i == 0:
                            dve.wait_ge(wo_loaded, 32)
                        tt(row, row, turn_bank, ALU.add).then_inc(turn_taken, 1)
                        dve.wait_ge(turn_taken, turn_use[event] + 1)
                        then(tt(row, row, bo[:, :], ALU.add))
                        then(nc.vector.bn_stats(c.stats[:, qt, :], row))
                        nc.vector.bn_aggr(c.mean_var[:, qt, :], c.stats[:, qt, :]).then_inc(var_ready, 1)
                    elif kind == "norm":
                        dve.wait_ge(std_ready, i + 1)
                        then(nc.vector.reciprocal(c.rstd[:, qt:qt + 1], c.std[:, qt:qt + 1]))
                        ts(row, row, c.mean_var[:, qt, 0:1], c.rstd[:, qt:qt + 1], ALU.subtract, ALU.mult)\
                            .then_inc(normed, 1)


def only_rotation(c, a):
    with c.nc.Block() as block:
        @block.sync
        def _(sp):
            c.rot.load(sp, a)

        @block.vector
        def _(dve):
            c.rot.dve(dve)

        @block.scalar
        def _(act):
            c.rot.act(act)

        @block.gpsimd
        def _(pool):
            c.rot.pool(pool)


LAYERS = ["L0_attn", "L0_ffn", "L1_attn", "L1_ffn", "L2_attn", "L2_ffn", "L3_attn", "L3_ffn"]


def build(nc, a, out):
    with ExitStack() as ctx:
        c = Chip(nc, ctx)
        setup(c, a["x_tok"], a["x_feat"])
        if "L0_attn" in LAYERS:
            gradient_ffn(c, a)
        out_rows = out.rearrange("(t p) n -> t p n", p=P)
        if "L0_ffn" in LAYERS:
            merged_lora(c, a)
        with ExitStack() as scope:
            c.rot = Rotation(c, scope)
            if "L1_attn" in LAYERS:
                single_key_attention(c, a)
            elif "L2_attn" in LAYERS:
                only_rotation(c, a)
        if "L1_ffn" in LAYERS:
            swiglu(c, "L1_ffn", a["L1_w"].shape[0], a["L1_w"], zeros=a["L1_z"], scales=a["L1_s"])
        if "L2_attn" in LAYERS:
            conv_stack(c, a)
        if "L2_ffn" in LAYERS:
            two_loras(c, a)
        if "L3_attn" in LAYERS:
            causal_attention(c, a)
        swiglu(c, "L3_ffn", a["L3_w"].shape[0], a["L3_w"],
               scale=[a["L3_scale_gate"], a["L3_scale_up"], a["L3_scale_down"]], last=out_rows)


def up_tiles(w, tiles):
    w = np.asarray(w)
    w = np.pad(w, ((0, 0), (0, tiles * P - w.shape[1])))
    return w.reshape(KC, P, tiles, P).transpose(2, 1, 0, 3).reshape(tiles, P, KC * P)


def down_tiles(w, tiles):
    w = np.asarray(w)
    return np.pad(w, ((0, tiles * P - w.shape[0]), (0, 0))).reshape(tiles, P, w.shape[1])


def chunks(w):
    return w.reshape(-1, P, w.shape[1]).transpose(1, 0, 2)


def layout(v):
    v = {k: np.asarray(x) for k, x in v.items()}
    x = np.asarray(v["L0_attn_hidden_states"])[0]
    a = {"x_tok": x, "x_feat": x.T}
    a["L1_w"] = np.concatenate([up_tiles(v["L1_ffn_gate_w"], 14), up_tiles(v["L1_ffn_up_w"], 14),
                                down_tiles(v["L1_ffn_down_w"], 14)], 2)
    for n, k in (("z", "z"), ("s", "s")):
        g, u, d = (np.asarray(v[f"L1_ffn_{w}_{k}"]) for w in ("gate", "up", "down"))
        cols = lambda m: m.reshape(KC, 14, P).transpose(1, 0, 2).reshape(14, KC * P)
        a["L1_" + n] = np.concatenate([cols(g), cols(u), d], 1)
    a["L3_w"] = np.concatenate([up_tiles(v["L3_ffn_w_gate"].T, 11), up_tiles(v["L3_ffn_w_up"].T, 11),
                                down_tiles(v["L3_ffn_w_down"].T, 11)], 2)
    for n in ("scale_gate", "scale_up", "scale_down"):
        a["L3_" + n] = v["L3_ffn_" + n].reshape(1)
    a["L0_w"] = np.concatenate([up_tiles(v["L0_attn_ffn_gate_w"].T, 10), up_tiles(v["L0_attn_ffn_up_w"].T, 10)], 2)
    a["L0_down"] = down_tiles(v["L0_attn_ffn_down_w"].T, 10).transpose(1, 0, 2)
    a["L0_proj"] = np.stack([chunks(v["L0_attn_up_w"].T), chunks(v["L0_attn_gate_w"].T)], 1)
    a["L0_fuse"] = np.concatenate([v["L0_attn_local_approx_output"].T[:, None],
                                   v["L0_attn_fuse_weight"].transpose(1, 2, 0)], 1)
    a["L0_point"] = v["L0_attn_local_point"].reshape(P, 1)
    a["L0_disc"] = v["L0_attn_discount_factor"]
    a["L0_org"] = chunks(v["L0_ffn_W_org"].T)
    a["L0_lora_down"] = chunks(v["L0_ffn_lora_down"].transpose(0, 2, 1).reshape(DIM, DIM))
    a["L0_up"] = chunks(v["L0_ffn_lora_up"].reshape(DIM, DIM))
    a["L0_wq"] = chunks(v["L0_ffn_Wq"].T)
    a["L0_keys"] = v["L0_ffn_lora_keys"].T
    qkv = v["L1_attn_weight_qkv"].reshape(8, 6, P, DIM)
    a["L1_wv"] = qkv[:, 5].transpose(1, 0, 2)
    a["L1_wo"] = v["L1_attn_weight_proj"].reshape(DIM, 8, 4, P).transpose(1, 3, 2, 0)
    k_w, k_b = v["L3_attn_wk_w"].T, v["L3_attn_wk_b"]
    wk, bk = np.zeros((DIM, 2, P), k_w.dtype), np.zeros((P, 2), k_b.dtype)
    for head in range(2):
        for slot in range(3):
            at = 32 * slot + HD * head
            wk[:, head, at:at + HD], bk[at:at + HD, head] = k_w, k_b
    wk[:, 0, SPLIT:SPLIT + HD], bk[SPLIT:SPLIT + HD, 0] = v["L3_attn_wv_w"].T, v["L3_attn_wv_b"]
    a["A_wk"] = wk.reshape(KC, P, 2, P).transpose(1, 0, 2, 3)
    a["A_bk"] = bk
    a["A_wq"], a["A_wo"] = chunks(v["L3_attn_wq_w"].T), chunks(v["L3_attn_wo_w"].T)
    a["A_bq"], a["A_bo"] = v["L3_attn_wq_b"].reshape(KC, P).T, v["L3_attn_wo_b"]
    twice = lambda m: np.concatenate([m.T, m.T], 0)
    g = lambda n: v["L2_attn_" + n]
    a["L2_par"] = np.stack([twice(g(n)) for n in ("phz_re", "phz_im", "lc_re", "lc_im")], 1)
    a["C_in"], a["C_out"] = chunks(g("Win").T), g("Wout").T
    a["C_w1"] = g("W1").transpose(2, 0, 1)
    a["C_w2"] = g("W2").reshape(4, 64, 2, P).transpose(3, 0, 2, 1)
    a["C_cols"] = np.concatenate([np.stack([twice(g(n)) for n in ("ln1_w", "ln1_b", "ln2_w", "ln2_b")], 2),
                                  g("b1").reshape(4, 2, P).transpose(2, 0, 1)], 2)
    a["C_last"] = np.stack([g("lnl_w"), g("lnl_b")], 1)
    a["C_b2"], a["C_sc"], a["C_bin"], a["C_bout"] = g("b2"), g("sc_lin"), g("bin"), g("bout")
    a["L2_low"] = np.stack([v["L2_ffn_A"], v["L2_ffn_WL"]], 1)
    a["L2_high"] = np.stack([v["L2_ffn_B"].T, v["L2_ffn_WR"].T], 1)
    a["L2_base"], a["L2_bias"] = chunks(v["L2_ffn_W_base"].T), v["L2_ffn_b_base"]
    return a


def kernel(**inputs):
    import concourse.bacc as bacc
    from concourse.bass_utils import run_bass_kernel_spmd

    nc = bacc.Bacc("TRN2", target_bir_lowering=False, num_devices=1)
    arrays = {f"in_{k}": np.ascontiguousarray(v) for k, v in layout(inputs).items()}
    args = {k[3:]: nc.dram_tensor(k, v.shape, mybir.dt.from_np(v.dtype), kind="ExternalInput").ap()
            for k, v in arrays.items()}
    out = nc.dram_tensor("out_0_dram", (TOK, DIM), F32, kind="ExternalOutput").ap()
    build(nc, args, out)
    r = run_bass_kernel_spmd(nc, [arrays], core_ids=[0])
    return r.results[0]["out_0_dram"].reshape(1, TOK, DIM)
```

```python
from contextlib import ExitStack

import numpy as np

import concourse.bass as bass
from concourse import mybir

F32 = mybir.dt.float32
F32R = mybir.dt.float32r
BF16 = mybir.dt.bfloat16
I32 = mybir.dt.int32
ALU = mybir.AluOpType
ACT = mybir.ActivationFunctionType
AX = mybir.AxisListType

P = 128
TOK = 1024
DIM = 512
NT = TOK // P
KC = DIM // P
HALF = 512
EPS = 1e-5
FFN_COUNTERS = ("x_hi", "x_lo", "w_hi", "w_lo", "gate_done", "up_done", "gated", "product", "wd_hi", "wd_lo",
                "h_hi", "h_lo", "h_used", "dequantised")


class Chip:

    def __init__(self, nc, ctx):
        self.nc, self.ctx = nc, ctx
        self.x_tok = self.sb("x_tok", [P, NT, DIM], F32)
        self.x_feat = self.sb("x_feat", [P, KC, TOK], F32)
        self.ident = self.sb("ident", [P, P], F32)
        self.stats = self.sb("ln_stats", [P, NT, 6], F32)
        self.mean_var = self.sb("ln_mean_var", [P, NT, 2], F32)
        self.std = self.sb("ln_std", [P, NT], F32)
        self.rstd = self.sb("ln_rstd", [P, NT], F32)
        self.tail_sems = [self.sem(n) for n in Tail.NAMES]
        self.ffn_sems = [self.sem("ffn_" + n) for n in FFN_COUNTERS]
        self.ffn_loaded = [self.sem(f"ffn_loaded{i}") for i in range(2)]
        self.ffn_base = {n: 0 for n in FFN_COUNTERS}
        self.ffn_base["loaded"] = [0, 0]
        self.tails = self.ln_count = 0
        psum = ctx.enter_context(nc.psum_tensor("psum", [P, 8, 512], F32))
        self.bank = [psum[:, i, :] for i in range(8)]

    def sb(self, name, shape, dt, ctx=None):
        return (ctx or self.ctx).enter_context(self.nc.sbuf_tensor(name, shape, dt))

    def sem(self, name):
        return self.ctx.enter_context(self.nc.semaphore(name))


class Tail:

    NAMES = ("out_ready", "out_taken", "ln_step", "var_ready", "std_ready", "normed", "transposed", "feat_ready")

    def __init__(self, chip, out_bank, tr_bank, last=False):
        self.c, self.out_bank, self.tr_bank, self.last = chip, out_bank, tr_bank, last
        (self.out_ready, self.out_taken, self.ln_step, self.var_ready, self.std_ready, self.normed,
         self.transposed, self.feat_ready) = chip.tail_sems
        self.base = NT * chip.tails
        chip.tails += 1

    def dve(self, dve, t, bias=None):
        c, nc = self.c, self.c.nc
        row = c.x_tok[:, t, :]

        def step(ins):
            c.ln_count += 1
            ins.then_inc(self.ln_step, 1)
            dve.wait_ge(self.ln_step, c.ln_count)

        dve.wait_ge(self.out_ready, self.base + t + 1)
        if bias is None:
            nc.vector.tensor_tensor(row, row, self.out_bank[t % 2][:, :], ALU.add).then_inc(self.out_taken, 1)
            dve.wait_ge(self.out_taken, self.base + t + 1)
        else:
            nc.vector.tensor_tensor(row, row, self.out_bank[t % 2][:, :], ALU.add).then_inc(self.out_taken, 1)
            dve.wait_ge(self.out_taken, self.base + t + 1)
            step(nc.vector.tensor_tensor(row, row, bias[:, :], ALU.add))
        step(nc.vector.bn_stats(c.stats[:, t, :], row))
        nc.vector.bn_aggr(c.mean_var[:, t, :], c.stats[:, t, :]).then_inc(self.var_ready, 1)
        dve.wait_ge(self.std_ready, self.base + t + 1)
        step(nc.vector.reciprocal(c.rstd[:, t:t + 1], c.std[:, t:t + 1]))
        nc.vector.tensor_scalar(row, row, c.mean_var[:, t, 0:1], c.rstd[:, t:t + 1],
                                ALU.subtract, ALU.mult).then_inc(self.normed, 1)

    def act_std(self, act, t):
        c, nc = self.c, self.c.nc
        act.wait_ge(self.var_ready, self.base + t + 1)
        nc.scalar.activation(c.std[:, t:t + 1], c.mean_var[:, t, 1:2], ACT.Sqrt,
                             bias=c.eps[:, 0:1]).then_inc(self.std_ready, 1)

    def act_copy(self, act, t):
        c, nc = self.c, self.c.nc
        act.wait_ge(self.transposed, self.base + t + 1)
        src = self.tr_bank[t % 2][:, :].rearrange("p (k n) -> p k n", k=KC)
        nc.scalar.copy(c.x_feat[:, :, t * P:(t + 1) * P], src).then_inc(self.feat_ready, 1)

    def act(self, act):
        for t in range(NT):
            self.act_std(act, t)
            if t and not self.last:
                self.act_copy(act, t - 1)
        if not self.last:
            self.act_copy(act, NT - 1)
            act.wait_ge(self.feat_ready, self.base + NT)

    def pe(self, pe, t):
        c, nc = self.c, self.c.nc
        if self.last:
            return
        pe.wait_ge(self.normed, self.base + t + 1)
        if t + self.base >= 2:
            pe.wait_ge(self.feat_ready, self.base + t - 1)
        for k in range(KC):
            ins = nc.tensor.transpose(self.tr_bank[t % 2][:, k * P:(k + 1) * P],
                                      c.x_tok[:, t, k * P:(k + 1) * P], c.ident[:, :])
        ins.then_inc(self.transposed, 1)


def each_tile(eng, tiles, body):
    body(0, 0, True)
    body(1, 1, True)
    if tiles >= 4:
        with eng.Fori(1, tiles // 2) as i:
            body(2 * i, 0, False)
            body(2 * i + 1, 1, False)
    if tiles % 2:
        body(tiles - 1, 0, False)


def setup(c):
    nc = c.nc
    c.eps = c.sb("eps", [P, 1], F32)
    ready, zeroed = c.sem("const_ready"), c.sem("ident_zeroed")
    with nc.Block() as block:

        @block.gpsimd
        def _(pool):
            nc.gpsimd.memset(c.eps[:, :], EPS)
            nc.gpsimd.memset(c.ident[:, :], 0.0).then_inc(zeroed, 1)
            pool.wait_ge(zeroed, 1)
            nc.gpsimd.affine_select(out=c.ident[:, :], in_=c.ident[:, :], compare_op=ALU.not_equal, fill=1.0,
                                    base=0, pattern=[[-1, P]], channel_multiplier=1).then_inc(ready, 1)
            pool.wait_ge(ready, 1)


PASSES = ((0, 0), (0, 1), (1, 0))


class FfnFront:

    UP = 2 * KC * P

    def __init__(self, c, name, weights, zeros=None, scales=None, scale=None, down_too=True):
        self.c, self.scope, self.name = c, ExitStack(), name
        self.weights, self.zeros, self.scales, self.scale = weights, zeros, scales, scale
        self.down_too, self.tiles = down_too, weights.shape[0]
        self.width = self.UP + (DIM if down_too else 0)
        self.stage = c.sb(f"{name}_stage", [P, 2, self.width], F32, self.scope)
        self.raw = self.stage.bitcast(I32) if down_too else self.stage
        self.loaded = c.ffn_loaded
        if zeros is not None:
            self.z_int = c.sb(f"{name}_z_int", [P, self.width], I32, self.scope)
            self.s_all = c.sb(f"{name}_s_all", [P, self.width], F32, self.scope)
            self.zs_loaded = c.sem(f"{name}_zs_loaded")
        if scale is not None:
            self.sc = c.sb(f"{name}_sc", [P, 3], F32, self.scope)
            self.scale_loaded = c.sem(f"{name}_scale_loaded")

    def load_tile(self, sp, f, slot):
        sp.dma_start(self.raw[:, slot, :], self.weights[f]).then_inc(self.loaded[slot], 16)

    def load_zeros_scales(self, sp, f):
        sp.dma_start(self.z_int[:, :], self.zeros[f].partition_broadcast(P)).then_inc(self.zs_loaded, 16)
        sp.dma_start(self.s_all[:, :], self.scales[f].partition_broadcast(P)).then_inc(self.zs_loaded, 16)

    def load_first(self, sp):
        self.load_tile(sp, 0, 0)
        if self.zeros is not None:
            self.load_zeros_scales(sp, 0)
        if self.scale is not None:
            for i, one in enumerate(self.scale):
                sp.dma_start(self.sc[:, i:i + 1], one.partition_broadcast(P)).then_inc(self.scale_loaded, 16)
        self.load_tile(sp, 1, 1)


def swiglu(c, front, down=None, last=None, x_loaded=None, first_loads=None, extra_loads=None,
           extra_dve=None, extra_pe=None, extra_act=None):
    nc = c.nc
    name, tiles, quantised = front.name, front.tiles, front.down_too
    zeros, scale = front.zeros, front.scale
    up_width, width = front.UP, front.width
    per = -(-tiles // 2)
    groups = (range(0, per), range(per, tiles))
    with ExitStack() as own:
        def sb(n, shape, dt, scope=own):
            return c.sb(f"{name}_{n}", shape, dt, scope)

        def sem(n):
            return c.sem(f"{name}_{n}")

        stage, w_int = front.stage, front.raw
        with ExitStack() as up_stage:
            x = sb("x", [P, 2, KC, TOK], F32R, up_stage)
            w_up = sb("w_up", [P, 2, 2, up_width], F32R, up_stage)
            gate = sb("gate", [P, HALF], F32, up_stage)
        front.scope.close()
        if zeros is not None:
            z_int, s_all, zs_loaded = front.z_int, front.s_all, front.zs_loaded
        if scale is not None:
            sc, scale_loaded = front.sc, front.scale_loaded
        wd = sb("wd", [P, 2, tiles, DIM], F32R)
        part_h = sb("part_h", [P, 2, 2, per, P], F32R)
        up_size = (2 * KC * TOK + 4 * up_width + HALF + (2 if zeros is None else 4) * width + 3)
        down_size = 2 * tiles * DIM + 4 * per * P
        sb("above_both", [P, max(8, up_size - down_size + 64)], F32)
        w_down = sb("w_down", [P, tiles, DIM], F32)
        hidden = sb("hidden", [P, tiles, TOK], F32)
        g_bank, u_bank = c.bank[0:2], c.bank[2:4]
        tail = Tail(c, c.bank[4:6], c.bank[6:8], last is not None)
        base = c.ffn_base
        (x_hi, x_lo, w_hi, w_lo, gate_done, up_done, gated, product, wd_hi, wd_lo, h_hi, h_lo, h_used,
         dequantised) = c.ffn_sems
        loaded = c.ffn_loaded
        if not quantised:
            down_loaded = sem("down_loaded")
        if zeros is not None:
            centred, zs_used = sem("centred"), sem("zs_used")
        if last is not None:
            stored = sem("stored")

        def split_h(engine, t, g, part):
            src = hidden[:, groups[g].start:groups[g].stop, t * P:(t + 1) * P]
            n, u = len(groups[g]), 2 * t + g
            if part == 0:
                if t and g == 0:
                    engine.wait_ge(h_used, base["h_used"] + t)
                elif t:
                    engine.wait_ge(tail.out_ready, tail.base + t)
                nc.scalar.copy(part_h[:, g, 0, 0:n, :], src).then_inc(h_hi, 1)
            else:
                engine.wait_ge(h_hi, base["h_hi"] + u + 1)
                nc.vector.tensor_tensor(part_h[:, g, 1, 0:n, :], src, part_h[:, g, 0, 0:n, :].bitcast(F32),
                                        ALU.subtract).then_inc(h_lo, 1)

        def split_w_down(engine, g, part):
            for f in groups[g]:
                if part == 0:
                    nc.scalar.copy(wd[:, 0, f, :], w_down[:, f, :]).then_inc(wd_hi, 1)
                else:
                    engine.wait_ge(wd_hi, base["wd_hi"] + f + 1)
                    nc.vector.tensor_tensor(wd[:, 1, f, :], w_down[:, f, :], wd[:, 0, f, :].bitcast(F32),
                                            ALU.subtract).then_inc(wd_lo, 1)

        with nc.Block() as block:

            @block.sync
            def _(sp):
                if first_loads is not None:
                    first_loads(sp)
                    front.load_first(sp)

                def load(f, slot, first):
                    if not first:
                        sp.wait_ge(w_lo, base["w_lo"] + f - 1)
                        front.load_tile(sp, f, slot)
                    if zeros is not None and not (first and slot == 0):
                        sp.wait_ge(zs_used, f)
                        front.load_zeros_scales(sp, f)
                    if first and slot == 1 and extra_loads is not None:
                        extra_loads(sp)
                    if first and slot == 1 and not quantised:
                        sp.dma_start(w_down[:, :, :], down).then_inc(down_loaded, 16)

                each_tile(sp, tiles, load)
                if last is not None:
                    for t in range(NT):
                        sp.wait_ge(tail.normed, tail.base + t + 1)
                        sp.dma_start(last[t], c.x_tok[:, t, :]).then_inc(stored, 16)
                    sp.wait_ge(stored, 16 * NT)

            @block.tensor
            def _(pe):
                if extra_pe is not None:
                    extra_pe[0](pe)

                def gate_and_up(f, slot, first):
                    pe.wait_ge(w_lo, base["w_lo"] + f + 1)
                    for half in range(2):
                        if first and slot == 0:
                            pe.wait_ge(x_lo, base["x_lo"] + half + 1)
                        else:
                            pe.wait_ge(product, base["product"] + 2 * f + half - 1)
                        for which, bank, done in ((0, g_bank, gate_done), (1, u_bank, up_done)):
                            for k in range(KC):
                                at = (which * KC + k) * P
                                for n, (w_part, x_part) in enumerate(PASSES):
                                    ins = nc.tensor.matmul(bank[half][:, :], w_up[:, slot, w_part, at:at + P],
                                                           x[:, x_part, k, half * HALF:(half + 1) * HALF],
                                                           start=k == 0 and n == 0, stop=k == KC - 1 and n == 2)
                            ins.then_inc(done, 1)

                each_tile(pe, tiles, gate_and_up)
                for t in range(NT):
                    if t >= 2:
                        pe.wait_ge(tail.out_taken, tail.base + t - 1)
                    if extra_pe is not None:
                        extra_pe[1](pe, t, tail.out_bank[t % 2])
                    for g in range(2):
                        pe.wait_ge(h_lo, base["h_lo"] + 2 * t + g + 1)
                        for f in groups[g]:
                            if t == 0:
                                pe.wait_ge(wd_lo, base["wd_lo"] + f + 1)
                            for n, (h_part, w_part) in enumerate(PASSES):
                                ins = nc.tensor.matmul(tail.out_bank[t % 2][:, :],
                                                       part_h[:, g, h_part, f - groups[g].start, :],
                                                       wd[:, w_part, f, :],
                                                       start=f == 0 and n == 0 and extra_pe is None,
                                                       stop=f == tiles - 1 and n == 2)
                        ins.then_inc(h_used if g == 0 else tail.out_ready, 1)
                        if g == 0 and t:
                            tail.pe(pe, t - 1)
                tail.pe(pe, NT - 1)

            @block.scalar
            def _(act):
                def split_x(half):
                    cols = slice(half * HALF, (half + 1) * HALF)
                    if x_loaded is not None:
                        act.wait_ge(x_loaded[half], 16)
                    nc.scalar.copy(x[:, 0, :, cols], c.x_feat[:, :, cols]).then_inc(x_hi, 1)

                def split_w_up(f, slot, first):
                    if quantised:
                        act.wait_ge(dequantised, base["dequantised"] + f + 1)
                    else:
                        act.wait_ge(loaded[slot], base["loaded"][slot] + 8 * (f - slot) + 16)
                    if not first:
                        act.wait_ge(up_done, base["up_done"] + 2 * f - 2)
                    nc.scalar.copy(w_up[:, slot, 0, :], stage[:, slot, 0:up_width]).then_inc(w_hi, 1)

                def silu(f, fresh=False):
                    for half in range(2):
                        act.wait_ge(gate_done, base["gate_done"] + 2 * f + half + 1)
                        if not (fresh and half == 0):
                            act.wait_ge(product, base["product"] + 2 * f + half)
                        nc.scalar.activation(gate[:, :], g_bank[half][:, :], ACT.Silu).then_inc(gated, 1)

                def tile(f, slot, first):
                    silu(f, first and slot == 0)
                    split_w_up(f + 2, slot, False)

                split_x(0)
                split_w_up(0, 0, True)
                split_x(1)
                split_w_up(1, 1, True)
                if extra_act is not None:
                    extra_act(act)
                each_tile(act, tiles - 2, tile)
                silu(tiles - 2)
                silu(tiles - 1)
                act.wait_ge(product, base["product"] + 2 * tiles)
                if not quantised:
                    act.wait_ge(down_loaded, 16)
                for g in range(2):
                    split_h(act, 0, g, 0)
                    split_w_down(act, g, 0)
                split_h(act, 1, 0, 0)
                for t in range(NT):
                    if t + 1 < NT:
                        split_h(act, t + 1, 1, 0)
                    tail.act_std(act, t)
                    if t + 2 < NT:
                        split_h(act, t + 2, 0, 0)
                    if t and not tail.last:
                        tail.act_copy(act, t - 1)
                if not tail.last:
                    tail.act_copy(act, NT - 1)
                    act.wait_ge(tail.feat_ready, tail.base + NT)

            @block.vector
            def _(dve):
                if scale is not None:
                    dve.wait_ge(scale_loaded, 16 * len(scale))

                def split_w_up(f, slot, first):
                    if zeros is not None:
                        dve.wait_ge(loaded[slot], base["loaded"][slot] + 8 * (f - slot) + 16)
                        dve.wait_ge(zs_loaded, 32 * f + 32)
                        nc.vector.tensor_tensor(stage[:, slot, :], w_int[:, slot, :], z_int[:, :],
                                                ALU.subtract).then_inc(centred, 1)
                        dve.wait_ge(centred, f + 1)
                        nc.vector.tensor_tensor(stage[:, slot, 0:up_width], stage[:, slot, 0:up_width],
                                                s_all[:, 0:up_width], ALU.mult).then_inc(dequantised, 1)
                        nc.vector.tensor_tensor(w_down[:, f, :], stage[:, slot, up_width:width],
                                                s_all[:, up_width:width], ALU.mult).then_inc(zs_used, 1)
                    elif quantised:
                        dve.wait_ge(loaded[slot], base["loaded"][slot] + 8 * (f - slot) + 16)
                        for i in range(2):
                            at = slice(i * KC * P, (i + 1) * KC * P)
                            ins = nc.vector.tensor_scalar(stage[:, slot, at], w_int[:, slot, at], sc[:, i:i + 1],
                                                          None, ALU.mult)
                        ins.then_inc(dequantised, 1)
                        nc.vector.tensor_scalar(w_down[:, f, :], w_int[:, slot, up_width:width], sc[:, 2:3], None,
                                                ALU.mult)
                    dve.wait_ge(w_hi, base["w_hi"] + f + 1)
                    nc.vector.tensor_tensor(w_up[:, slot, 1, :], stage[:, slot, 0:up_width],
                                            w_up[:, slot, 0, :].bitcast(F32), ALU.subtract).then_inc(w_lo, 1)

                def multiply(f):
                    for half in range(2):
                        dve.wait_ge(gated, base["gated"] + 2 * f + half + 1)
                        dve.wait_ge(up_done, base["up_done"] + 2 * f + half + 1)
                        nc.vector.tensor_tensor(hidden[:, f, half * HALF:(half + 1) * HALF], gate[:, :],
                                                u_bank[half][:, :], ALU.mult).then_inc(product, 1)

                def tile(f, slot, first):
                    multiply(f)
                    split_w_up(f + 2, slot, False)

                split_w_up(0, 0, True)
                for half in range(2):
                    dve.wait_ge(x_hi, base["x_hi"] + half + 1)
                    cols = slice(half * HALF, (half + 1) * HALF)
                    nc.vector.tensor_tensor(x[:, 1, :, cols], c.x_feat[:, :, cols], x[:, 0, :, cols].bitcast(F32),
                                            ALU.subtract).then_inc(x_lo, 1)
                split_w_up(1, 1, True)
                if extra_dve is not None:
                    extra_dve(dve)
                each_tile(dve, tiles - 2, tile)
                multiply(tiles - 2)
                multiply(tiles - 1)
                for g in range(2):
                    split_h(dve, 0, g, 1)
                    split_w_down(dve, g, 1)
                split_h(dve, 1, 0, 1)
                for t in range(NT):
                    if t + 1 < NT:
                        split_h(dve, t + 1, 1, 1)
                    tail.dve(dve, t)
                    if t + 2 < NT:
                        split_h(dve, t + 2, 0, 1)

    for counter, times in (("x_hi", 2), ("x_lo", 2), ("w_hi", tiles), ("w_lo", tiles), ("gate_done", 2 * tiles),
                           ("up_done", 2 * tiles), ("gated", 2 * tiles), ("product", 2 * tiles),
                           ("wd_hi", tiles), ("wd_lo", tiles), ("h_hi", 2 * NT), ("h_lo", 2 * NT),
                           ("h_used", NT), ("dequantised", tiles if quantised else 0)):
        base[counter] += times
    for slot in range(2):
        base["loaded"][slot] += 16 * len(range(slot, tiles, 2))


def gradient_ffn(c, a):
    nc = c.nc
    G, GRAD_ORDER_MIN, THD = 6, 4, 2.5
    with ExitStack() as own:
        def sb(n, shape):
            return c.sb(f"series_{n}", shape, F32, own)

        with ExitStack() as before_terms:
            w_proj = c.sb("series_w_proj", [P, 2, KC, P], F32, before_terms)
        terms = sb("terms", [P, G + 1, TOK])
        w_fuse = sb("w_fuse", [P, G + 1, DIM])
        delta, keep = sb("delta", [P, TOK]), sb("keep", [P, TOK])
        point, disc = sb("point", [P, 1]), sb("disc", [P, G])
        diff, ratio = sb("diff", [P, G]), sb("ratio", [P, G])
        proj_loaded, small_loaded = c.sem("series_proj_loaded"), c.sem("series_small_loaded")
        fuse_loaded, projected = c.sem("series_fuse_loaded"), c.sem("series_projected")
        diff_ready, ratio_ready = c.sem("series_diff_ready"), c.sem("series_ratio_ready")
        step, tok_loaded = c.sem("series_step"), c.sem("x_tok_loaded")
        x_loaded = [c.sem(f"x_loaded{half}") for half in range(2)]

        def stream(sp):
            sp.dma_start(w_proj[:, :, :, :], a["L0_proj"]).then_inc(proj_loaded, 16)
            for half in range(2):
                cols = slice(half * HALF, (half + 1) * HALF)
                sp.dma_start(c.x_feat[:, :, cols], a["x_feat"].rearrange("(k p) n -> p k n", p=P)[:, :, cols])\
                    .then_inc(x_loaded[half], 16)

        def loads(sp):
            sp.dma_start(point[:, :], a["L0_point"]).then_inc(small_loaded, 16)
            sp.dma_start(disc[:, :], a["L0_disc"].partition_broadcast(P)).then_inc(small_loaded, 16)
            sp.dma_start(w_fuse[:, :, :], a["L0_fuse"]).then_inc(fuse_loaded, 16)
            sp.dma_start(c.x_tok[:, :, :], a["x_tok"].rearrange("(t p) n -> p t n", p=P)).then_inc(tok_loaded, 16)

        def project(pe):
            pe.wait_ge(proj_loaded, 16)
            for half in range(2):
                pe.wait_ge(x_loaded[half], 16)
                for which in range(2):
                    for k in range(KC):
                        ins = nc.tensor.matmul(c.bank[4 + 2 * which + half][:, :], w_proj[:, which, k, :],
                                               c.x_feat[:, k, half * HALF:(half + 1) * HALF],
                                               start=k == 0, stop=k == KC - 1)
            ins.then_inc(projected, 1)

        def series(pe, t, bank):
            if t == 0:
                pe.wait_ge(fuse_loaded, 16)
                pe.wait_ge(step, G + 5)
            for m in range(G + 1):
                nc.tensor.matmul(bank[:, :], terms[:, m, t * P:(t + 1) * P], w_fuse[:, m, :],
                                 start=m == 0, stop=False)

        def ratios(act):
            act.wait_ge(diff_ready, 2)
            nc.scalar.activation(ratio[:, :], diff[:, :], ACT.Exp).then_inc(ratio_ready, 1)

        def make_terms(dve):
            count = 0

            def then(ins):
                nonlocal count
                count += 1
                ins.then_inc(step, 1)
                dve.wait_ge(step, count)

            dve.wait_ge(small_loaded, 32)
            nc.vector.tensor_scalar(diff[:, 0:1], disc[:, 0:1], -1.0, None, ALU.mult).then_inc(diff_ready, 1)
            nc.vector.tensor_tensor(diff[:, 1:G], disc[:, 0:G - 1], disc[:, 1:G], ALU.subtract).then_inc(diff_ready, 1)
            dve.wait_ge(projected, 1)
            for half in range(2):
                cols = slice(half * HALF, (half + 1) * HALF)
                nc.vector.tensor_copy(terms[:, 0, cols], c.bank[4 + half][:, :])
                then(nc.vector.tensor_scalar(delta[:, cols], c.bank[6 + half][:, :], point[:, 0:1], None,
                                             ALU.subtract))
            then(nc.vector.tensor_scalar(keep[:, :], delta[:, :], THD, None, ALU.is_le))
            then(nc.vector.scalar_tensor_tensor(keep[:, :], delta[:, :], -THD, keep[:, :], ALU.is_ge, ALU.mult))
            dve.wait_ge(ratio_ready, 1)
            for m in range(1, G + 1):
                then(nc.vector.scalar_tensor_tensor(terms[:, m, :], terms[:, m - 1, :], ratio[:, m - 1:m],
                                                    delta[:, :], ALU.mult, ALU.mult))
                if m == GRAD_ORDER_MIN + 1:
                    then(nc.vector.tensor_tensor(terms[:, m, :], terms[:, m, :], keep[:, :], ALU.mult))
            dve.wait_ge(tok_loaded, 16)

        front = FfnFront(c, "L0_attn", a["L0_w"], down_too=False)
        swiglu(c, front, down=a["L0_down"], x_loaded=x_loaded, first_loads=stream,
               extra_loads=loads, extra_dve=make_terms,
               extra_pe=(project, series), extra_act=ratios)


def product_tiles(c, pe, tail, w, t, chunks=KC):
    nc = c.nc
    if t + tail.base >= 2:
        pe.wait_ge(tail.out_taken, tail.base + t - 1)
    for k in range(chunks):
        ins = nc.tensor.matmul(tail.out_bank[t % 2][:, :], c.x_feat[:, k, t * P:(t + 1) * P], w[:, k, :],
                               start=k == 0, stop=k == chunks - 1)
    ins.then_inc(tail.out_ready, 1)


def lora_then_single_key(c, a, load_ahead):
    nc = c.nc
    E, R, K = 8, 64, P
    RC = E * R // P
    KV, PER, SLOTS = 8, 4, 3
    with ExitStack() as own:
        def sb(n, shape):
            return c.sb(f"lora_{n}", shape, F32, own)

        def sem(n):
            return c.sem(f"lora_{n}")

        w_org, w_eff = sb("w_org", [P, KC, DIM]), sb("w_eff", [P, KC, DIM])
        down, up, up_c = sb("down", [P, RC, DIM]), sb("up", [P, RC, DIM]), sb("up_c", [P, RC, DIM])
        wq, keys = sb("wq", [P, KC, K]), sb("keys", [P, E])
        mean, q, q_wide = sb("mean", [P, KC]), sb("q", [P, 1]), sb("q_wide", [P, P])
        top, neg, e, total, inv, coeff = (sb("top", [P, 1]), sb("neg", [P, 1]), sb("e", [P, E]),
                                          sb("total", [P, 1]), sb("inv", [P, 1]), sb("coeff", [P, E]))
        ones = sb("ones", [P, P])
        wv, wo = sb("wv", [P, KV, DIM]), sb("wo", [P, SLOTS, PER, DIM])
        pair, wo_sum, w_values = sb("pair", [P, 2, DIM]), sb("wo_sum", [P, KV, DIM]), sb("w_values", [P, KC, DIM])
        tail = Tail(c, c.bank[4:6], c.bank[6:8])
        tail_values = Tail(c, c.bank[4:6], c.bank[6:8])
        wv_loaded, wo_loaded = sem("wv_loaded"), [sem(f"wo_loaded{g}") for g in range(SLOTS)]
        paired, summed, merged, values_ready = sem("paired"), sem("summed"), sem("merged"), sem("values_ready")
        w_loaded, org_loaded, q_loaded = sem("w_loaded"), sem("org_loaded"), sem("q_loaded")
        ones_ready, mean_ready, q_ready, wide_ready = sem("ones"), sem("mean"), sem("q"), sem("wide")
        scores_ready, top_ready, e_ready, coeff_ready = sem("scores"), sem("top"), sem("e"), sem("coeff")
        delta_ready, eff_ready, step = sem("delta"), sem("eff"), sem("step")

        with nc.Block() as block:

            @block.sync
            def _(sp):
                sp.dma_start(wq[:, :, :], a["L0_wq"]).then_inc(q_loaded, 16)
                sp.dma_start(keys[:, :], a["L0_keys"]).then_inc(q_loaded, 16)
                sp.dma_start(up[:, :, :], a["L0_up"]).then_inc(w_loaded, 16)
                sp.dma_start(down[:, :, :], a["L0_lora_down"]).then_inc(w_loaded, 16)
                c.rot.load(sp, a)
                sp.dma_start(w_org[:, :, :], a["L0_org"]).then_inc(org_loaded, 16)
                sp.dma_start(wv[:, :, :], a["L1_wv"]).then_inc(wv_loaded, 16)
                for g in range(KV):
                    if g >= SLOTS:
                        sp.wait_ge(paired, g - SLOTS + 1)
                    sp.dma_start(wo[:, g % SLOTS, :, :], a["L1_wo"][g]).then_inc(wo_loaded[g % SLOTS], 16)
                load_ahead(sp)

            @block.gpsimd
            def _(pool):
                nc.gpsimd.memset(ones[:, :], 1.0).then_inc(ones_ready, 1)
                c.rot.pool(pool)

            @block.tensor
            def _(pe):
                pe.wait_ge(q_loaded, 32)
                pe.wait_ge(mean_ready, 1)
                for k in range(KC):
                    ins = nc.tensor.matmul(c.bank[0][:, 0:1], wq[:, k, :], mean[:, k:k + 1],
                                           start=k == 0, stop=k == KC - 1)
                ins.then_inc(q_ready, 1)
                pe.wait_ge(wide_ready, 1)
                nc.tensor.matmul(c.bank[1][:, 0:E], q_wide[:, :], keys[:, :], start=True, stop=True)\
                    .then_inc(scores_ready, 1)
                pe.wait_ge(w_loaded, 32)
                pe.wait_ge(coeff_ready, 1)
                for i in range(KC):
                    for r in range(RC):
                        ins = nc.tensor.matmul(c.bank[i][:, :], down[:, r, i * P:(i + 1) * P], up_c[:, r, :],
                                               start=r == 0, stop=r == RC - 1)
                    ins.then_inc(delta_ready, 1)
                pe.wait_ge(eff_ready, KC)
                for t in range(NT):
                    product_tiles(c, pe, tail, w_eff, t)
                    if t:
                        tail.pe(pe, t - 1)
                pe.wait_ge(wv_loaded, 16)
                for g in range(KV):
                    pe.wait_ge(summed, g + 1)
                    for i in range(KC):
                        ins = nc.tensor.matmul(c.bank[i][:, :], wv[:, g, i * P:(i + 1) * P], wo_sum[:, g, :],
                                               start=g == 0, stop=g == KV - 1)
                        if g == KV - 1:
                            ins.then_inc(merged, 1)
                    if g == 1:
                        tail.pe(pe, NT - 1)
                pe.wait_ge(tail.feat_ready, tail.base + NT)
                for t in range(NT):
                    if t == 0:
                        pe.wait_ge(values_ready, KC)
                    product_tiles(c, pe, tail_values, w_values, t)
                    if t:
                        tail_values.pe(pe, t - 1)
                tail_values.pe(pe, NT - 1)

            @block.scalar
            def _(act):
                act.wait_ge(top_ready, 1)
                nc.scalar.activation(e[:, :], c.bank[1][:, 0:E], ACT.Exp, bias=neg[:, 0:1], scale=K ** -0.5)\
                    .then_inc(e_ready, 1)
                c.rot.act(act)
                tail.act(act)
                tail_values.act(act)

            @block.vector
            def _(dve):
                count = 0

                def then(ins):
                    nonlocal count
                    count += 1
                    ins.then_inc(step, 1)
                    dve.wait_ge(step, count)

                then(nc.vector.tensor_reduce(mean[:, :], c.x_feat[:, :, :], AX.X, ALU.add))
                nc.vector.tensor_scalar(mean[:, :], mean[:, :], 1.0 / TOK, None, ALU.mult).then_inc(mean_ready, 1)
                dve.wait_ge(q_ready, 1)
                then(nc.vector.tensor_copy(q[:, :], c.bank[0][:, 0:1]))
                dve.wait_ge(ones_ready, 1)
                nc.vector.tensor_scalar(q_wide[:, :], ones[:, :], q[:, 0:1], None, ALU.mult).then_inc(wide_ready, 1)
                dve.wait_ge(scores_ready, 1)
                then(nc.vector.tensor_reduce(top[:, :], c.bank[1][:, 0:E], AX.X, ALU.max))
                nc.vector.tensor_scalar(neg[:, :], top[:, :], -(K ** -0.5), None, ALU.mult).then_inc(top_ready, 1)
                dve.wait_ge(e_ready, 1)
                then(nc.vector.tensor_reduce(total[:, :], e[:, :], AX.X, ALU.add))
                then(nc.vector.reciprocal(inv[:, :], total[:, :]))
                then(nc.vector.tensor_scalar(coeff[:, :], e[:, :], inv[:, 0:1], None, ALU.mult))
                dve.wait_ge(w_loaded, 32)
                for r in range(RC):
                    for h in range(P // R):
                        rows, expert = slice(h * R, (h + 1) * R), r * (P // R) + h
                        ins = nc.vector.tensor_scalar(up_c[rows, r, :], up[rows, r, :],
                                                      coeff[rows, expert:expert + 1], None, ALU.mult)
                ins.then_inc(coeff_ready, 1)
                c.rot.dve(dve)
                dve.wait_ge(org_loaded, 16)
                for i in range(KC):
                    dve.wait_ge(delta_ready, i + 1)
                    nc.vector.tensor_tensor(w_eff[:, i, :], w_org[:, i, :], c.bank[i][:, :], ALU.add)\
                        .then_inc(eff_ready, 1)
                for t in range(NT):
                    tail.dve(dve, t)
                    dve.wait_ge(wo_loaded[t % SLOTS], 16 * (t // SLOTS + 1))
                    if t:
                        dve.wait_ge(summed, t)
                    nc.vector.tensor_tensor(pair[:, :, :], wo[:, t % SLOTS, 0:2, :], wo[:, t % SLOTS, 2:4, :],
                                            ALU.add).then_inc(paired, 1)
                    dve.wait_ge(paired, t + 1)
                    nc.vector.tensor_tensor(wo_sum[:, t, :], pair[:, 0, :], pair[:, 1, :], ALU.add)\
                        .then_inc(summed, 1)
                for i in range(KC):
                    dve.wait_ge(merged, i + 1)
                    nc.vector.tensor_copy(w_values[:, i, :], c.bank[i][:, :]).then_inc(values_ready, 1)
                for t in range(NT):
                    tail_values.dve(dve, t)


class TwoLorasWeights:
    def __init__(self, c, own):
        self.base, self.bias = c.sb("two_base", [P, KC, DIM], F32, own), c.sb("two_bias", [P, DIM], F32, own)
        self.low, self.high = c.sb("two_low", [64, 2, DIM], F32, own), c.sb("two_high", [64, 2, DIM], F32, own)
        self.loaded, self.base_loaded = c.sem("two_loaded"), c.sem("two_base_loaded")

    def load(self, sp, a):
        sp.dma_start(self.low[:, :, :], a["L2_low"]).then_inc(self.loaded, 16)
        sp.dma_start(self.high[:, :, :], a["L2_high"]).then_inc(self.loaded, 16)
        sp.dma_start(self.base[:, :, :], a["L2_base"]).then_inc(self.base_loaded, 16)
        sp.dma_start(self.bias[:, :], a["L2_bias"].partition_broadcast(P)).then_inc(self.base_loaded, 16)


def two_loras(c, weights):
    nc = c.nc
    R, SCALING = 64, 16 / 64
    with ExitStack() as own:
        def sb(n, shape):
            return c.sb(f"two_{n}", shape, F32, own)

        def sem(n):
            return c.sem(f"two_{n}")

        base, bias, low, high = weights.base, weights.bias, weights.low, weights.high
        w_eff = sb("w_eff", [P, KC, DIM])
        low_sum, high_sum = sb("low_sum", [R, DIM]), sb("high_sum", [R, DIM])
        tail = Tail(c, c.bank[4:6], c.bank[6:8])
        loaded, base_loaded = weights.loaded, weights.base_loaded
        summed, delta_ready, eff_ready = sem("summed"), sem("delta"), sem("eff")

        with nc.Block() as block:

            @block.tensor
            def _(pe):
                pe.wait_ge(summed, 2)
                for i in range(KC):
                    nc.tensor.matmul(c.bank[i][:, :], low_sum[:, i * P:(i + 1) * P], high_sum[:, :],
                                     start=True, stop=True).then_inc(delta_ready, 1)
                pe.wait_ge(eff_ready, KC)
                for t in range(NT):
                    product_tiles(c, pe, tail, w_eff, t)
                    if t:
                        tail.pe(pe, t - 1)
                tail.pe(pe, NT - 1)

            @block.scalar
            def _(act):
                tail.act(act)

            @block.vector
            def _(dve):
                dve.wait_ge(loaded, 32)
                for pair, total in ((low, low_sum), (high, high_sum)):
                    nc.vector.tensor_tensor(total[:, :], pair[:, 0, :], pair[:, 1, :], ALU.add).then_inc(summed, 1)
                dve.wait_ge(base_loaded, 32)
                for i in range(KC):
                    dve.wait_ge(delta_ready, i + 1)
                    nc.vector.scalar_tensor_tensor(w_eff[:, i, :], c.bank[i][:, :], SCALING, base[:, i, :],
                                                   ALU.mult, ALU.add).then_inc(eff_ready, 1)
                for t in range(NT):
                    tail.dve(dve, t, bias)


C_DIM, C_DEPTH, C_FF = 64, 4, 256


class Rotation:

    LEVELS = 10

    def __init__(self, c):
        self.c = c
        self.wave = c.sb("wave", [P, C_DEPTH, TOK], F32)
        self.decay = c.sb("decay", [P, C_DEPTH], F32)
        self.start = c.sb("scan_start", [P, C_DEPTH], F32)
        self.half_ready = c.sem("rot_done")

    def scratch(self, own):
        c = self.c
        self.other = c.sb("rot_other", [P, C_DEPTH, TOK // 2], F32, own)
        self.tmp = c.sb("rot_tmp", [P, C_DEPTH, TOK // 2], F32, own)
        self.par = c.sb("rot_par", [P, 4, C_DEPTH], F32, own)
        self.turn = c.sb("rot_turn", [P, self.LEVELS, 2, C_DEPTH], F32, own)
        self.small = c.sb("rot_small", [P, 8, C_DEPTH], F32, own)
        self.sign = c.sb("rot_sign", [P, 1], F32, own)
        self.loaded, self.step = c.sem("rot_loaded"), c.sem("rot_step")
        self.size_ready, self.root_ready = c.sem("rot_size"), c.sem("rot_root")
        self.decay_ready = c.sem("rot_decay")
        self.turns_ready, self.turn_step = c.sem("rot_turns"), c.sem("rot_turn_step")

    def load(self, sp, a):
        sp.dma_start(self.par[:, :, :], a["L2_par"]).then_inc(self.loaded, 16)

    def act(self, act):
        nc, small = self.c.nc, self.small
        act.wait_ge(self.size_ready, 1)
        nc.scalar.activation(small[:, 5, :], small[:, 4, :], ACT.Sqrt).then_inc(self.root_ready, 1)
        act.wait_ge(self.size_ready, 2)
        nc.scalar.activation(self.decay[:, :], small[:, 6, :], ACT.Tanh).then_inc(self.decay_ready, 1)

    def dve(self, dve):
        nc, small, par = self.c.nc, self.small, self.par
        count = 0

        def then(ins):
            nonlocal count
            count += 1
            ins.then_inc(self.turn_step, 1)
            dve.wait_ge(self.turn_step, count)

        tt, ts, stt = nc.vector.tensor_tensor, nc.vector.tensor_scalar, nc.vector.scalar_tensor_tensor
        big, zero, re, im, size, root, length = (small[:, i, :] for i in range(7))
        dve.wait_ge(self.loaded, 16)
        then(stt(re, par[:, 0, :], -1.0, par[:, 0, :], ALU.mult, ALU.max))
        then(stt(im, par[:, 1, :], -1.0, par[:, 1, :], ALU.mult, ALU.max))
        then(tt(big, re, im, ALU.max))
        then(ts(zero, big, 0.0, None, ALU.is_equal))
        then(tt(length, big, zero, ALU.add))
        then(nc.vector.reciprocal(size, length))
        then(tt(re, par[:, 0, :], size, ALU.mult))
        then(tt(im, par[:, 1, :], size, ALU.mult))
        then(tt(re, re, zero, ALU.add))
        then(tt(size, re, re, ALU.mult))
        then(tt(root, im, im, ALU.mult))
        tt(size, size, root, ALU.add).then_inc(self.size_ready, 1)
        dve.wait_ge(self.root_ready, 1)
        then(tt(length, big, root, ALU.mult))
        nc.vector.tensor_copy(length, length).then_inc(self.size_ready, 1)
        then(nc.vector.reciprocal(size, root))
        then(tt(re, re, size, ALU.mult))
        then(tt(im, im, size, ALU.mult))
        then(tt(size, re, re, ALU.mult))
        then(tt(root, im, im, ALU.mult))
        then(tt(size, size, root, ALU.add))
        then(ts(size, size, -0.5, 1.5, ALU.mult, ALU.add))
        turn = self.turn
        then(tt(turn[:, 0, 0, :], re, size, ALU.mult))
        then(tt(turn[:, 0, 1, :], im, size, ALU.mult))
        for n in range(1, self.LEVELS):
            cos, sin = turn[:, n - 1, 0, :], turn[:, n - 1, 1, :]
            then(tt(re, cos, cos, ALU.mult))
            then(tt(im, sin, sin, ALU.mult))
            then(tt(turn[:, n, 0, :], re, im, ALU.subtract))
            then(stt(turn[:, n, 1, :], cos, 2.0, sin, ALU.mult, ALU.mult))
        nc.vector.tensor_copy(re, re).then_inc(self.turns_ready, 1)

    def pool(self, pool):
        nc, wave, other, tmp = self.c.nc, self.wave, self.other, self.tmp
        count = 0

        def then(ins):
            nonlocal count
            count += 1
            ins.then_inc(self.step, 1)
            pool.wait_ge(self.step, count)

        mul = nc.gpsimd.tensor_tensor
        for half, (re, im, sign) in enumerate(((1.0, 0.0, 1.0), (0.0, 1.0, -1.0))):
            rows = slice(half * C_DIM, (half + 1) * C_DIM)
            nc.gpsimd.memset(wave[rows, :, 0:1], re)
            nc.gpsimd.memset(other[rows, :, 0:1], im)
            then(nc.gpsimd.memset(self.sign[rows, :], sign))
        pool.wait_ge(self.turns_ready, 1)
        for level in range(self.LEVELS):
            n = 1 << level
            cos, sin = (self.turn[:, level, i, :].unsqueeze(2).to_broadcast([P, C_DEPTH, n]) for i in range(2))
            src, dst = slice(0, n), slice(n, 2 * n)
            then(mul(tmp[:, :, src], other[:, :, src], sin, ALU.mult))
            then(mul(wave[:, :, dst], wave[:, :, src], cos, ALU.mult))
            then(mul(wave[:, :, dst], wave[:, :, dst], tmp[:, :, src], ALU.subtract))
            if level < self.LEVELS - 1:
                then(mul(tmp[:, :, src], wave[:, :, src], sin, ALU.mult))
                then(mul(other[:, :, dst], other[:, :, src], cos, ALU.mult))
                then(mul(other[:, :, dst], other[:, :, dst], tmp[:, :, src], ALU.add))
        pool.wait_ge(self.loaded, 16)
        then(mul(tmp[:, :, 0], self.par[:, 2, :], wave[:, :, 1], ALU.mult))
        then(mul(tmp[:, :, 1], self.par[:, 3, :], other[:, :, 1], ALU.mult))
        then(mul(tmp[:, :, 0], tmp[:, :, 0], tmp[:, :, 1], ALU.subtract))
        nc.gpsimd.tensor_scalar(self.start[:, :], tmp[:, :, 0], self.sign[:, 0:1], None, ALU.mult)\
            .then_inc(self.half_ready, 1)


def conv_stack(c, a, load_ahead):
    nc, rot = c.nc, c.rot
    FT = C_FF // P
    LOW = C_DIM
    ONE = 96
    with ExitStack() as own:
        def sb(n, shape):
            return c.sb(f"conv_{n}", shape, F32, own)

        def sem(n):
            return c.sem(f"conv_{n}")

        w_in, w_out = sb("w_in", [P, KC, LOW]), sb("w_out", [ONE + 1, DIM])
        w1_all, w2 = sb("w1_all", [ONE + 1, C_DEPTH, C_FF]), sb("w2", [P, C_DEPTH, FT, LOW])
        w1 = sb("w1", [ONE + 1, C_FF])
        cols, col, last_cols = sb("cols", [P, C_DEPTH, 4]), sb("col", [P, 4]), sb("last_cols", [LOW, 2])
        rows = sb("rows", [P, 2 * C_DEPTH + 1, LOW])
        fold = sb("fold", [P, LOW])
        fold_sc = sb("fold_sc", [P, C_DEPTH, LOW])
        h, centred, square = sb("h", [P, NT, LOW]), sb("centred", [P, NT, LOW]), sb("square", [P, NT, LOW])
        twice = sb("twice", [P, NT, 2, LOW])
        total, mean, var, rstd = sb("total", [P, NT]), sb("mean", [P, NT]), sb("var", [P, NT]), sb("rstd", [P, NT])
        power = sb("power", [P, NT])
        y, turned, state, back = sb("y", [P, TOK]), sb("turned", [P, TOK]), sb("state", [P, TOK]), sb("back", [P, TOK])
        normed2, hidden = sb("normed2", [ONE + 1, TOK]), sb("hidden", [P, FT, TOK])
        tail = Tail(c, c.bank[4:6], c.bank[6:8])
        tr_bank, half_bank, ff_bank = c.bank[0:2], (c.bank[2], c.bank[7]), c.bank[3:7]
        HT = NT // 2

        in_loaded, loaded, const = sem("in_loaded"), sem("loaded"), sem("const")
        step, h_in = sem("step"), sem("h_in")
        var_ready, rstd_ready = sem("var_ready"), sem("rstd_ready")
        normed, turned_up, y_ready = sem("normed"), sem("transposed"), sem("y_ready")
        back_ready, conv_ready = sem("back_ready"), sem("conv_ready")
        w1_ready, ff_ready, hidden_ready, mlp_ready = sem("w1_ready"), sem("ff_ready"), sem("hidden"), sem("mlp")
        n2_ready, col_ready = sem("n2_ready"), sem("col_ready")
        LOADS = 16 * 8

        with nc.Block() as block:

            @block.sync
            def _(sp):
                sp.dma_start(w_in[:, :, :], a["C_in"]).then_inc(in_loaded, 16)
                for dst, src in ((w_out, "C_out"), (w1_all, "C_w1"), (w2, "C_w2"), (cols, "C_cols"),
                                 (last_cols, "C_last")):
                    sp.dma_start(dst[:], a[src]).then_inc(loaded, 16)
                for i, src in enumerate(("C_b2", "C_sc")):
                    part = rows[:, i * C_DEPTH:(i + 1) * C_DEPTH, :]
                    sp.dma_start(part, a[src].partition_broadcast(P)).then_inc(loaded, 16)
                sp.dma_start(rows[:, 2 * C_DEPTH, :], a["C_bin"].partition_broadcast(P)).then_inc(loaded, 16)
                load_ahead(sp)

            @block.gpsimd
            def _(pool):
                nc.gpsimd.memset(power[:, :], -0.5).then_inc(const, 1)
                pool.wait_ge(const, 1)
                nc.gpsimd.memset(normed2[LOW:ONE + 1, :], 0.0).then_inc(const, 1)
                pool.wait_ge(const, 2)
                nc.gpsimd.memset(fold[:, :], 0.0).then_inc(const, 1)
                pool.wait_ge(const, 3)
                nc.gpsimd.memset(normed2[ONE:ONE + 1, :], 1.0).then_inc(const, 1)
                pool.wait_ge(const, 4)
                nc.gpsimd.affine_select(out=fold[:, :], in_=fold[:, :], compare_op=ALU.not_equal, fill=1.0,
                                        base=0, pattern=[[-1, LOW]], channel_multiplier=1).then_inc(const, 1)
                pool.wait_ge(const, 5)
                nc.gpsimd.affine_select(out=fold[:, :], in_=fold[:, :], compare_op=ALU.not_equal, fill=1.0,
                                        base=-LOW, pattern=[[-1, LOW]], channel_multiplier=1).then_inc(const, 1)
                pool.wait_ge(const, 6)
                pool.wait_ge(loaded, LOADS)
                for i in range(C_DEPTH):
                    ins = nc.gpsimd.tensor_tensor(fold_sc[:, i, :], fold[:, :], rows[:, C_DEPTH + i, :], ALU.mult)
                ins.then_inc(const, 1)

                def root(n):
                    for half in range(2):
                        tiles = slice(half * HT, (half + 1) * HT)
                        pool.wait_ge(var_ready, 2 * n + half + 1)
                        nc.gpsimd.tensor_tensor(rstd[:, tiles], var[:, tiles], power[:, tiles], ALU.pow)\
                            .then_inc(rstd_ready, 1)

                def prepare(i, first):
                    if not first:
                        pool.wait_ge(ff_ready, 4 * i)
                    nc.gpsimd.tensor_copy(w1[:, :], w1_all[:, i, :]).then_inc(w1_ready, 1)
                    if not first:
                        pool.wait_ge(hidden_ready, 4 * i)
                    nc.gpsimd.tensor_copy(col[:, :], cols[:, i, :]).then_inc(col_ready, 1)
                    root(2 * i)
                    root(2 * i + 1)

                prepare(0, True)
                with pool.Fori(1, C_DEPTH) as i:
                    prepare(i, False)
                root(2 * C_DEPTH)

            @block.tensor
            def _(pe):
                pe.wait_ge(in_loaded, 16)
                for t in range(NT):
                    for k in range(KC):
                        ins = nc.tensor.matmul(half_bank[t // HT][:, t % HT * LOW:(t % HT + 1) * LOW],
                                               c.x_feat[:, k, t * P:(t + 1) * P], w_in[:, k, :],
                                               start=k == 0, stop=k == KC - 1)
                ins.then_inc(h_in, 1)

                def transposes(n):
                    for half in range(2):
                        pe.wait_ge(normed, 2 * n + half + 1)
                        for t in range(NT // 2):
                            ins = nc.tensor.transpose(tr_bank[half][:, t * P:(t + 1) * P],
                                                      twice[:, half * NT // 2 + t, :, :]
                                                      .rearrange("p a d -> p (a d)"), c.ident[:, :])
                        ins.then_inc(turned_up, 1)

                def layer(i):
                    transposes(2 * i)
                    for half in range(2):
                        pe.wait_ge(back_ready, 2 * i + half + 1)
                        for t in range(half * NT // 2, (half + 1) * NT // 2):
                            ins = nc.tensor.matmul(half_bank[half][:, t % HT * LOW:(t % HT + 1) * LOW],
                                                   back[:, t * P:(t + 1) * P], fold_sc[:, i, :],
                                                   start=True, stop=True)
                        ins.then_inc(conv_ready, 1)
                    transposes(2 * i + 1)
                    pe.wait_ge(w1_ready, i + 1)
                    for half in range(2):
                        pe.wait_ge(n2_ready, 2 * i + half + 1)
                        for f in range(FT):
                            nc.tensor.matmul(ff_bank[2 * half + f][:, :], w1[:, f * P:(f + 1) * P],
                                             normed2[:, half * HALF:(half + 1) * HALF],
                                             start=True, stop=True).then_inc(ff_ready, 1)
                    for half in range(2):
                        pe.wait_ge(hidden_ready, 4 * i + 2 * half + 2)
                        for t in range(half * NT // 2, (half + 1) * NT // 2):
                            for f in range(FT):
                                ins = nc.tensor.matmul(half_bank[half][:, t % HT * LOW:(t % HT + 1) * LOW],
                                                       hidden[:, f, t * P:(t + 1) * P], w2[:, i, f, :],
                                                       start=f == 0, stop=f == FT - 1)
                        ins.then_inc(mlp_ready, 1)

                pe.wait_ge(const, 7)
                with pe.Fori(0, C_DEPTH) as i:
                    layer(i)
                transposes(2 * C_DEPTH)
                pe.wait_ge(n2_ready, 2 * C_DEPTH + 2)
                for t in range(NT):
                    if t >= 2:
                        pe.wait_ge(tail.out_taken, tail.base + t - 1)
                    nc.tensor.matmul(tail.out_bank[t % 2][:, :], normed2[:, t * P:(t + 1) * P], w_out[:, :],
                                     start=True, stop=True).then_inc(tail.out_ready, 1)
                    if t:
                        tail.pe(pe, t - 1)
                tail.pe(pe, NT - 1)

            @block.scalar
            def _(act):
                act.wait_ge(loaded, LOADS)

                def affine(n, weight, bias):
                    for half in range(2):
                        act.wait_ge(turned_up, 2 * n + half + 1)
                        nc.scalar.activation(normed2[0:LOW, half * HALF:(half + 1) * HALF], tr_bank[half][0:LOW, :],
                                             ACT.Identity, scale=weight, bias=bias).then_inc(n2_ready, 1)

                with act.Fori(0, C_DEPTH) as i:
                    act.wait_ge(col_ready, i + 1)
                    for half in range(2):
                        act.wait_ge(turned_up, 4 * i + half + 1)
                        nc.scalar.activation(y[:, half * HALF:(half + 1) * HALF], tr_bank[half][:, :], ACT.Silu,
                                             scale=col[:, 0:1], bias=col[:, 1:2])\
                            .then_inc(y_ready, 1)
                    affine(2 * i + 1, col[0:LOW, 2:3], col[0:LOW, 3:4])
                    for half in range(2):
                        for f in range(FT):
                            act.wait_ge(ff_ready, 4 * i + 2 * half + f + 1)
                            nc.scalar.activation(hidden[:, f, half * HALF:(half + 1) * HALF],
                                                 ff_bank[2 * half + f][:, :], ACT.Silu)\
                                .then_inc(hidden_ready, 1)
                affine(2 * C_DEPTH, last_cols[:, 0:1], last_cols[:, 1:2])
                tail.act(act)

            @block.vector
            def _(dve):
                state_of = {"count": 0, "base": 0}

                def then(ins):
                    state_of["count"] += 1
                    ins.then_inc(step, 1)
                    dve.wait_ge(step, state_of["base"] + state_of["count"])

                tt, ts = nc.vector.tensor_tensor, nc.vector.tensor_scalar

                def tiles(half):
                    return slice(half * HT, (half + 1) * HT)

                def by_tile(x, half):
                    return x[:, tiles(half)].unsqueeze(2).to_broadcast([P, HT, LOW])

                def flat(half):
                    return h[:, tiles(half), :].rearrange("p t d -> p (t d)")

                def norm(n, copies, update=None):
                    for half in range(2):
                        at = tiles(half)
                        if update is not None:
                            update(half)
                        then(nc.vector.tensor_reduce(total[:, at], h[:, at, :], AX.X, ALU.add))
                        then(ts(mean[:, at], total[:, at], 1.0 / LOW, None, ALU.mult))
                        then(tt(centred[:, at, :], h[:, at, :], by_tile(mean, half), ALU.subtract))
                        then(tt(square[:, at, :], centred[:, at, :], centred[:, at, :], ALU.mult))
                        then(nc.vector.tensor_reduce(total[:, at], square[:, at, :], AX.X, ALU.add))
                        ts(var[:, at], total[:, at], 1.0 / LOW, EPS, ALU.mult, ALU.add).then_inc(var_ready, 1)
                    for half in range(2):
                        at = tiles(half)
                        dve.wait_ge(rstd_ready, 2 * n + half + 1)
                        for j in range(copies):
                            ins = tt(twice[:, at, j, :], centred[:, at, :], by_tile(rstd, half), ALU.mult)
                        ins.then_inc(normed, 1)

                dve.wait_ge(loaded, LOADS)
                dve.wait_ge(rot.half_ready, 1)
                dve.wait_ge(rot.decay_ready, 1)
                dve.wait_ge(h_in, 1)
                for half in range(2):
                    then(tt(h[:, tiles(half), :], half_bank[half][:, 0:HT * LOW].rearrange("p (t d) -> p t d", t=HT),
                            rows[:, 2 * C_DEPTH, :].unsqueeze(1).to_broadcast([P, HT, LOW]), ALU.add))
                norm(0, 2)
                PRE, STEPS = state_of["count"], 30

                with dve.Fori(0, C_DEPTH) as i:
                    state_of["count"], state_of["base"] = PRE, STEPS * i
                    for half in range(2):
                        part = slice(half * HALF, (half + 1) * HALF)
                        dve.wait_ge(y_ready, 2 * i + half + 1)
                        then(tt(turned[:, part], y[:, part], rot.wave[:, i, part], ALU.mult))
                        before = rot.start[:, bass.ds(i, 1)] if half == 0 else state[:, HALF - 1:HALF]
                        then(nc.vector.tensor_tensor_scan(state[:, part],
                                                          rot.decay[:, bass.ds(i, 1)].to_broadcast([P, HALF]),
                                                          turned[:, part], before, ALU.mult, ALU.add))
                        tt(back[:, part], state[:, part], rot.wave[:, i, part], ALU.mult).then_inc(back_ready, 1)

                    def add_conv(half):
                        dve.wait_ge(conv_ready, 2 * i + half + 1)
                        then(tt(flat(half), flat(half), half_bank[half][:, 0:HT * LOW], ALU.add))

                    def add_mlp(half):
                        dve.wait_ge(mlp_ready, 2 * i + half + 1)
                        then(tt(flat(half), flat(half), half_bank[half][:, 0:HT * LOW], ALU.add))
                        then(tt(h[:, tiles(half), :], h[:, tiles(half), :],
                                rows[:, bass.ds(i, 1), :].to_broadcast([P, HT, LOW]), ALU.add))

                    norm(2 * i + 1, 1, add_conv)
                    norm(2 * i + 2, 2, add_mlp)
                    assert state_of["count"] == PRE + STEPS, state_of
                state_of["count"], state_of["base"] = PRE + STEPS * C_DEPTH, 0
                for t in range(NT):
                    tail.dve(dve, t)


HEADS, HD = 32, 16
PROBS = 8
PAIRS = HEADS // 2
SPLIT = 3 * 2 * HD
SHIFTED = SPLIT + 4


def attention_plan():
    order = list(range(NT))

    def max_units(i):
        keys = (order[i] + 1) * P
        found = []
        for lo in range(0, keys, HALF):
            n = min(HALF, keys - lo)
            per = HALF // n
            found += [(range(h, min(h + per, HEADS)), lo, n) for h in range(0, HEADS, per)]
        return found

    plan, pending, step, value_lag = [], [], 0, 5
    n_max = n_score = 0

    def later(steps, *event):
        pending.append((step + steps, event))

    def flush(everything=False):
        while pending and (everything or min(pending)[0] <= step):
            at = pending.index(min(pending, key=lambda x: x[0]))
            _, event = pending.pop(at)
            plan.append(event)
            if event[0] == "value" and event[4] and event[3] % 4 == 3:
                later(3, "heads", event[1], event[3] // 4)
            elif event[0] == "heads" and event[2] == 1:
                later(2, "turn", event[1])
            elif event[0] == "turn":
                later(2, "project", event[1])
            elif event[0] == "project":
                later(3, "std", event[1])
            elif event[0] == "std":
                later(1, "norm", event[1])
            elif event[0] == "norm":
                later(3, "feat", event[1])

    for unit in max_units(0):
        plan.append(("max", 0, n_max, *unit))
        n_max += 1
    plan += [("shift", 0), ("shift_rows", 0)]
    for i, qt in enumerate(order):
        todo = max_units(i + 1) if i + 1 < NT else []
        total, steps = len(todo), 8 * (qt + 1)
        for n in range(steps):
            four, kt, u = n // (4 * (qt + 1)), n // 4 % (qt + 1), n % 4
            u += 4 * four
            plan.append(("score", i, n_score, u, kt))
            later(value_lag, "value", i, n_score, u, kt == qt, kt)
            n_score += 1
            step += 1
            done = total - len(todo)
            want = min(total, -(-total * (n + 1) // max(1, steps - 6)))
            for _ in range(want - done):
                plan.append(("max", i + 1, n_max, *todo.pop(0)))
                n_max += 1
                if not todo:
                    plan.append(("shift", i + 1))
                    later(2, "shift_rows", i + 1)
            flush()
        rest = [p for p in pending if p[1][0] == "shift_rows"]
        for p in rest:
            pending.remove(p)
            plan.append(p[1])
    step += 1000
    flush(everything=True)
    while pending:
        flush(everything=True)
    return order, plan


class AttentionWeights:
    def __init__(self, c, own):
        def sb(n, shape):
            return c.sb(f"mqa_{n}", shape, F32, own)

        self.wq, self.wo = sb("wq", [P, KC, DIM]), sb("wo", [P, KC, DIM])
        self.wk = sb("wk", [P, KC, 2, P])
        self.bq, self.bk, self.bo = sb("bq", [P, KC]), sb("bk", [P, 2]), sb("bo", [P, DIM])
        self.w_loaded, self.wo_loaded = c.sem("mqa_w_loaded"), c.sem("mqa_wo_loaded")

    def load(self, sp, a):
        for dst, src in ((self.wk, "A_wk"), (self.bk, "A_bk"), (self.wq, "A_wq"), (self.bq, "A_bq")):
            sp.dma_start(dst[:], a[src]).then_inc(self.w_loaded, 16)
        sp.dma_start(self.wo[:, :, :], a["A_wo"]).then_inc(self.wo_loaded, 16)
        sp.dma_start(self.bo[:, :], a["A_bo"].partition_broadcast(P)).then_inc(self.wo_loaded, 16)


def causal_attention(c, weights, load_ahead):
    nc = c.nc
    order, plan = attention_plan()
    TURNS = ("shift_rows", "heads", "turn", "project", "feat")
    turn_use = {e: n for n, e in enumerate(e for e in plan if e[0] in TURNS)}
    SCALE = HD ** -0.5
    HIDE = -3.0e38
    with ExitStack() as own:
        def sb(n, shape, dt=F32, scope=own):
            return c.sb(f"mqa_{n}", shape, dt, scope)

        def sem(n):
            return c.sem(f"mqa_{n}")

        wq, wo, wk, bq, bk, bo = weights.wq, weights.wo, weights.wk, weights.bq, weights.bk, weights.bo
        stack = sb("stack", [P, PAIRS, TOK], F32R)
        q_hi, q_lo = sb("q_hi", [P, 2, TOK], F32R), sb("q_lo", [P, 2, TOK], F32R)
        keys = sb("keys", [P, 2, TOK], F32R)
        v_feat, v = sb("v_feat", [P, TOK]), sb("v", [P, NT, 2 * HD])
        ident_b, hide_k, hide_q = sb("ident_b", [P, P], BF16), sb("hide_k", [P, P], BF16), sb("hide_q", [P, 4, P], BF16)
        top, shift = sb("top", [P, 2, 2, HEADS]), sb("shift", [P, 2, 2, 2, PAIRS], F32R)
        both = sb("both", [P, HEADS])
        rows = sb("rows", [4 * PAIRS, 2, P], F32R)
        prob = sb("prob", [P, PROBS, HALF])
        o_sb = sb("o_sb", [P, 2, HALF])
        inv = sb("inv", [P, 4, 2, 2])
        attn, a_feat = sb("attn", [P, 2, DIM]), sb("a_feat", [P, 2, KC, P])
        max_bank, score_bank, value_bank = [c.bank[0], c.bank[1], c.bank[7]], [c.bank[2], c.bank[3], c.bank[5]], c.bank[4]
        turn_bank = c.bank[6]

        w_loaded, wo_loaded, const = weights.w_loaded, weights.wo_loaded, sem("const")
        q_ready, q_rounded, q_split = sem("q_ready"), sem("q_rounded"), sem("q_split")
        k_ready, k_rounded, k_split, v_turned, v_ready = (sem("k_ready"), sem("k_rounded"), sem("k_split"),
                                                          sem("v_turned"), sem("v_ready"))
        stacked = [sem(f"stacked{i}") for i in range(KC)]
        max_ready, max_taken, step = sem("max_ready"), sem("max_taken"), sem("step")
        shift_ready, shift_turned = sem("shift_ready"), sem("shift_turned")
        rows_sent = [sem(f"rows_sent{i}") for i in range(2)]
        score_ready, exp_ready, value_done = sem("score_ready"), sem("exp_ready"), sem("value_done")
        o_copied, heads_turned = sem("o_copied"), sem("heads_turned")
        turned, out_ready = sem("turned"), sem("out_ready")
        var_ready, std_ready, normed = sem("var_ready"), sem("std_ready"), sem("normed")
        feat_turned, turn_taken = sem("feat_turned"), sem("turn_taken")

        def cols(t):
            return slice(t * P, (t + 1) * P)

        with nc.Block() as block:

            @block.sync
            def _(sp):
                load_ahead(sp)
                for m in range(KC):
                    sp.wait_ge(q_split, 2 * m + 2)
                    for j in range(4):
                        src = slice(32 * j, 32 * j + 32)
                        for slot, part in enumerate((q_hi, q_hi, q_lo)):
                            sp.dma_start(stack[32 * slot:32 * slot + 32, 4 * m + j, :].bitcast(F32),
                                         part[src, m % 2, :].bitcast(F32))\
                                .then_inc(stacked[m], 16)
                for event in plan:
                    if event[0] == "shift_rows":
                        i = event[1]
                        sp.wait_ge(turn_taken, turn_use[event] + 1)
                        sp.dma_start(stack[SPLIT:SHIFTED, :, cols(order[i])].bitcast(F32), rows[:, i % 2, :].bitcast(F32))\
                            .then_inc(rows_sent[i % 2], 16)

            @block.gpsimd
            def _(pool):
                nc.gpsimd.memset(ident_b[:, :], 0.0)
                nc.gpsimd.memset(hide_k[:, :], 0.0)
                nc.gpsimd.memset(hide_q[:, :, :], 0.0).then_inc(const, 1)
                pool.wait_ge(const, 1)
                nc.gpsimd.affine_select(out=ident_b[:, :], in_=ident_b[:, :], compare_op=ALU.not_equal, fill=1.0,
                                        base=0, pattern=[[-1, P]], channel_multiplier=1)
                nc.gpsimd.affine_select(out=hide_k[:, :], in_=hide_k[:, :], compare_op=ALU.is_ge, fill=HIDE,
                                        base=0, pattern=[[-1, P]], channel_multiplier=1)
                nc.gpsimd.affine_select(out=hide_q[:, :, :], in_=hide_q[:, :, :], compare_op=ALU.is_ge, fill=HIDE,
                                        base=0, pattern=[[0, 4], [1, P]], channel_multiplier=-1).then_inc(const, 1)

            @block.tensor
            def _(pe):
                pe.wait_ge(w_loaded, 64)
                for head in range(2):
                    for half in range(2):
                        for k in range(KC):
                            ins = nc.tensor.matmul(c.bank[4 + 2 * head + half], wk[:, k, head, :],
                                                   c.x_feat[:, k, half * HALF:(half + 1) * HALF],
                                                   start=k == 0, stop=k == KC - 1)
                        ins.then_inc(k_ready, 1)
                for m in range(KC):
                    for half in range(2):
                        n = 2 * m + half
                        if n >= 4:
                            pe.wait_ge(q_split, n - 3)
                        for k in range(KC):
                            ins = nc.tensor.matmul(c.bank[n % 4], wq[:, k, cols(m)],
                                                   c.x_feat[:, k, half * HALF:(half + 1) * HALF],
                                                   start=k == 0, stop=k == KC - 1)
                        ins.then_inc(q_ready, 1)
                pe.wait_ge(k_split, 4)
                for t in range(NT):
                    ins = nc.tensor.transpose(c.bank[4][:, t * 2 * HD:(t + 1) * 2 * HD], v_feat[SPLIT:P, cols(t)],
                                              c.ident[SPLIT:P, SPLIT:P])
                ins.then_inc(v_turned, 1)
                pe.wait_ge(q_split, 8)
                pe.wait_ge(v_ready, 2)
                pe.wait_ge(const, 2)

                for event in plan:
                    kind, i = event[0], event[1]
                    qt = order[i]
                    if turn_use.get(event, 0):
                        pe.wait_ge(turn_taken, turn_use[event])
                    if kind == "max":
                        _, _, n, heads, lo, width = event
                        if n >= 3:
                            pe.wait_ge(max_taken, n - 2)
                        for at, head in enumerate(heads):
                            if i == 0 and lo == 0 and head % 8 == 0:
                                pe.wait_ge(stacked[head // 8], 16 * 12)
                            masked = lo + width == (qt + 1) * P
                            out = max_bank[n % 3]
                            ins = nc.tensor.matmul(out[:, at * width:(at + 1) * width],
                                                   stack[0:SPLIT, head // 2, cols(qt)],
                                                   keys[0:SPLIT, head % 2, lo:lo + width],
                                                   start=True, stop=not masked)
                            if masked:
                                ins = nc.tensor.matmul(out[:, (at + 1) * width - P:(at + 1) * width],
                                                       ident_b[:, :], hide_k[:, :], start=False, stop=True)
                        ins.then_inc(max_ready, 1)
                    elif kind == "shift_rows":
                        pe.wait_ge(shift_ready, i + 1)
                        nc.tensor.transpose(turn_bank[0:4 * PAIRS, 0:P],
                                            shift[:, i % 2, :, :, :].rearrange("p h s j -> p (h s j)").bitcast(F32),
                                            c.ident[:, :]).then_inc(shift_turned, 1)
                    elif kind == "score":
                        _, _, n, u, kt = event
                        if u == 0 and kt == 0:
                            pe.wait_ge(rows_sent[i % 2], 16 * (i // 2 + 1))
                        if n >= 3:
                            pe.wait_ge(exp_ready, n - 2)
                        g, head = divmod(u, 2)
                        ins = nc.tensor.matmul(score_bank[n % 3], keys[0:SHIFTED, head, cols(kt)],
                                               stack[0:SHIFTED, 4 * g:4 * g + 4, cols(qt)],
                                               start=True, stop=kt != qt)
                        if kt == qt:
                            ins = nc.tensor.matmul(score_bank[n % 3], ident_b[:, :],
                                                   hide_q[:, :, :].rearrange("p a b -> p (a b)"),
                                                   start=False, stop=True)
                        ins.then_inc(score_ready, 1)
                    elif kind == "value":
                        _, _, n, u, final, kt = event
                        four, row = 2 * i + u // 4, 32 * (u % 4)
                        if kt == 0 and u % 4 == 0 and four:
                            pe.wait_ge(o_copied, four)
                        pe.wait_ge(exp_ready, n + 1)
                        nc.tensor.matmul(value_bank[row:row + 32, :], v[:, kt, :], prob[:, n % PROBS, :],
                                         start=kt == 0, stop=final).then_inc(value_done, 1)
                    elif kind == "heads":
                        four = 2 * i + event[2]
                        pe.wait_ge(o_copied, four + 1)
                        for j in range(4):
                            ins = nc.tensor.transpose(turn_bank[:, cols(j)], o_sb[:, four % 2, cols(j)], c.ident[:, :])
                        ins.then_inc(heads_turned, 1)
                    elif kind == "turn":
                        pe.wait_ge(turn_taken, turn_use[("heads", i, 1)] + 1)
                        for k in range(KC):
                            ins = nc.tensor.transpose(turn_bank[:, cols(k)], attn[:, i % 2, cols(k)], c.ident[:, :])
                        ins.then_inc(turned, 1)
                    elif kind == "project":
                        if i == 0:
                            pe.wait_ge(wo_loaded, 32)
                        pe.wait_ge(turn_taken, turn_use[("turn", i)] + 1)
                        for k in range(KC):
                            ins = nc.tensor.matmul(turn_bank, a_feat[:, i % 2, k, :], wo[:, k, :],
                                                   start=k == 0, stop=k == KC - 1)
                        ins.then_inc(out_ready, 1)
                    elif kind == "feat":
                        pe.wait_ge(normed, i + 1)
                        for k in range(KC):
                            ins = nc.tensor.transpose(turn_bank[:, cols(k)], c.x_tok[:, qt, cols(k)], c.ident[:, :])
                        ins.then_inc(feat_turned, 1)

            @block.scalar
            def _(act):
                act.wait_ge(w_loaded, 64)
                for head in range(2):
                    for half in range(2):
                        part, bank = slice(half * HALF, (half + 1) * HALF), c.bank[4 + 2 * head + half]
                        act.wait_ge(k_ready, 2 * head + half + 1)
                        if head == 0:
                            nc.scalar.activation(v_feat[SPLIT:P, part], bank[SPLIT:P, :], ACT.Identity,
                                                 bias=bk[SPLIT:P, 0:1])
                        nc.scalar.activation(keys[0:SPLIT, head, part], bank[0:SPLIT, :], ACT.Identity,
                                             bias=bk[0:SPLIT, head:head + 1]).then_inc(k_rounded, 1)
                for n in range(2 * KC):
                    m, half = divmod(n, 2)
                    act.wait_ge(q_ready, n + 1)
                    if m >= 2 and half == 0:
                        act.wait_ge(stacked[m - 2], 16 * 12)
                    nc.scalar.activation(q_hi[:, m % 2, half * HALF:(half + 1) * HALF], c.bank[n % 4], ACT.Identity,
                                         bias=bq[:, m:m + 1]).then_inc(q_rounded, 1)

                for event in plan:
                    kind, i = event[0], event[1]
                    qt = order[i]
                    if kind == "score":
                        n = event[2]
                        act.wait_ge(score_ready, n + 1)
                        if n >= PROBS:
                            act.wait_ge(value_done, n - PROBS + 1)
                        nc.scalar.activation(prob[:, n % PROBS, :], score_bank[n % 3], ACT.Exp, scale=SCALE)\
                            .then_inc(exp_ready, 1)
                    elif kind == "value" and event[4] and event[3] % 4 == 3:
                        _, _, n, u, _, _ = event
                        four = 2 * i + u // 4
                        act.wait_ge(value_done, n + 1)
                        if four >= 2:
                            act.wait_ge(heads_turned, four - 1)
                        nc.scalar.copy(o_sb[:, four % 2, :], value_bank).then_inc(o_copied, 1)
                    elif kind == "shift_rows":
                        act.wait_ge(shift_turned, i + 1)
                        if i >= 2:
                            act.wait_ge(rows_sent[i % 2], 16 * (i // 2))
                        nc.scalar.copy(rows[:, i % 2, :], turn_bank[0:4 * PAIRS, 0:P]).then_inc(turn_taken, 1)
                    elif kind == "turn":
                        act.wait_ge(turned, i + 1)
                        if i >= 2:
                            act.wait_ge(out_ready, i - 1)
                        nc.scalar.copy(a_feat[:, i % 2, :, :].rearrange("p k n -> p (k n)"), turn_bank)\
                            .then_inc(turn_taken, 1)
                    elif kind == "std":
                        act.wait_ge(var_ready, i + 1)
                        nc.scalar.activation(c.std[:, qt:qt + 1], c.mean_var[:, qt, 1:2], ACT.Sqrt,
                                             bias=c.eps[:, 0:1]).then_inc(std_ready, 1)
                    elif kind == "feat":
                        act.wait_ge(feat_turned, i + 1)
                        nc.scalar.copy(c.x_feat[:, :, cols(qt)], turn_bank.rearrange("p (k n) -> p k n", k=KC))\
                            .then_inc(turn_taken, 1)

            @block.vector
            def _(dve):
                count = 0

                def then(ins):
                    nonlocal count
                    count += 1
                    ins.then_inc(step, 1)
                    dve.wait_ge(step, count)

                tt, ts, stt = nc.vector.tensor_tensor, nc.vector.tensor_scalar, nc.vector.scalar_tensor_tensor
                last = slice(SPLIT, SHIFTED)
                for head, (both_rows, first_rows) in enumerate(((0.0, 1.0), (1.0, 0.0))):
                    then(nc.vector.memset(keys[last, head, :].bitcast(F32), both_rows))
                    then(nc.vector.memset(keys[SPLIT:SPLIT + 2, head, :].bitcast(F32), first_rows))
                dve.wait_ge(w_loaded, 64)
                mid = slice(32, 64)
                for head in range(2):
                    for half in range(2):
                        part, bank = slice(half * HALF, (half + 1) * HALF), c.bank[4 + 2 * head + half]
                        dve.wait_ge(k_rounded, 2 * head + half + 1)
                        stt(keys[mid, head, part], bank[mid, :], bk[mid, head:head + 1],
                            keys[mid, head, part].bitcast(F32), ALU.add, ALU.subtract).then_inc(k_split, 1)
                for n in range(2 * KC):
                    m, half = divmod(n, 2)
                    part = slice(half * HALF, (half + 1) * HALF)
                    dve.wait_ge(q_rounded, n + 1)
                    stt(q_lo[:, m % 2, part], c.bank[n % 4], bq[:, m:m + 1],
                        q_hi[:, m % 2, part].bitcast(F32), ALU.add, ALU.subtract).then_inc(q_split, 1)
                dve.wait_ge(v_turned, 1)
                nc.vector.tensor_copy(v[:, :, :], c.bank[4][:, 0:NT * 2 * HD].rearrange("p (t d) -> p t d", t=NT))\
                    .then_inc(v_ready, 1)
                dve.wait_ge(v_ready, 1)
                nc.vector.memset(v[:, :, HD:HD + 1], 1.0).then_inc(v_ready, 1)

                for event in plan:
                    kind, i = event[0], event[1]
                    qt = order[i]
                    row = c.x_tok[:, qt, :]
                    segments = -(-(qt + 1) * P // HALF)
                    if kind == "max":
                        _, _, n, heads, lo, width = event
                        dve.wait_ge(max_ready, n + 1)
                        nc.vector.tensor_reduce(top[:, i % 2, lo // HALF, heads[0]:heads[-1] + 1],
                                                max_bank[n % 3][:, 0:len(heads) * width]
                                                .rearrange("p (h k) -> p h k", h=len(heads)), AX.X, ALU.max)\
                            .then_inc(max_taken, 1)
                    elif kind == "shift":
                        last_max = max(e[2] for e in plan if e[0] == "max" and e[1] == i)
                        dve.wait_ge(max_taken, last_max + 1)
                        if i >= 2:
                            dve.wait_ge(shift_turned, i - 1)
                        if segments == 2:
                            then(tt(both[:, :], top[:, i % 2, 0, :], top[:, i % 2, 1, :], ALU.max))
                            found = both[:, :]
                        else:
                            found = top[:, i % 2, 0, :]
                        found = found.rearrange("p (j h) -> p h j", h=2)
                        high, low = shift[:, i % 2, :, 0, :], shift[:, i % 2, :, 1, :]
                        then(ts(high, found, -1.0, None, ALU.mult))
                        stt(low, found, -1.0, high.bitcast(F32), ALU.mult, ALU.subtract).then_inc(shift_ready, 1)
                    elif kind == "heads":
                        four = event[2]
                        dve.wait_ge(heads_turned, 2 * i + four + 1)
                        if i >= 2 and four == 0:
                            dve.wait_ge(turned, i - 1)
                        parts = turn_bank.rearrange("p (j g h d) -> p g j h d", j=4, g=2, h=2)
                        then(nc.vector.reciprocal(inv[:, :, :, :], turn_bank.rearrange(
                            "p (j g h d) -> p j g h d", j=4, g=2, h=2)[:, :, :, :, HD]))
                        for g in range(2):
                            at = (2 * four + g) * P
                            dst = attn[:, i % 2, at:at + P].rearrange("p (j h d) -> p j h d", j=4, h=2)
                            ins = tt(dst, parts[:, g, :, :, 0:HD],
                                     inv[:, :, g, :].unsqueeze(3).to_broadcast([P, 4, 2, HD]), ALU.mult)
                        ins.then_inc(turn_taken, 1)
                    elif kind == "project":
                        dve.wait_ge(out_ready, i + 1)
                        if i == 0:
                            dve.wait_ge(wo_loaded, 32)
                        tt(row, row, turn_bank, ALU.add).then_inc(turn_taken, 1)
                        dve.wait_ge(turn_taken, turn_use[event] + 1)
                        then(tt(row, row, bo[:, :], ALU.add))
                        then(nc.vector.bn_stats(c.stats[:, qt, :], row))
                        nc.vector.bn_aggr(c.mean_var[:, qt, :], c.stats[:, qt, :]).then_inc(var_ready, 1)
                    elif kind == "norm":
                        dve.wait_ge(std_ready, i + 1)
                        then(nc.vector.reciprocal(c.rstd[:, qt:qt + 1], c.std[:, qt:qt + 1]))
                        ts(row, row, c.mean_var[:, qt, 0:1], c.rstd[:, qt:qt + 1], ALU.subtract, ALU.mult)\
                            .then_inc(normed, 1)


def build(nc, a, out):
    with ExitStack() as ctx:
        c = Chip(nc, ctx)
        setup(c)
        gradient_ffn(c, a)
        c.rot = Rotation(c)
        front1 = FfnFront(c, "L1_ffn", a["L1_w"], zeros=a["L1_z"], scales=a["L1_s"])
        with ExitStack() as scope:
            c.rot.scratch(scope)
            lora_then_single_key(c, a, front1.load_first)
        swiglu(c, front1)
        front3 = FfnFront(c, "L3_ffn", a["L3_w"], scale=[a["L3_scale_gate"], a["L3_scale_up"], a["L3_scale_down"]])
        with ExitStack() as scope:
            attention = AttentionWeights(c, scope)
            with ExitStack() as lora_scope:
                loras = TwoLorasWeights(c, lora_scope)

                def load_both(sp):
                    loras.load(sp, a)
                    attention.load(sp, a)

                conv_stack(c, a, load_both)
                two_loras(c, loras)
            causal_attention(c, attention, front3.load_first)
        swiglu(c, front3, last=out.rearrange("(t p) n -> t p n", p=P))


def up_tiles(w, tiles):
    w = np.asarray(w)
    w = np.pad(w, ((0, 0), (0, tiles * P - w.shape[1])))
    return w.reshape(KC, P, tiles, P).transpose(2, 1, 0, 3).reshape(tiles, P, KC * P)


def down_tiles(w, tiles):
    w = np.asarray(w)
    return np.pad(w, ((0, tiles * P - w.shape[0]), (0, 0))).reshape(tiles, P, w.shape[1])


def chunks(w):
    return w.reshape(-1, P, w.shape[1]).transpose(1, 0, 2)


def layout(v):
    v = {k: np.asarray(x) for k, x in v.items()}
    x = np.asarray(v["L0_attn_hidden_states"])[0]
    a = {"x_tok": x, "x_feat": x.T}
    a["L1_w"] = np.concatenate([up_tiles(v["L1_ffn_gate_w"], 14), up_tiles(v["L1_ffn_up_w"], 14),
                                down_tiles(v["L1_ffn_down_w"], 14)], 2)
    for n, k in (("z", "z"), ("s", "s")):
        g, u, d = (np.asarray(v[f"L1_ffn_{w}_{k}"]) for w in ("gate", "up", "down"))
        cols = lambda m: m.reshape(KC, 14, P).transpose(1, 0, 2).reshape(14, KC * P)
        a["L1_" + n] = np.concatenate([cols(g), cols(u), d], 1)
    a["L3_w"] = np.concatenate([up_tiles(v["L3_ffn_w_gate"].T, 11), up_tiles(v["L3_ffn_w_up"].T, 11),
                                down_tiles(v["L3_ffn_w_down"].T, 11)], 2)
    for n in ("scale_gate", "scale_up", "scale_down"):
        a["L3_" + n] = v["L3_ffn_" + n].reshape(1)
    a["L0_w"] = np.concatenate([up_tiles(v["L0_attn_ffn_gate_w"].T, 10), up_tiles(v["L0_attn_ffn_up_w"].T, 10)], 2)
    a["L0_down"] = down_tiles(v["L0_attn_ffn_down_w"].T, 10).transpose(1, 0, 2)
    a["L0_proj"] = np.stack([chunks(v["L0_attn_up_w"].T), chunks(v["L0_attn_gate_w"].T)], 1)
    a["L0_fuse"] = np.concatenate([v["L0_attn_local_approx_output"].T[:, None],
                                   v["L0_attn_fuse_weight"].transpose(1, 2, 0)], 1)
    a["L0_point"] = v["L0_attn_local_point"].reshape(P, 1)
    a["L0_disc"] = v["L0_attn_discount_factor"]
    a["L0_org"] = chunks(v["L0_ffn_W_org"].T)
    a["L0_lora_down"] = chunks(v["L0_ffn_lora_down"].transpose(0, 2, 1).reshape(DIM, DIM))
    a["L0_up"] = chunks(v["L0_ffn_lora_up"].reshape(DIM, DIM))
    a["L0_wq"] = chunks(v["L0_ffn_Wq"].T)
    a["L0_keys"] = v["L0_ffn_lora_keys"].T
    qkv = v["L1_attn_weight_qkv"].reshape(8, 6, P, DIM)
    a["L1_wv"] = qkv[:, 5].transpose(1, 0, 2)
    a["L1_wo"] = v["L1_attn_weight_proj"].reshape(DIM, 8, 4, P).transpose(1, 3, 2, 0)
    k_w, k_b = v["L3_attn_wk_w"].T, v["L3_attn_wk_b"]
    wk, bk = np.zeros((DIM, 2, P), k_w.dtype), np.zeros((P, 2), k_b.dtype)
    for head in range(2):
        for slot in range(3):
            at = 32 * slot + HD * head
            wk[:, head, at:at + HD], bk[at:at + HD, head] = k_w, k_b
    wk[:, 0, SPLIT:SPLIT + HD], bk[SPLIT:SPLIT + HD, 0] = v["L3_attn_wv_w"].T, v["L3_attn_wv_b"]
    a["A_wk"] = wk.reshape(KC, P, 2, P).transpose(1, 0, 2, 3)
    a["A_bk"] = bk
    a["A_wq"], a["A_wo"] = chunks(v["L3_attn_wq_w"].T), chunks(v["L3_attn_wo_w"].T)
    a["A_bq"], a["A_bo"] = v["L3_attn_wq_b"].reshape(KC, P).T, v["L3_attn_wo_b"]
    twice = lambda m: np.concatenate([m.T, m.T], 0)
    g = lambda n: v["L2_attn_" + n]
    a["L2_par"] = np.stack([twice(g(n)) for n in ("phz_re", "phz_im", "lc_re", "lc_im")], 1)
    a["C_in"] = chunks(g("Win").T)
    gap = 96 - 64
    a["C_out"] = np.concatenate([np.pad(g("Wout").T, ((0, gap), (0, 0))), g("bout")[None]], 0)
    a["C_w1"] = np.concatenate([np.pad(g("W1").transpose(2, 0, 1), ((0, gap), (0, 0), (0, 0))), g("b1")[None]], 0)
    a["C_w2"] = g("W2").reshape(4, 64, 2, P).transpose(3, 0, 2, 1)
    a["C_cols"] = np.stack([twice(g(n)) for n in ("ln1_w", "ln1_b", "ln2_w", "ln2_b")], 2)
    a["C_last"] = np.stack([g("lnl_w"), g("lnl_b")], 1)
    a["C_b2"], a["C_sc"], a["C_bin"] = g("b2"), g("sc_lin"), g("bin")
    a["L2_low"] = np.stack([v["L2_ffn_A"], v["L2_ffn_WL"]], 1)
    a["L2_high"] = np.stack([v["L2_ffn_B"].T, v["L2_ffn_WR"].T], 1)
    a["L2_base"], a["L2_bias"] = chunks(v["L2_ffn_W_base"].T), v["L2_ffn_b_base"]
    return a


def kernel(**inputs):
    import concourse.bacc as bacc
    from concourse.bass_utils import run_bass_kernel_spmd

    nc = bacc.Bacc("TRN2", target_bir_lowering=False, num_devices=1)
    arrays = {f"in_{k}": np.ascontiguousarray(v) for k, v in layout(inputs).items()}
    args = {k[3:]: nc.dram_tensor(k, v.shape, mybir.dt.from_np(v.dtype), kind="ExternalInput").ap()
            for k, v in arrays.items()}
    out = nc.dram_tensor("out_0_dram", (TOK, DIM), F32, kind="ExternalOutput").ap()
    build(nc, args, out)
    r = run_bass_kernel_spmd(nc, [arrays], core_ids=[0])
    return r.results[0]["out_0_dram"].reshape(1, TOK, DIM)
```
